# Optimizing a Trainium2 kernel written in Bass

```python
import numpy as np
import jax
import jax.numpy as jnp

def _softmax(x, axis=-1):
    return jax.nn.softmax(x, axis=axis)

def _gelu(x):
    return jax.nn.gelu(x, approximate=True)

def _silu(x):
    return jax.nn.silu(x)

def _sigmoid(x):
    return jax.nn.sigmoid(x)

def _layernorm(x, axis=-1, eps=1e-05):
    m = jnp.mean(x, axis=axis, keepdims=True)
    v = jnp.var(x, axis=axis, keepdims=True)
    return (x - m) / jnp.sqrt(v + eps)

def _scatter_add(tgt, idx, src, axis=0):
    return tgt.at[idx].add(src)

def _segment_sum(src, seg, n):
    return jax.ops.segment_sum(src, seg, n)
kernel_name = 'mk_gps_d1_gnn_r8_301588'

def setup_inputs(seed: int=0):
    np.random.seed(seed)
    _w = jnp.asarray

    def _rec_inputs():
        import jax
        import jax.numpy as jnp
        _gk = jax.random.key(seed)
        x = -0.0003713 + 1 * jax.random.normal(jax.random.fold_in(_gk, 1), (12500, 256), jnp.float32)
        src = jax.random.randint(jax.random.fold_in(_gk, 2), (200000,), 0, 12500, jnp.int32)
        dst = jnp.minimum((12500 * jax.random.uniform(jax.random.fold_in(_gk, 3), (200000,)) ** 2.0).astype(jnp.int32), 99999)
        _o = jnp.argsort(dst, stable=True)
        src = src[_o]
        dst = dst[_o]
        return (x, src, dst)
    x, src, dst = _rec_inputs()

    def _L0_gnn_setup():
        import jax, jax.numpy as jnp
        import numpy as np
        N = 6250
        E = 100000
        D = 256
        H = 4
        F = D // H

        def gat_layer(x, src, dst, W, att_src, att_dst, bias):
            n = x.shape[0]
            h = (x @ W).reshape(n, H, F)
            a_src = jnp.sum(h * att_src[None], axis=-1)
            a_dst = jnp.sum(h * att_dst[None], axis=-1)
            e = jax.nn.leaky_relu(a_src[src] + a_dst[dst], 0.2)
            m = jax.ops.segment_max(e, dst, num_segments=n)
            m = jnp.where(jnp.isfinite(m), m, 0.0)
            ex = jnp.exp(e - m[dst])
            denom = jax.ops.segment_sum(ex, dst, num_segments=n)
            alpha = ex / (denom[dst] + 1e-16)
            msg = h[src] * alpha[..., None]
            out = jax.ops.segment_sum(msg, dst, num_segments=n)
            return out.reshape(n, H * F) + bias
        key = jax.random.key(seed)
        ks = jax.random.split(key, 8)
        x = jax.random.normal(ks[0], (N, D), dtype=jnp.float32)
        edge_index = jax.random.randint(ks[1], (2, E), 0, N, dtype=jnp.int32)
        W = jax.random.normal(ks[2], (D, H * F), dtype=jnp.float32) * (1.0 / np.sqrt(D))
        att_src = jax.random.normal(ks[3], (H, F), dtype=jnp.float32) * (1.0 / np.sqrt(F))
        att_dst = jax.random.normal(ks[4], (H, F), dtype=jnp.float32) * (1.0 / np.sqrt(F))
        bias = jnp.zeros((D,), dtype=jnp.float32)
        ln_gamma = jnp.ones((D,), dtype=jnp.float32)
        ln_beta = jnp.zeros((D,), dtype=jnp.float32)
        return {'x': x, 'edge_index': edge_index, 'W': W, 'att_src': att_src, 'att_dst': att_dst, 'bias': bias, 'ln_gamma': ln_gamma, 'ln_beta': ln_beta}
    _L0_gnn_all = _L0_gnn_setup()
    _L0_gnn_in = {k: v for k, v in _L0_gnn_all.items() if k in ('W', 'att_src', 'att_dst', 'bias', 'ln_gamma', 'ln_beta')}
    del _L0_gnn_all

    def _L0_mix_setup():
        import jax, jax.numpy as jnp
        import numpy as np
        EPS_NORM = 1e-06
        EPS_ATTN = 1e-06
        HEADS = 8

        def rmsnorm(x, w):
            ms = jnp.mean(x * x, axis=-1, keepdims=True)
            return w * (x * jax.lax.rsqrt(ms + EPS_NORM))

        def linear_attention(x, w_qkv, w_out, b_out):
            B, N, D = x.shape
            hd = D // HEADS
            qkv = (x @ w_qkv).reshape(B, N, 3, HEADS, hd)
            q, k, v = (qkv[:, :, 0], qkv[:, :, 1], qkv[:, :, 2])
            q = jax.nn.elu(q) + 1.0
            k = jax.nn.elu(k) + 1.0
            kv = jnp.einsum('bnhd,bnhm->bhdm', k, v)
            z = 1.0 / (jnp.einsum('bnhd,bhd->bnh', q, k.sum(axis=1)) + EPS_ATTN)
            out = jnp.einsum('bnhd,bhdm,bnh->bnhm', q, kv, z)
            out = out.reshape(B, N, D)
            return out @ w_out + b_out
        key = jax.random.key(seed)
        ks = jax.random.split(key, 4)
        B, N, D = (16, 1024, 256)
        x = jax.random.normal(ks[0], (B, N, D), dtype=jnp.float32)
        w_norm1 = jnp.ones((D,), dtype=jnp.float32)
        w_qkv = jax.random.normal(ks[1], (D, 3 * D), dtype=jnp.float32) * 0.02
        w_out = jax.random.normal(ks[2], (D, D), dtype=jnp.float32) * 0.02
        b_out = jnp.zeros((D,), dtype=jnp.float32)
        w_norm2 = jnp.ones((D,), dtype=jnp.float32)
        return {'x': x, 'w_norm1': w_norm1, 'w_qkv': w_qkv, 'w_out': w_out, 'b_out': b_out, 'w_norm2': w_norm2}
    _L0_mix_all = _L0_mix_setup()
    _L0_mix_in = {k: v for k, v in _L0_mix_all.items() if k in ('w_norm1', 'w_qkv', 'w_out', 'b_out', 'w_norm2')}
    del _L0_mix_all

    def _L0_ffn_setup():
        import jax, jax.numpy as jnp
        import numpy as np
        E = 8
        K = 2
        D = 256
        H = 512
        DOUT = 256
        EPS = 1e-05
        key = jax.random.key(seed)
        ks = jax.random.split(key, 9)
        s = 0.02
        return {'x': jax.random.normal(ks[0], (4, 1024, D), jnp.float32), 'gamma': 1.0 + 0.05 * jax.random.normal(ks[1], (D,), jnp.float32), 'beta': 0.05 * jax.random.normal(ks[2], (D,), jnp.float32), 'Wr': 0.01 * jax.random.normal(ks[3], (D, E), jnp.float32), 'br': jnp.zeros((E,), jnp.float32), 'W1': s * jax.random.normal(ks[4], (E, D, H), jnp.float32), 'b1': s * jax.random.normal(ks[5], (E, H), jnp.float32), 'W2': s * jax.random.normal(ks[6], (E, H, DOUT), jnp.float32), 'b2': s * jax.random.normal(ks[7], (E, DOUT), jnp.float32)}
    _L0_ffn_all = _L0_ffn_setup()
    _L0_ffn_in = {k: v for k, v in _L0_ffn_all.items() if k in ('gamma', 'beta', 'Wr', 'br', 'W1', 'b1', 'W2', 'b2')}
    del _L0_ffn_all
    return {'x': x, 'src': src, 'dst': dst, 'L0_gnn_W': _L0_gnn_in['W'], 'L0_gnn_att_src': _L0_gnn_in['att_src'], 'L0_gnn_att_dst': _L0_gnn_in['att_dst'], 'L0_gnn_bias': _L0_gnn_in['bias'], 'L0_gnn_ln_gamma': _L0_gnn_in['ln_gamma'], 'L0_gnn_ln_beta': _L0_gnn_in['ln_beta'], 'L0_mix_w_norm1': _L0_mix_in['w_norm1'], 'L0_mix_w_qkv': _L0_mix_in['w_qkv'], 'L0_mix_w_out': _L0_mix_in['w_out'], 'L0_mix_b_out': _L0_mix_in['b_out'], 'L0_mix_w_norm2': _L0_mix_in['w_norm2'], 'L0_ffn_gamma': _L0_ffn_in['gamma'], 'L0_ffn_beta': _L0_ffn_in['beta'], 'L0_ffn_Wr': _L0_ffn_in['Wr'], 'L0_ffn_br': _L0_ffn_in['br'], 'L0_ffn_W1': _L0_ffn_in['W1'], 'L0_ffn_b1': _L0_ffn_in['b1'], 'L0_ffn_W2': _L0_ffn_in['W2'], 'L0_ffn_b2': _L0_ffn_in['b2']}

def reference(x, src, dst, L0_gnn_W, L0_gnn_att_src, L0_gnn_att_dst, L0_gnn_bias, L0_gnn_ln_gamma, L0_gnn_ln_beta, L0_mix_w_norm1, L0_mix_w_qkv, L0_mix_w_out, L0_mix_b_out, L0_mix_w_norm2, L0_ffn_gamma, L0_ffn_beta, L0_ffn_Wr, L0_ffn_br, L0_ffn_W1, L0_ffn_b1, L0_ffn_W2, L0_ffn_b2):
    import jax
    import jax.numpy as jnp

    def _L0_gnn_ref(x, edge_index, W, att_src, att_dst, bias, ln_gamma, ln_beta):
        import jax, jax.numpy as jnp
        import numpy as np
        N = 6250
        E = 100000
        D = 256
        H = 4
        F = D // H

        def gat_layer(x, src, dst, W, att_src, att_dst, bias):
            n = x.shape[0]
            h = (x @ W).reshape(n, H, F)
            a_src = jnp.sum(h * att_src[None], axis=-1)
            a_dst = jnp.sum(h * att_dst[None], axis=-1)
            e = jax.nn.leaky_relu(a_src[src] + a_dst[dst], 0.2)
            m = jax.ops.segment_max(e, dst, num_segments=n)
            m = jnp.where(jnp.isfinite(m), m, 0.0)
            ex = jnp.exp(e - m[dst])
            denom = jax.ops.segment_sum(ex, dst, num_segments=n)
            alpha = ex / (denom[dst] + 1e-16)
            msg = h[src] * alpha[..., None]
            out = jax.ops.segment_sum(msg, dst, num_segments=n)
            return out.reshape(n, H * F) + bias
        n = x.shape[0]
        loops = jnp.arange(n, dtype=edge_index.dtype)
        src = jnp.concatenate([edge_index[0], loops])
        dst = jnp.concatenate([edge_index[1], loops])
        h = gat_layer(x, src, dst, W, att_src, att_dst, bias)
        y = h + x
        mu = jnp.mean(y, axis=-1, keepdims=True)
        var = jnp.mean((y - mu) ** 2, axis=-1, keepdims=True)
        y = (y - mu) / jnp.sqrt(var + 1e-05) * ln_gamma + ln_beta
        return jax.nn.relu(y)

    def _L0_mix_ref(x, w_norm1, w_qkv, w_out, b_out, w_norm2):
        import jax, jax.numpy as jnp
        import numpy as np
        EPS_NORM = 1e-06
        EPS_ATTN = 1e-06
        HEADS = 8

        def rmsnorm(x, w):
            ms = jnp.mean(x * x, axis=-1, keepdims=True)
            return w * (x * jax.lax.rsqrt(ms + EPS_NORM))

        def linear_attention(x, w_qkv, w_out, b_out):
            B, N, D = x.shape
            hd = D // HEADS
            qkv = (x @ w_qkv).reshape(B, N, 3, HEADS, hd)
            q, k, v = (qkv[:, :, 0], qkv[:, :, 1], qkv[:, :, 2])
            q = jax.nn.elu(q) + 1.0
            k = jax.nn.elu(k) + 1.0
            kv = jnp.einsum('bnhd,bnhm->bhdm', k, v)
            z = 1.0 / (jnp.einsum('bnhd,bhd->bnh', q, k.sum(axis=1)) + EPS_ATTN)
            out = jnp.einsum('bnhd,bhdm,bnh->bnhm', q, kv, z)
            out = out.reshape(B, N, D)
            return out @ w_out + b_out
        h = x + linear_attention(rmsnorm(x, w_norm1), w_qkv, w_out, b_out)
        return h + rmsnorm(h, w_norm2)

    def _L0_ffn_ref(x, gamma, beta, Wr, br, W1, b1, W2, b2):
        import jax, jax.numpy as jnp
        import numpy as np
        E = 8
        K = 2
        D = 256
        H = 512
        DOUT = 256
        EPS = 1e-05
        mu = jnp.mean(x, axis=-1, keepdims=True)
        var = jnp.mean(jnp.square(x - mu), axis=-1, keepdims=True)
        xn = (x - mu) * jax.lax.rsqrt(var + EPS) * gamma + beta
        logits = jnp.einsum('bsd,de->bse', xn, Wr) + br
        top_vals, top_idx = jax.lax.top_k(logits, K)
        w = jax.nn.softmax(top_vals, axis=-1)
        w_full = jnp.einsum('bsk,bske->bse', w, jax.nn.one_hot(top_idx, E, dtype=w.dtype))
        y = jnp.zeros(x.shape[:-1] + (DOUT,), x.dtype)
        for e in range(E):
            h = jax.nn.gelu(jnp.einsum('bsd,dh->bsh', xn, W1[e]) + b1[e], approximate=False)
            y_e = jnp.einsum('bsh,hd->bsd', h, W2[e]) + b2[e]
            y = y + y_e * w_full[..., e, None]
        return y
    edge_index = jnp.stack([src, dst])
    xn = _layernorm(x, axis=-1)
    x = x + _L0_gnn_ref(xn, edge_index, L0_gnn_W, L0_gnn_att_src, L0_gnn_att_dst, L0_gnn_bias, L0_gnn_ln_gamma, L0_gnn_ln_beta) + _L0_mix_ref(xn[None], L0_mix_w_norm1, L0_mix_w_qkv, L0_mix_w_out, L0_mix_b_out, L0_mix_w_norm2)[0]
    x = x + _L0_ffn_ref(_layernorm(x, axis=-1)[None], L0_ffn_gamma, L0_ffn_beta, L0_ffn_Wr, L0_ffn_br, L0_ffn_W1, L0_ffn_b1, L0_ffn_W2, L0_ffn_b2)[0]
    return x

_drawn_inputs = setup_inputs


def setup_inputs(seed=0):
    import zlib

    import numpy as np

    out = dict(_drawn_inputs(seed))
    spreads = {'L0_gnn_bias': (0.0, 0.421),
     'L0_gnn_ln_gamma': (1.0, 0.2),
     'L0_gnn_ln_beta': (0.0, 0.394),
     'L0_mix_w_norm1': (1.0, 0.6),
     'L0_mix_b_out': (0.0, 0.1),
     'L0_mix_w_norm2': (1.0, 0.2),
     'L0_ffn_br': (0.0, 0.517)}
    factors = {'L0_gnn_att_dst': 4.408,
     'L0_mix_w_qkv': 8.0,
     'L0_mix_w_out': 8.0,
     'L0_ffn_gamma': 8.0,
     'L0_ffn_beta': 8.0,
     'L0_ffn_Wr': 5.211,
     'L0_ffn_W1': 3.733,
     'L0_ffn_b1': 28.033,
     'L0_ffn_W2': 3.628,
     'L0_ffn_b2': 33.233}
    for name, (base, spread) in spreads.items():
        noise = np.random.default_rng([zlib.crc32(name.encode()), seed]).standard_normal(out[name].shape)
        drawn = base * np.exp(spread * noise) if base else spread * noise
        out[name] = jnp.asarray(drawn.astype(out[name].dtype))
    for name, factor in factors.items():
        out[name] = (out[name] * factor).astype(out[name].dtype)
    return out
```

```python
from contextlib import ExitStack, contextmanager

import concourse.bass as bass
from concourse import mybir

P = 128
N = 12500
D = 256
E = 200000
TILES = (N + P - 1) // P
TAIL = N - (TILES - 1) * P
NP = TILES * P
GH = 4
GF = D // GH
MH = 8
MF = D // MH
C = D // P
ROW = D + GH
G = 2
SPAN = G * P
RING = 8
HEAD = 5
GROUPS = -(-E // SPAN) + TILES
GROUPS = HEAD + -(-(GROUPS - HEAD) // RING) * RING
EPART = 125
ECOL = E // EPART
NO_NODE = 1 << 20
EXPERTS = 8
HID = 512
HC = HID // P
EX_RING = 4
EX_HEAD = 4
EX_TILES = (2 * N + EXPERTS * (P - 1)) // P
EX_TILES = EX_HEAD + -(-(EX_TILES - EX_HEAD) // EX_RING) * EX_RING
ZERO_TILES = 12

F32 = mybir.dt.float32
I32 = mybir.dt.int32
U32 = mybir.dt.uint32
ALU = mybir.AluOpType
ACT = mybir.ActivationFunctionType
AX = mybir.AxisListType
RMAX = bass.bass_isa.ReduceOp.max


class Store:
    pass


def allocate(nc, ctx):
    def sb(name, shape, dt=F32):
        return ctx.enter_context(nc.sbuf_tensor(name, shape, dt))

    s = Store()
    s.node_rows = nc.dram_tensor("node_rows", [NP, ROW], F32).ap()
    s.queries = nc.dram_tensor("queries", [NP, D], F32).ap()
    s.edges = nc.dram_tensor("edges", [E + SPAN, 2], I32).ap()
    s.mixed = nc.dram_tensor("mixed", [NP, D], F32).ap()
    s.ffn_in = nc.dram_tensor("ffn_in", [NP, D], F32).ap()
    s.expert_in = nc.dram_tensor("expert_in", [EX_TILES * P, D], F32).ap()
    s.expert_out = nc.dram_tensor("expert_out", [EX_TILES * P, D], F32).ap()
    s.big = sb("big", [P, TILES * ROW])
    s.x_tiles = s.big[:, 0:(TILES + 1) * D].rearrange("p (t d) -> p t d", d=D)
    s.sums = s.big[:, :].rearrange("p (t d) -> p t d", d=ROW)
    s.scores = sb("scores", [P, TILES, 2 * GH])
    s.shift = sb("shift", [P, TILES, 2 * GH])
    s.ln_scale = sb("ln_scale", [P, TILES + 1])
    s.ln_bias = sb("ln_bias", [P, TILES + 1])
    s.kv = sb("kv", [P, C, P + 4])
    s.ident = sb("ident", [P, P])
    s.row_iota = sb("row_iota", [P, P])
    s.valid = sb("valid", [P, TILES])
    s.first_edge = sb("first_edge", [P, 1])
    s.ones = sb("ones", [P, P])
    return s


@contextmanager
def stage(nc):
    before = nc.snapshot_sems()
    yield
    nc.clear_and_free_semaphores(nc.allocated_since(before))
    nc.all_engine_barrier()


def in_step(eng, steps, lag, count, head, ring):
    assert max(lag) <= head and (count - head) % ring == 0
    for n in range(head):
        for k, step in enumerate(steps):
            if n - lag[k] >= 0:
                step(n - lag[k], (n - lag[k]) % ring, (n - lag[k]) // ring)
    with eng.Fori(0, (count - head) // ring) as i:
        for m in range(ring):
            for k, step in enumerate(steps):
                off = head + m - lag[k]
                step(i * ring + off, off % ring, i + off // ring)
    for n in range(count, count + max(lag)):
        for k, step in enumerate(steps):
            if n - lag[k] < count:
                step(n - lag[k], (n - lag[k]) % ring, (n - lag[k]) // ring)


def from_item(eng, sem, n, first, value):
    if not isinstance(n, int) or n >= first:
        eng.wait_ge(sem, value)


def fixed(eng, value):
    return value if isinstance(value, int) else eng.snap(value)


def mean_and_variance(v, stats, mean, var, tmp, done):
    v.tensor_tensor(mean, stats[:, :, 1], stats[:, :, 4], ALU.add).then_inc(done, 1)
    v.tensor_tensor(tmp, stats[:, :, 1], stats[:, :, 4], ALU.subtract).then_inc(done, 1)
    v.tensor_tensor(var, stats[:, :, 2], stats[:, :, 5], ALU.add).then_inc(done, 1)
    v.wait_ge(done, 3)
    v.tensor_scalar(mean, mean, 0.5, None, ALU.mult).then_inc(done, 1)
    v.scalar_tensor_tensor(tmp, tmp, 0.25, tmp, ALU.mult, ALU.mult).then_inc(done, 1)
    v.wait_ge(done, 5)
    v.scalar_tensor_tensor(var, var, 1.0 / D, tmp, ALU.mult, ALU.add).then_inc(done, 1)
    v.wait_ge(done, 6)


def project(nc, s, x, src, dst, W, att_src, att_dst, w_norm1, w_qkv):
    with ExitStack() as ctx:
        def sb(name, shape, dt=F32):
            return ctx.enter_context(nc.sbuf_tensor(name, shape, dt))

        def psum(name, shape):
            return ctx.enter_context(nc.psum_tensor(name, shape, F32))

        def sem(name):
            return nc.alloc_semaphore(name=name)

        w_ext = sb("w_ext", [P, C, D + 2 * GH])
        wq = sb("wq", [P, C, 3 * D])
        att = sb("att", [P, 2, D])
        att_w = sb("att_w", [P, 4, D])
        wn = sb("wn", [P, C])
        stats = sb("stats", [P, TILES + 1, 6])
        mean = sb("mean", [P, TILES + 1])
        var = sb("var", [P, TILES + 1])
        tmp = sb("tmp", [P, TILES + 1])
        h_scale = sb("h_scale", [P, TILES + 1])
        r_scale = sb("r_scale", [P, TILES + 1])
        r_bias = sb("r_bias", [P, TILES + 1])
        r = sb("r", [P, 2, D])
        rT = sb("rT", [P, 2, C, P])
        k_exp = sb("k_exp", [P, 2, D])
        q_exp = sb("q_exp", [P, 2, D])
        keys = sb("keys", [P, 2, D])
        values = sb("values", [P, 2, D])
        q_out = sb("q_out", [P, 2, D])
        h_out = sb("h_out", [P, 2, ROW])
        edge_src = sb("edge_src", [P, ECOL], I32)
        edge_dst = sb("edge_dst", [P, ECOL], I32)
        edge_pair = sb("edge_pair", [P, ECOL, 2], I32)
        edge_pad = sb("edge_pad", [P, G, 2], I32)
        node_id = sb("node_id", [P, TILES])
        pos = sb("pos", [P, 1])
        cand = sb("cand", [P, 1])
        probe = sb("probe", [P, 1], I32)
        found = sb("found", [P, 1], I32)
        below = sb("below", [P, 1])
        inside = sb("inside", [P, 1])
        window_key = sb("window_key", [P, 1])

        ps_t = psum("ps_t", [P, 2, 512])
        ps_h = psum("ps_h", [P, 512])
        ps_kv = psum("ps_kv", [P, 2, 512])
        ps_q = psum("ps_q", [P, 2, 512])
        ps_acc = psum("ps_acc", [P, 512])
        acc = ps_acc[:, 0:C * (P + 1)].rearrange("p (c n) -> p c n", c=C)

        pad_set = sem("a_pad_set")
        x_in = [sem(f"a_x_in{j}") for j in range(7)]
        w_in = sem("a_w_in")
        w_ready = sem("a_w_ready")
        w_steps = sem("a_w_steps")
        consts = sem("a_consts")
        stats_done = sem("a_stats_done")
        agg_done = sem("a_agg_done")
        var_eps = sem("a_var_eps")
        var_sqrt = sem("a_var_sqrt")
        ms_eps = sem("a_ms_eps")
        ms_sqrt = sem("a_ms_sqrt")
        chain = sem("a_scales_chain")
        r_ready = sem("a_r_ready")
        rT_psum = sem("a_rT_psum")
        rT_ready = sem("a_rT_ready")
        kv_psum = sem("a_kv_psum")
        q_psum = sem("a_q_psum")
        h_psum = sem("a_h_psum")
        acc_done = sem("a_acc_done")
        h_free = sem("a_h_free")
        k_free = sem("a_k_free")
        v_ready = sem("a_v_ready")
        q_free = sem("a_q_free")
        k_min = sem("a_k_min")
        q_min = sem("a_q_min")
        k_expd = sem("a_k_expd")
        q_expd = sem("a_q_expd")
        k_ready = sem("a_k_ready")
        q_ready = sem("a_q_ready")
        h_ready = sem("a_h_ready")
        store_free = sem("a_store_free")
        h_stored = [sem(f"a_h_stored{u}") for u in range(2)]
        q_stored = [sem(f"a_q_stored{u}") for u in range(2)]
        kv_parts = sem("a_kv_parts")
        e_in = sem("a_e_in")
        pair_ready = sem("a_pair_ready")
        pair_stored = sem("a_pair_stored")
        pool_step = sem("a_pool_step")
        probed = sem("a_probed")

        with nc.Block() as block:

            @block.sync
            def _(sp):
                sp.dma_start(w_ext[:, :, 0:D], W.rearrange("(c p) n -> p c n", p=P)).then_inc(w_in, 16)
                sp.dma_start(wq[:, :, :], w_qkv.rearrange("(c p) n -> p c n", p=P)).then_inc(w_in, 16)
                sp.dma_start(att[:, 0, :], att_src.rearrange("h f -> (h f)").partition_broadcast(P)).then_inc(w_in, 16)
                sp.dma_start(att[:, 1, :], att_dst.rearrange("h f -> (h f)").partition_broadcast(P)).then_inc(w_in, 16)
                for c in range(C):
                    sp.dma_start(wn[:, c:c + 1], w_norm1[c * P:(c + 1) * P].rearrange("(p o) -> p o", o=1)).then_inc(w_in, 16)
                for j in range(7):
                    full = 14 if j < 6 else 13
                    sp.dma_start(s.x_tiles[:, 14 * j:14 * j + full, :],
                                 x[14 * j * P:(14 * j + full) * P, :].rearrange("(t p) d -> p t d", p=P)).then_inc(x_in[j], 16)
                sp.wait_ge(pad_set, 1)
                sp.dma_start(s.x_tiles[0:TAIL, TILES - 1, :], x[N - TAIL:N, :]).then_inc(x_in[6], 16)
                sp.sem_inc(store_free, 2)
                with sp.Fori(0, TILES - 1, 2) as t0:
                    for u in range(2):
                        t = t0 + u
                        sp.wait_ge(h_ready, 2 * t + 2)
                        sp.dma_start(s.node_rows[bass.ds(t * P, P), :], h_out[:, u, :]).then_inc(h_stored[u], 16)
                        sp.wait_ge(q_ready, t + 1)
                        sp.dma_start(s.queries[bass.ds(t * P, P), :], q_out[:, u, :]).then_inc(q_stored[u], 16)
                        sp.wait_ge(h_stored[u], 8 * t0 + 16)
                        sp.wait_ge(q_stored[u], 8 * t0 + 16)
                        sp.sem_inc(store_free, 1)

            @block.gpsimd
            def _(g):
                g.dma_start(edge_src[0:EPART, :], src.rearrange("(p c) -> p c", p=EPART)).then_inc(e_in, 16)
                g.dma_start(edge_dst[0:EPART, :], dst.rearrange("(p c) -> p c", p=EPART)).then_inc(e_in, 16)
                g.memset(s.ident[:, :], 0.0).then_inc(consts, 1)
                g.memset(s.ones[:, :], 1.0).then_inc(consts, 1)
                g.iota(s.row_iota[:, :], [[1, P]], base=0, channel_multiplier=0,
                       allow_small_or_imprecise_dtypes=True).then_inc(consts, 1)
                g.iota(node_id[:, :], [[P, TILES]], base=0, channel_multiplier=1,
                       allow_small_or_imprecise_dtypes=True).then_inc(consts, 1)
                g.iota(window_key[:, :], [[0, 1]], base=0, channel_multiplier=P,
                       allow_small_or_imprecise_dtypes=True).then_inc(consts, 1)
                g.memset(pos[:, :], 0.0).then_inc(consts, 1)
                g.memset(edge_pad[:, :, 0:1], 0).then_inc(consts, 1)
                g.memset(edge_pad[:, :, 1:2].bitcast(F32), float(NO_NODE)).then_inc(consts, 1)
                g.wait_ge(consts, 8)
                g.affine_select(out=s.ident[:, :], in_=s.ident[:, :], compare_op=ALU.not_equal, fill=1.0,
                                base=0, pattern=[[-1, P]], channel_multiplier=1).then_inc(consts, 1)
                g.tensor_scalar(s.valid[:, :], node_id[:, :], float(N), None, ALU.is_lt).then_inc(consts, 1)
                g.wait_ge(e_in, 32)
                g.tensor_copy(edge_pair[0:EPART, :, 0], edge_src[0:EPART, :]).then_inc(pair_ready, 1)
                g.tensor_copy(edge_pair[0:EPART, :, 1:2].bitcast(F32), edge_dst[0:EPART, :]).then_inc(pair_ready, 1)
                g.wait_ge(pair_ready, 2)
                g.dma_start(s.edges[0:E, :].rearrange("(p c) k -> p c k", p=EPART), edge_pair[0:EPART, :, :]).then_inc(pair_stored, 16)
                g.dma_start(s.edges[E:E + SPAN, :].rearrange("(p c) k -> p c k", p=P), edge_pad[:, :, :]).then_inc(pair_stored, 16)
                dst_rows = dst.rearrange("(e o) -> e o", o=1)
                step = 1 << (E.bit_length() - 1)
                n = 0
                k = 0
                while step:
                    g.tensor_scalar(cand[:, :], pos[:, :], float(step), None, ALU.add).then_inc(pool_step, 1)
                    g.wait_ge(pool_step, n + 1)
                    g.tensor_scalar(probe[:, :], cand[:, :], float(E), -1.0, ALU.min, ALU.add).then_inc(pool_step, 1)
                    g.tensor_scalar(inside[:, :], cand[:, :], float(E), float(step), ALU.is_le, ALU.mult).then_inc(pool_step, 1)
                    g.wait_ge(pool_step, n + 3)
                    g.indirect_dma_start(found[:, :], None, dst_rows,
                                         bass.IndirectOffsetOnAxis(ap=probe[:, :], axis=0)).then_inc(probed, 16)
                    g.wait_ge(probed, 16 * (k + 1))
                    g.tensor_scalar(below[:, :], found[:, :], window_key[:, :], inside[:, :], ALU.is_lt, ALU.mult).then_inc(pool_step, 1)
                    g.wait_ge(pool_step, n + 4)
                    g.tensor_tensor(pos[:, :], pos[:, :], below[:, :], ALU.add).then_inc(pool_step, 1)
                    g.wait_ge(pool_step, n + 5)
                    n += 5
                    k += 1
                    step >>= 1
                g.tensor_copy(s.first_edge[:, :], pos[:, :]).then_inc(pool_step, 1)
                g.wait_ge(pair_stored, 32)

            @block.vector
            def _(v):
                v.memset(s.x_tiles[:, TILES - 1:TILES + 1, :], 0.0).then_inc(pad_set, 1)
                v.wait_ge(w_in, 6 * 16)
                for c in range(C):
                    for a in range(2):
                        v.tensor_tensor(att_w[:, 2 * c + a, :], w_ext[:, c, 0:D], att[:, a, :], ALU.mult).then_inc(w_steps, 1)
                v.wait_ge(w_steps, 4)
                for c in range(C):
                    for a in range(2):
                        v.tensor_reduce(w_ext[:, c, D + GH * a:D + GH * (a + 1)],
                                        att_w[:, 2 * c + a, :].rearrange("p (h f) -> p h f", h=GH), AX.X, ALU.add).then_inc(w_ready, 1)
                for c in range(C):
                    v.tensor_scalar(wq[:, c, :], wq[:, c, :], wn[:, c:c + 1], None, ALU.mult).then_inc(w_ready, 1)
                for j in range(7):
                    v.wait_ge(x_in[j], 16 if j < 6 else 32)
                    with v.Fori(14 * j, 14 * (j + 1) + (j == 6)) as t:
                        v.bn_stats(stats[:, bass.ds(t, 1), :].rearrange("p t k -> p (t k)"),
                                   s.x_tiles[:, bass.ds(t, 1), :].rearrange("p t d -> p (t d)")).then_inc(stats_done, 1)
                v.wait_ge(stats_done, TILES + 1)
                mean_and_variance(v, stats, mean[:, :], var[:, :], tmp[:, :], agg_done)
                v.tensor_scalar(tmp[:, :], var[:, :], 1e-5, None, ALU.add).then_inc(var_eps, 1)
                v.wait_ge(var_sqrt, 1)
                v.reciprocal(s.ln_scale[:, :], tmp[:, :]).then_inc(chain, 1)
                v.wait_ge(chain, 1)
                v.tensor_tensor(tmp[:, :], s.ln_scale[:, :], s.ln_scale[:, :], ALU.mult).then_inc(chain, 1)
                v.scalar_tensor_tensor(s.ln_bias[:, :], mean[:, :], -1.0, s.ln_scale[:, :], ALU.mult, ALU.mult).then_inc(chain, 1)
                v.wait_ge(chain, 3)
                v.tensor_tensor(tmp[:, :], tmp[:, :], var[:, :], ALU.mult).then_inc(chain, 1)
                v.wait_ge(chain, 4)
                v.tensor_scalar(tmp[:, :], tmp[:, :], 1e-6, None, ALU.add).then_inc(ms_eps, 1)
                v.wait_ge(ms_sqrt, 1)
                v.reciprocal(tmp[:, :], h_scale[:, :]).then_inc(chain, 1)
                v.wait_ge(chain, 5)
                v.tensor_tensor(r_scale[:, :], s.ln_scale[:, :], tmp[:, :], ALU.mult).then_inc(chain, 1)
                v.tensor_tensor(r_bias[:, :], s.ln_bias[:, :], tmp[:, :], ALU.mult).then_inc(chain, 1)
                v.wait_ge(chain, 7)

                def normalise(t, u):
                    v.tensor_scalar(r[:, u, :], s.x_tiles[:, bass.ds(t, 1), :].rearrange("p t d -> p (t d)"),
                                    r_scale[:, bass.ds(t, 1)], r_bias[:, bass.ds(t, 1)], ALU.mult, ALU.add).then_inc(r_ready, 1)

                v.sem_inc(h_free, 1)
                v.sem_inc(k_free, 2)
                v.sem_inc(q_free, 2)
                normalise(0, 0)
                with v.Fori(0, TILES - 1, 2) as t0:
                    for u in range(2):
                        t = t0 + u
                        normalise(t + 1, 1 - u)
                        v.wait_ge(kv_psum, t + 1)
                        v.tensor_scalar(k_exp[:, u, :], ps_kv[:, u, 0:D], 0.0, None, ALU.min).then_inc(k_min, 1)
                        v.wait_ge(q_psum, t + 1)
                        v.tensor_scalar(q_exp[:, u, :], ps_q[:, u, 0:D], 0.0, None, ALU.min).then_inc(q_min, 1)
                        v.wait_ge(k_expd, t + 1)
                        v.scalar_tensor_tensor(keys[:, u, :], ps_kv[:, u, 0:D], 0.0, k_exp[:, u, :],
                                               ALU.max, ALU.add).then_inc(k_ready, 1)
                        v.wait_ge(k_ready, t + 1)
                        v.sem_inc(k_free, 1)
                        v.wait_ge(h_psum, t + 1)
                        v.wait_ge(store_free, t + 1)
                        v.tensor_scalar(h_out[:, u, :], ps_h[:, 0:ROW], h_scale[:, bass.ds(t, 1)], None, ALU.mult).then_inc(h_ready, 1)
                        v.tensor_scalar(s.scores[:, bass.ds(t, 1), :].rearrange("p t k -> p (t k)"), ps_h[:, D:D + 2 * GH],
                                        h_scale[:, bass.ds(t, 1)], None, ALU.mult).then_inc(h_ready, 1)
                        v.wait_ge(h_ready, 2 * t + 2)
                        v.sem_inc(h_free, 1)
                        v.wait_ge(q_expd, t + 1)
                        v.scalar_tensor_tensor(q_out[:, u, :], ps_q[:, u, 0:D], 0.0, q_exp[:, u, :],
                                               ALU.max, ALU.add).then_inc(q_ready, 1)
                        v.wait_ge(q_ready, t + 1)
                        v.sem_inc(q_free, 1)
                v.wait_ge(acc_done, 1)
                v.memset(s.kv[:, :, :], 0.0).then_inc(kv_parts, 1)
                v.wait_ge(kv_parts, 1)
                for j in range(4):
                    a, b = MF * j, MF * (j + 1)
                    v.tensor_copy(s.kv[a:b, :, a:b], acc[a:b, :, a:b]).then_inc(kv_parts, 1)
                    v.tensor_copy(s.kv[a:b, :, P + j:P + j + 1], acc[a:b, :, P:P + 1]).then_inc(kv_parts, 1)

            @block.scalar
            def _(act):
                act.wait_ge(var_eps, 1)
                act.activation(tmp[:, :], tmp[:, :], ACT.Sqrt).then_inc(var_sqrt, 1)
                act.wait_ge(ms_eps, 1)
                act.activation(h_scale[:, :], tmp[:, :], ACT.Sqrt).then_inc(ms_sqrt, 1)

                def copy_rT(t, u):
                    act.wait_ge(rT_psum, t + 1)
                    act.activation(rT[:, u, :, :], ps_t[:, u, 0:D].rearrange("p (c n) -> p c n", c=C), ACT.Copy).then_inc(rT_ready, 1)

                copy_rT(0, 0)
                with act.Fori(0, TILES - 1, 2) as t0:
                    for u in range(2):
                        t = t0 + u
                        act.wait_ge(k_min, t + 1)
                        act.activation(values[:, u, :], ps_kv[:, u, D:2 * D], ACT.Copy).then_inc(v_ready, 1)
                        act.activation(k_exp[:, u, :], k_exp[:, u, :], ACT.Exp).then_inc(k_expd, 1)
                        act.wait_ge(q_min, t + 1)
                        act.activation(q_exp[:, u, :], q_exp[:, u, :], ACT.Exp).then_inc(q_expd, 1)
                        copy_rT(t + 1, 1 - u)

            @block.tensor
            def _(pe):
                pe.wait_ge(consts, 10)
                pe.wait_ge(w_ready, 6)

                def transpose_r(t, u):
                    pe.wait_ge(r_ready, t + 1)
                    for c in range(C):
                        mm = pe.transpose(ps_t[:, u, c * P:(c + 1) * P], r[:, u, c * P:(c + 1) * P], s.ident[:, :])
                    mm.then_inc(rT_psum, 1)

                pe.wait_ge(pad_set, 1)
                nothing = s.x_tiles[:, TILES, :]
                pe.matmul(ps_acc[:, 0:D], s.ident[:, :], nothing, start=True, stop=False, skip_group_check=True)
                pe.matmul(ps_acc[:, D:C * (P + 1)], s.ident[:, :], nothing[:, 0:C], start=False, stop=False,
                          skip_group_check=True)
                transpose_r(0, 0)
                with pe.Fori(0, TILES - 1, 2) as t0:
                    for u in range(2):
                        t = t0 + u
                        pe.wait_ge(rT_ready, t + 1)
                        pe.wait_ge(k_free, t + 1)
                        for c in range(C):
                            mm = pe.matmul(ps_kv[:, u, :], rT[:, u, c, :], wq[:, c, D:3 * D], start=(c == 0), stop=(c == C - 1))
                        mm.then_inc(kv_psum, 1)
                        pe.wait_ge(q_free, t + 1)
                        for m in range(C):
                            for c in range(C):
                                mm = pe.matmul(ps_q[:, u, m * P:(m + 1) * P], wq[:, c, m * P:(m + 1) * P], rT[:, u, c, :],
                                               start=(c == 0), stop=(c == C - 1))
                        mm.then_inc(q_psum, 1)
                        pe.wait_ge(h_free, t + 1)
                        for c in range(C):
                            mm = pe.matmul(ps_h[:, 0:D + 2 * GH], rT[:, u, c, :], w_ext[:, c, :], start=(c == 0), stop=(c == C - 1))
                        mm.then_inc(h_psum, 1)
                        transpose_r(t + 1, 1 - u)
                        pe.wait_ge(k_ready, t + 1)
                        pe.wait_ge(v_ready, t + 1)
                        for m in range(C):
                            pe.matmul(acc[:, m, 0:P], keys[:, u, m * P:(m + 1) * P], values[:, u, m * P:(m + 1) * P],
                                      start=False, stop=False, skip_group_check=True)
                            pe.matmul(acc[:, m, P:P + 1], keys[:, u, m * P:(m + 1) * P], s.valid[:, bass.ds(t, 1)],
                                      start=False, stop=False, skip_group_check=True)
                pe.matmul(acc[:, 0, P:P + 1], s.ident[:, :], s.x_tiles[:, TILES, 0:1],
                          start=False, stop=True, skip_group_check=True).then_inc(acc_done, 1)


def plan_groups(nc, s, plan):
    with ExitStack() as ctx:
        def sb(name, shape, dt=F32):
            return ctx.enter_context(nc.sbuf_tensor(name, shape, dt))

        def sem(name):
            return nc.alloc_semaphore(name=name)

        bounds = sb("bounds", [1, P])
        length = sb("length", [1, P])
        length_i = sb("length_i", [1, P], I32)
        ends = sb("ends", [1, P])
        ahead = sb("ahead", [1, P])
        zeros = sb("zeros", [1, P])
        columns = sb("columns", [P, 4])
        group_id = sb("group_id", [P, GROUPS])
        after = sb("after", [P, GROUPS])
        owner = sb("owner", [P, GROUPS])
        from_window = sb("from_window", [1, GROUPS])
        window_f = sb("window_f", [1, GROUPS])
        peak = sb("peak", [P, GH])
        peak_all = sb("peak_all", [P, GH])
        sloped = sb("sloped", [P, TILES, GH])
        ps = [ctx.enter_context(nc.psum_tensor(f"plan_ps{j}", [P, 512], F32)) for j in range(4)]

        iotas = sem("b_iotas")
        step = sem("b_step")
        turned = sem("b_turned")
        columned = sem("b_columned")
        masks = sem("b_masks")
        counted = sem("b_counted")
        evacuated = sem("b_evacuated")
        peaked = sem("b_peaked")
        reduced = sem("b_reduced")
        shifted = sem("b_shifted")
        CH = 448
        chunks = [(a, min(a + CH, GROUPS)) for a in range(0, GROUPS, CH)]

        with nc.Block() as block:

            @block.gpsimd
            def _(g):
                g.iota(group_id[:, :], [[1, GROUPS]], base=0, channel_multiplier=0,
                       allow_small_or_imprecise_dtypes=True).then_inc(iotas, 1)
                g.wait_ge(peaked, 1)
                g.partition_all_reduce(peak_all[:, :], peak[:, :], P, RMAX).then_inc(reduced, 1)

            @block.tensor
            def _(pe):
                pe.transpose(ps[0][0:1, 0:P], s.first_edge[:, :], s.ident[:, :]).then_inc(turned, 1)
                pe.wait_ge(step, 8)
                for j, row in enumerate((bounds, ahead, ends)):
                    mm = pe.matmul(ps[1][:, j:j + 1], row[0:1, :], s.ones[0:1, 0:1], start=True, stop=True)
                mm.then_inc(columned, 1)
                for k, (a, b) in enumerate(chunks):
                    pe.wait_ge(masks, 2)
                    if k >= 1:
                        pe.wait_ge(evacuated, 3 * k)
                    pe.matmul(ps[2][:, 0:b - a], s.ones[0:TILES, :], after[0:TILES, a:b], start=True, stop=True)
                    pe.matmul(ps[3][0:1, 0:b - a], columns[0:TILES, 3:4], owner[0:TILES, a:b], start=True, stop=True).then_inc(counted, 1)

            @block.vector
            def _(v):
                v.memset(zeros[:, :], 0.0).then_inc(step, 1)
                v.memset(bounds[:, :], 0.0).then_inc(step, 1)
                v.memset(ahead[:, :], 0.0).then_inc(step, 1)
                v.wait_ge(turned, 1)
                v.wait_ge(step, 3)
                v.tensor_copy(bounds[0:1, :], ps[0][0:1, 0:P]).then_inc(step, 1)
                v.wait_ge(step, 4)
                v.tensor_tensor(length[0:1, 0:P - 1], bounds[0:1, 1:P], bounds[0:1, 0:P - 1], ALU.subtract).then_inc(step, 1)
                v.wait_ge(step, 5)
                v.tensor_scalar(length_i[0:1, 0:P - 1], length[0:1, 0:P - 1], float(SPAN - 1), None, ALU.add).then_inc(step, 1)
                v.wait_ge(step, 6)
                v.tensor_scalar(length_i[0:1, 0:P - 1], length_i[0:1, 0:P - 1], SPAN.bit_length() - 1, None,
                                ALU.arith_shift_right).then_inc(step, 1)
                v.memset(ends[:, :], 0.0).then_inc(shifted, 1)
                v.wait_ge(step, 7)
                v.wait_ge(shifted, 1)
                v.tensor_copy(length[0:1, 0:P - 1], length_i[0:1, 0:P - 1]).then_inc(shifted, 1)
                v.wait_ge(shifted, 2)
                v.tensor_tensor_scan(ends[0:1, 0:P - 1], length[0:1, 0:P - 1], zeros[0:1, 0:P - 1], 0.0,
                                     ALU.add, ALU.add).then_inc(shifted, 1)
                v.wait_ge(shifted, 3)
                v.tensor_copy(ahead[0:1, 1:P], ends[0:1, 0:P - 1]).then_inc(step, 1)
                v.wait_ge(columned, 1)
                v.tensor_copy(columns[:, 0:3], ps[1][:, 0:3]).then_inc(shifted, 1)
                v.wait_ge(shifted, 4)
                v.scalar_tensor_tensor(columns[:, 3:4], columns[:, 1:2], -float(SPAN), columns[:, 0:1],
                                       ALU.mult, ALU.add).then_inc(shifted, 1)
                v.wait_ge(iotas, 1)
                v.wait_ge(shifted, 5)
                v.tensor_scalar(owner[:, :], group_id[:, :], columns[:, 1:2], None, ALU.is_ge).then_inc(shifted, 1)
                v.tensor_scalar(after[:, :], group_id[:, :], columns[:, 2:3], None, ALU.is_ge).then_inc(masks, 1)
                v.wait_ge(shifted, 6)
                v.wait_ge(masks, 1)
                v.tensor_tensor(owner[:, :], owner[:, :], after[:, :], ALU.subtract).then_inc(masks, 1)
                for k, (a, b) in enumerate(chunks):
                    v.wait_ge(counted, k + 1)
                    v.tensor_scalar(plan.target0[:, a:b], ps[2][:, 0:b - a], float(P), None, ALU.mult).then_inc(evacuated, 1)
                    v.tensor_scalar(plan.window[0:1, a:b], ps[2][0:1, 0:b - a], float(TILES - 1), None, ALU.min).then_inc(evacuated, 1)
                    v.scalar_tensor_tensor(from_window[0:1, a:b], group_id[0:1, a:b], float(SPAN), ps[3][0:1, 0:b - a],
                                           ALU.mult, ALU.add).then_inc(evacuated, 1)
                v.wait_ge(evacuated, 3 * len(chunks))
                v.tensor_scalar(plan.edge0[0:1, :], from_window[0:1, :], float(E), None, ALU.min).then_inc(shifted, 1)
                v.tensor_reduce(peak[:, :], s.scores[:, :, 0:GH].rearrange("p t h -> p h t"), AX.X, ALU.max).then_inc(peaked, 1)
                v.tensor_copy(s.shift[:, :, 0:GH], s.scores[:, :, GH:2 * GH]).then_inc(shifted, 1)
                v.wait_ge(reduced, 1)
                v.tensor_tensor(sloped[:, :, :], s.scores[:, :, GH:2 * GH],
                                peak_all[:, :].unsqueeze(1).to_broadcast([P, TILES, GH]), ALU.add).then_inc(shifted, 1)
                v.wait_ge(shifted, 9)
                v.scalar_tensor_tensor(s.shift[:, :, GH:2 * GH], sloped[:, :, :], 0.2, sloped[:, :, :],
                                       ALU.mult, ALU.max).then_inc(shifted, 1)
                v.memset(s.big[:, :], 0.0).then_inc(shifted, 1)


def attend_edges(nc, s, plan):
    with ExitStack() as ctx:
        def sb(name, shape, dt=F32):
            return ctx.enter_context(nc.sbuf_tensor(name, shape, dt))

        def sem(name):
            return nc.alloc_semaphore(name=name)

        pairs = sb("pairs", [P, RING, G, 2], I32)
        rows = sb("rows", [P, RING, G * ROW])
        rows4 = rows[:, :, :].rearrange("p r (g n) -> p r g n", g=G)
        rel = sb("rel", [P, RING, G])
        hot = sb("hot", [P, RING, G, P])
        hotT = sb("hotT", [P, 2, G, P])
        e1 = sb("e1", [P, 2, G, GH])
        e2 = sb("e2", [P, 2, G, GH])
        e3 = sb("e3", [P, 2, G, GH])
        msg = sb("msg", [P, 4, G, ROW])
        ps_hot = ctx.enter_context(nc.psum_tensor("ps_hot", [P, 2, 512], F32))
        ps_tgt = ctx.enter_context(nc.psum_tensor("ps_tgt", [P, 2, 512], F32))
        ps_sum = ctx.enter_context(nc.psum_tensor("ps_sum", [P, 2, 512], F32))

        zeros = sb("c_zeros", [P, ZERO_TILES, D])
        zeros_set = sem("c_zeros_set")
        zeros_stored = sem("c_zeros_stored")
        pairs_in = [sem(f"c_pairs_in{j}") for j in range(RING)]
        rows_in = [sem(f"c_rows_in{j}") for j in range(RING)]
        pairs_seen = sem("c_pairs_seen")
        rel_done = sem("c_rel_done")
        hot_ready = sem("c_hot_ready")
        hotT_psum = sem("c_hotT_psum")
        hotT_ready = sem("c_hotT_ready")
        tgt_psum = sem("c_tgt_psum")
        scored = sem("c_scored")
        leaked = sem("c_leaked")
        e_shifted = sem("c_e_shifted")
        e_ready = sem("c_e_ready")
        w_ready = sem("c_w_ready")
        msg_ready = sem("c_msg_ready")
        sum_psum = sem("c_sum_psum")
        sum_added = sem("c_sum_added")

        LOOPS = (GROUPS - HEAD) // RING

        with nc.Block() as block:

            @block.sync
            def _(sp):
                def load(n, j):
                    first = sp.value_load(plan.edge0[0:1, bass.ds(n, 1)], min_val=0, max_val=E)
                    sp.dma_start(pairs[:, j, :, :], s.edges[bass.ds(first, SPAN), :].rearrange("(p g) k -> p g k", p=P))\
                      .then_inc(pairs_in[j], 16)

                for n in range(RING):
                    load(n, n)
                with sp.Fori(0, LOOPS - 1) as i:
                    for j in range(RING):
                        n = i * RING + RING + j
                        sp.wait_ge(msg_ready, n - RING + 1)
                        load(n, j)
                for n in range(LOOPS * RING, GROUPS):
                    sp.wait_ge(msg_ready, n - RING + 1)
                    load(n, n % RING)

            @block.gpsimd
            def _(g):
                def gather(j):
                    for k in range(G):
                        g.indirect_dma_start(rows[:, j, k * ROW:(k + 1) * ROW], None, s.node_rows,
                                             bass.IndirectOffsetOnAxis(ap=pairs[:, j, k, 0:1], axis=0)).then_inc(rows_in[j], 16)

                g.memset(zeros[:, :, :], 0.0).then_inc(zeros_set, 1)
                with g.Fori(0, LOOPS) as i:
                    for j in range(RING):
                        g.wait_ge(pairs_in[j], 16 * i + 16)
                        g.sem_inc(pairs_seen, 1)
                        gather(j)
                for n in range(LOOPS * RING, GROUPS):
                    g.wait_ge(pairs_in[n % RING], 16 * (n // RING + 1))
                    gather(n % RING)

            def in_groups(eng, steps, lag):
                in_step(eng, steps, lag, GROUPS, HEAD, RING)

            @block.vector
            def _(v):
                def relative(n, j, turn):
                    v.wait_ge(pairs_in[j], turn * 16 + 16)
                    v.tensor_scalar(rel[:, j, :], pairs[:, j, :, 1].bitcast(F32), plan.target0[:, bass.ds(n, 1)], None,
                                    ALU.subtract).then_inc(rel_done, 1)

                def one_hot(n, j, turn):
                    v.wait_ge(rel_done, n + 1)
                    v.tensor_tensor(hot[:, j, :, :], s.row_iota[:, :].unsqueeze(1).to_broadcast([P, G, P]),
                                    rel[:, j, :].unsqueeze(2).to_broadcast([P, G, P]), ALU.is_equal).then_inc(hot_ready, 1)

                def target(j):
                    return ps_tgt[:, j % 2, 0:G * 2 * GH].rearrange("p (g k) -> p g k", g=G)

                def score(n, j, turn):
                    v.wait_ge(rows_in[j], turn * (16 * G) + 16 * G)
                    v.wait_ge(tgt_psum, n + 1)
                    v.tensor_tensor(e1[:, j % 2, :, :], rows4[:, j, :, D:ROW], target(j)[:, :, 0:GH], ALU.add).then_inc(scored, 1)

                def leaky(n, j, turn):
                    v.wait_ge(scored, n + 1)
                    b = j % 2
                    v.scalar_tensor_tensor(e2[:, b, :, :], e1[:, b, :, :], 0.2, e1[:, b, :, :], ALU.mult, ALU.max).then_inc(leaked, 1)

                def shifted(n, j, turn):
                    v.wait_ge(leaked, n + 1)
                    v.tensor_tensor(e3[:, j % 2, :, :], e2[:, j % 2, :, :], target(j)[:, :, GH:2 * GH], ALU.subtract).then_inc(e_shifted, 1)

                def bounded(n, j, turn):
                    v.wait_ge(e_shifted, n + 1)
                    v.tensor_scalar(e1[:, j % 2, :, :], e3[:, j % 2, :, :], 0.0, None, ALU.min).then_inc(e_ready, 1)

                def weigh(n, j, turn):
                    v.wait_ge(w_ready, n + 1)
                    m = msg[:, j % 4, :, :]
                    for k in range(G):
                        mm = v.tensor_tensor(m[:, k, 0:D].rearrange("p (h f) -> p h f", h=GH),
                                             rows4[:, j, k, 0:D].rearrange("p (h f) -> p h f", h=GH),
                                             m[:, k, D:ROW].unsqueeze(2).to_broadcast([P, GH, GF]), ALU.mult)
                    mm.then_inc(msg_ready, 1)

                def add_sum(n, j, turn):
                    w = v.value_load(plan.window[0:1, bass.ds(n, 1)], min_val=0, max_val=TILES - 1)
                    v.wait_ge(sum_psum, n + 1)
                    from_item(v, sum_added, n, 1, n)
                    dest = s.sums[:, bass.ds(w, 1), :].rearrange("p t d -> p (t d)")
                    v.tensor_tensor(dest, dest, ps_sum[:, j % 2, 0:ROW], ALU.add).then_inc(sum_added, 1)

                in_groups(v, [relative, score, one_hot, leaky, add_sum, shifted, weigh, bounded], [0, 2, 0, 2, 5, 2, 3, 2])

            @block.scalar
            def _(act):
                def copy_hotT(n, j, turn):
                    act.wait_ge(hotT_psum, n + 1)
                    act.activation(hotT[:, j % 2, :, :], ps_hot[:, j % 2, 0:G * P].rearrange("p (g n) -> p g n", g=G),
                                   ACT.Copy).then_inc(hotT_ready, 1)

                def weights(n, j, turn):
                    act.wait_ge(e_ready, n + 1)
                    act.activation(msg[:, j % 4, :, D:ROW], e1[:, j % 2, :, :], ACT.Exp).then_inc(w_ready, 1)

                act.wait_ge(zeros_set, 1)
                for a in range(0, EX_TILES, ZERO_TILES):
                    b = min(a + ZERO_TILES, EX_TILES)
                    act.dma_start(s.expert_in[a * P:b * P, :].rearrange("(t p) d -> p t d", p=P), zeros[:, 0:b - a, :]).then_inc(zeros_stored, 16)
                in_groups(act, [copy_hotT, weights], [0, 2])
                act.wait_ge(zeros_stored, 16 * -(-EX_TILES // ZERO_TILES))

            @block.tensor
            def _(pe):
                def turn_hot(n, j, turn):
                    pe.wait_ge(hot_ready, n + 1)
                    for k in range(G):
                        mm = pe.transpose(ps_hot[:, j % 2, k * P:(k + 1) * P], hot[:, j, k, :], s.ident[:, :])
                    mm.then_inc(hotT_psum, 1)

                def target_scores(n, j, turn):
                    w = pe.value_load(plan.window[0:1, bass.ds(n, 1)], min_val=0, max_val=TILES - 1)
                    pe.wait_ge(hotT_ready, n + 1)
                    from_item(pe, e_ready, n, 2, n - 1)
                    for k in range(G):
                        mm = pe.matmul(ps_tgt[:, j % 2, k * 2 * GH:(k + 1) * 2 * GH], hotT[:, j % 2, k, :],
                                       s.shift[:, bass.ds(w, 1), :].rearrange("p t k -> p (t k)"), start=True, stop=True)
                    mm.then_inc(tgt_psum, 1)

                def sum_group(n, j, turn):
                    pe.wait_ge(msg_ready, n + 1)
                    for k in range(G):
                        mm = pe.matmul(ps_sum[:, j % 2, 0:ROW], hot[:, j, k, :], msg[:, j % 4, k, :],
                                       start=(k == 0), stop=(k == G - 1))
                    mm.then_inc(sum_psum, 1)

                in_groups(pe, [turn_hot, target_scores, sum_group], [0, 1, 4])


def combine(nc, s, x, gat_bias, w_out, b_out):
    with ExitStack() as ctx:
        def sb(name, shape, dt=F32):
            return ctx.enter_context(nc.sbuf_tensor(name, shape, dt))

        def psum(name):
            return ctx.enter_context(nc.psum_tensor(name, [P, 2, 512], F32))

        def sem(name):
            return nc.alloc_semaphore(name=name)

        h_row = sb("h_row", [P, 2, ROW])
        q_in = sb("q_in", [P, 2, D])
        x_row = sb("x_row", [P, 2, D])
        self_w = sb("self_w", [P, TILES, GH])
        self_t = sb("self_t", [P, TILES, GH])
        rden = sb("rden", [P, TILES, GH])
        xn = sb("xn", [P, 2, D])
        xn_bias = sb("xn_bias", [P, 2, D])
        xn_bout = sb("xn_bout", [P, 2, D])
        own = sb("own", [P, 3, D])
        z = sb("z", [P, 2, MH])
        heads = sb("heads", [P, 2, D])
        headsT = sb("headsT", [P, 2, C, P])
        wo = sb("wo", [P, C, D])
        bias_b = sb("bias_b", [P, D])
        bout_b = sb("bout_b", [P, D])
        hh = sb("hh", [P, 2, D])
        ps_a = psum("ps_a")
        ps_at = psum("ps_at")
        ps_o = psum("ps_o")

        w_in = sem("d_w_in")
        loaded = [sem(f"d_loaded{u}") for u in range(2)]
        self_step = sem("d_self_step")
        self_exp = sem("d_self_exp")
        xn_ready = sem("d_xn_ready")
        xn_biased = sem("d_xn_biased")
        attended = sem("d_attended")
        z_step = sem("d_z_step")
        heads_ready = sem("d_heads_ready")
        headsT_psum = sem("d_headsT_psum")
        headsT_ready = sem("d_headsT_ready")
        out_psum = sem("d_out_psum")
        hh_ready = sem("d_hh_ready")
        own_step = sem("d_own_step")
        tile_done = sem("d_tile_done")
        stored = [sem(f"d_stored{u}") for u in range(2)]
        hh_free = sem("d_hh_free")

        with nc.Block() as block:

            @block.sync
            def _(sp):
                sp.dma_start(wo[:, :, :], w_out.rearrange("(c p) n -> p c n", p=P)).then_inc(w_in, 16)
                sp.dma_start(bias_b[:, :], gat_bias.partition_broadcast(P)).then_inc(w_in, 16)
                sp.dma_start(bout_b[:, :], b_out.partition_broadcast(P)).then_inc(w_in, 16)
                sp.sem_inc(tile_done, 2)

                def load(t, u, rows):
                    sp.wait_ge(tile_done, t + 1)
                    sp.dma_start(h_row[:, u, :], s.node_rows[bass.ds(t * P, P), :]).then_inc(loaded[u], 16)
                    sp.dma_start(q_in[:, u, :], s.queries[bass.ds(t * P, P), :]).then_inc(loaded[u], 16)
                    sp.dma_start(x_row[0:rows, u, :], x[bass.ds(t * P, rows), :]).then_inc(loaded[u], 16)

                with sp.Fori(0, TILES - 3, 2) as t0:
                    load(t0, 0, P)
                    load(t0 + 1, 1, P)
                load(TILES - 2, 0, P)
                load(TILES - 1, 1, TAIL)

            @block.gpsimd
            def _(g):
                g.sem_inc(hh_free, 2)
                g.wait_ge(w_in, 48)
                with g.Fori(0, TILES - 1, 2) as t0:
                    for u in range(2):
                        t = t0 + u
                        g.wait_ge(xn_ready, t + 1)
                        g.tensor_tensor(xn_bias[:, u, :], xn[:, u, :], bias_b[:, :], ALU.add).then_inc(xn_biased, 1)
                        g.tensor_tensor(xn_bout[:, u, :], xn[:, u, :], bout_b[:, :], ALU.add).then_inc(xn_biased, 1)

            @block.scalar
            def _(act):
                act.wait_ge(self_step, 4)
                act.activation(self_w[:, :, :], self_t[:, :, :], ACT.Exp).then_inc(self_exp, 1)

                def tile(t, t0, u, first):
                    act.wait_ge(loaded[u], 24 * t0 + 48)
                    act.wait_ge(tile_done, t + 1)
                    act.activation(xn[:, u, :], x_row[:, u, :], ACT.Identity, bias=s.ln_bias[:, bass.ds(t, 1)],
                                   scale=s.ln_scale[:, bass.ds(t, 1)]).then_inc(xn_ready, 1)
                    act.wait_ge(headsT_psum, t + 1)
                    act.activation(headsT[:, u, :, :], ps_at[:, u, 0:D].rearrange("p (c n) -> p c n", c=C),
                                   ACT.Copy).then_inc(headsT_ready, 1)
                    act.wait_ge(hh_ready, t + 1)
                    act.dma_start(s.mixed[bass.ds(t * P, P), :], hh[:, u, :]).then_inc(stored[u], 16)
                    if not first:
                        act.wait_ge(stored[1 - u], 8 * t0 + 16 * u)
                        act.sem_inc(hh_free, 1)

                tile(0, 0, 0, True)
                tile(1, 0, 1, False)
                with act.Fori(2, TILES - 1, 2) as t0:
                    tile(t0, t0, 0, False)
                    tile(t0 + 1, t0, 1, False)
                for u in range(2):
                    act.wait_ge(stored[u], 16 * (TILES // 2))

            @block.tensor
            def _(pe):
                pe.wait_ge(w_in, 48)
                with pe.Fori(0, TILES - 1, 2) as t0:
                    for u in range(2):
                        t = t0 + u
                        pe.wait_ge(loaded[u], 24 * t0 + 48)
                        pe.wait_ge(tile_done, t + 1)
                        for c in range(C):
                            mm = pe.matmul(ps_a[:, u, c * (P + 4):(c + 1) * (P + 4)], q_in[:, u, c * P:(c + 1) * P], s.kv[:, c, :],
                                           start=True, stop=True)
                        mm.then_inc(attended, 1)
                        pe.wait_ge(heads_ready, t + 1)
                        for c in range(C):
                            mm = pe.transpose(ps_at[:, u, c * P:(c + 1) * P], heads[:, u, c * P:(c + 1) * P], s.ident[:, :])
                        mm.then_inc(headsT_psum, 1)
                        pe.wait_ge(headsT_ready, t + 1)
                        for c in range(C):
                            mm = pe.matmul(ps_o[:, u, 0:D], headsT[:, u, c, :], wo[:, c, :], start=(c == 0), stop=(c == C - 1))
                        mm.then_inc(out_psum, 1)

            @block.vector
            def _(v):
                v.tensor_tensor(self_w[:, :, :], s.scores[:, :, 0:GH], s.scores[:, :, GH:2 * GH], ALU.add).then_inc(self_step, 1)
                v.wait_ge(self_step, 1)
                v.scalar_tensor_tensor(self_t[:, :, :], self_w[:, :, :], 0.2, self_w[:, :, :], ALU.mult, ALU.max).then_inc(self_step, 1)
                v.wait_ge(self_step, 2)
                v.tensor_tensor(self_w[:, :, :], self_t[:, :, :], s.shift[:, :, GH:2 * GH], ALU.subtract).then_inc(self_step, 1)
                v.wait_ge(self_step, 3)
                v.tensor_scalar(self_t[:, :, :], self_w[:, :, :], 0.0, None, ALU.min).then_inc(self_step, 1)
                v.wait_ge(self_exp, 1)
                v.tensor_tensor(self_t[:, :, :], self_w[:, :, :], s.sums[:, :, D:ROW], ALU.add).then_inc(self_step, 1)
                v.wait_ge(self_step, 5)
                v.reciprocal(rden[:, :, :], self_t[:, :, :]).then_inc(self_step, 1)
                v.wait_ge(self_step, 6)
                with v.Fori(0, TILES - 1, 2) as t0:
                    for u in range(2):
                        t = t0 + u
                        base = t * 4
                        total = s.sums[:, bass.ds(t, 1), 0:D].rearrange("p t d -> p (t d)")

                        def per_head(table):
                            return table[:, bass.ds(t, 1), :].rearrange("p t h -> p (t h)").unsqueeze(2).to_broadcast([P, GH, GF])

                        def split(a):
                            return a.rearrange("p (h f) -> p h f", h=GH)

                        v.wait_ge(loaded[u], 24 * t0 + 48)
                        v.tensor_tensor(split(own[:, 0, :]), split(h_row[:, u, 0:D]), per_head(self_w), ALU.mult).then_inc(own_step, 1)
                        v.wait_ge(attended, t + 1)
                        att = ps_a[:, u, 0:C * (P + 4)].rearrange("p (c n) -> p c n", c=C)
                        v.tensor_scalar(z[:, 0, :].rearrange("p (c j) -> p c j", c=C), att[:, :, P:P + 4], 1e-6, None, ALU.add).then_inc(z_step, 1)
                        v.wait_ge(z_step, 2 * t + 1)
                        v.reciprocal(z[:, 1, :], z[:, 0, :]).then_inc(z_step, 1)
                        v.wait_ge(z_step, 2 * t + 2)
                        for c in range(C):
                            mm = v.tensor_tensor(heads[:, u, c * P:(c + 1) * P].rearrange("p (j m) -> p j m", j=4),
                                                 att[:, c, 0:P].rearrange("p (j m) -> p j m", j=4),
                                                 z[:, 1, 4 * c:4 * c + 4].unsqueeze(2).to_broadcast([P, 4, MF]), ALU.mult)
                        mm.then_inc(heads_ready, 1)
                        v.wait_ge(own_step, base + 1)
                        v.tensor_tensor(own[:, 1, :], own[:, 0, :], total, ALU.add).then_inc(own_step, 1)
                        v.wait_ge(own_step, base + 2)
                        v.tensor_tensor(split(own[:, 2, :]), split(own[:, 1, :]), per_head(rden), ALU.mult).then_inc(own_step, 1)
                        v.wait_ge(own_step, base + 3)
                        v.wait_ge(xn_biased, 2 * t + 2)
                        v.tensor_tensor(total, own[:, 2, :], xn_bias[:, u, :], ALU.add).then_inc(own_step, 1)
                        v.wait_ge(own_step, base + 4)
                        v.bn_stats(s.gat_stats[:, bass.ds(t, 1), :].rearrange("p t k -> p (t k)"), total).then_inc(s.gat_stat, 1)
                        v.wait_ge(out_psum, t + 1)
                        v.wait_ge(hh_free, t + 1)
                        v.tensor_tensor(hh[:, u, :], ps_o[:, u, 0:D], xn_bout[:, u, :], ALU.add).then_inc(hh_ready, 1)
                        v.wait_ge(hh_ready, t + 1)
                        v.bn_stats(s.mix_stats[:, bass.ds(t, 1), :].rearrange("p t k -> p (t k)"), hh[:, u, :]).then_inc(s.mix_stat, 1)
                        v.wait_ge(s.mix_stat, t + 1)
                        v.sem_inc(tile_done, 1)


def join(nc, s, x, gamma, beta, w_norm2):
    with ExitStack() as ctx:
        def sb(name, shape, dt=F32):
            return ctx.enter_context(nc.sbuf_tensor(name, shape, dt))

        def sem(name):
            return nc.alloc_semaphore(name=name)

        x_row = sb("e_x_row", [P, 2, D])
        hh = sb("e_hh", [P, 2, D])
        mean = sb("e_mean", [P, TILES])
        var = sb("e_var", [P, TILES])
        tmp = sb("e_tmp", [P, TILES])
        a_gat = sb("a_gat", [P, TILES])
        b_gat = sb("b_gat", [P, TILES])
        a_mix = sb("a_mix", [P, TILES])
        root = sb("e_root", [P, 2, TILES])
        gamma_b = sb("gamma_b", [P, D])
        beta_b = sb("beta_b", [P, D])
        w2_b = sb("w2_b", [P, D])
        yl = sb("yl", [P, 2, D])
        hr = sb("hr", [P, 2, D])
        hw = sb("hw", [P, 2, D])
        both = sb("both", [P, 2, D])
        g1 = sb("g1", [P, 3, D])

        w_in = sem("e_w_in")
        loaded = [sem(f"e_loaded{u}") for u in range(2)]
        gat_agg = sem("e_gat_agg")
        mix_agg = sem("e_mix_agg")
        chain = sem("e_chain")
        root_in = sem("e_root_in")
        rooted = sem("e_rooted")
        scales_ready = sem("e_scales_ready")
        yl_ready = sem("e_yl_ready")
        hr_ready = sem("e_hr_ready")
        hw_ready = sem("e_hw_ready")
        both_ready = sem("e_both_ready")
        g_step = sem("e_g_step")
        tile_done = sem("e_tile_done")
        stat = sem("e_stat")
        stat_agg = sem("e_stat_agg")

        with nc.Block() as block:

            @block.sync
            def _(sp):
                sp.dma_start(gamma_b[:, :], gamma.partition_broadcast(P)).then_inc(w_in, 16)
                sp.dma_start(beta_b[:, :], beta.partition_broadcast(P)).then_inc(w_in, 16)
                sp.dma_start(w2_b[:, :], w_norm2.partition_broadcast(P)).then_inc(w_in, 16)
                sp.sem_inc(tile_done, 2)

                def load(t, u, rows):
                    sp.wait_ge(tile_done, t + 1)
                    sp.dma_start(hh[:, u, :], s.mixed[bass.ds(t * P, P), :]).then_inc(loaded[u], 16)
                    sp.dma_start(x_row[0:rows, u, :], x[bass.ds(t * P, rows), :]).then_inc(loaded[u], 16)

                with sp.Fori(0, TILES - 3, 2) as t0:
                    load(t0, 0, P)
                    load(t0 + 1, 1, P)
                load(TILES - 2, 0, P)
                load(TILES - 1, 1, TAIL)

            @block.gpsimd
            def _(g):
                g.wait_ge(w_in, 48)
                with g.Fori(0, TILES - 1, 2) as t0:
                    for u in range(2):
                        t = t0 + u
                        g.wait_ge(hr_ready, t + 1)
                        g.tensor_tensor(hw[:, u, :], hr[:, u, :], w2_b[:, :], ALU.mult).then_inc(hw_ready, 1)
                        g.wait_ge(hw_ready, t + 1)
                        g.tensor_tensor(both[:, u, :], hw[:, u, :], hh[:, u, :], ALU.add).then_inc(both_ready, 1)

            @block.scalar
            def _(act):
                act.wait_ge(root_in, 2)
                act.activation(root[:, 0, :], root[:, 0, :], ACT.Sqrt).then_inc(rooted, 1)
                act.activation(root[:, 1, :], root[:, 1, :], ACT.Sqrt).then_inc(rooted, 1)
                act.wait_ge(scales_ready, 3)
                with act.Fori(0, TILES - 1, 2) as t0:
                    for u in range(2):
                        t = t0 + u
                        act.wait_ge(tile_done, t + 1)
                        act.activation(yl[:, u, :], s.sums[:, bass.ds(t, 1), 0:D].rearrange("p t d -> p (t d)"), ACT.Identity,
                                       bias=b_gat[:, bass.ds(t, 1)], scale=a_gat[:, bass.ds(t, 1)]).then_inc(yl_ready, 1)
                        act.wait_ge(loaded[u], 16 * t0 + 32)
                        act.activation(hr[:, u, :], hh[:, u, :], ACT.Copy, scale=a_mix[:, bass.ds(t, 1)]).then_inc(hr_ready, 1)

            @block.vector
            def _(v):
                mean_and_variance(v, s.mix_stats, mean[:, :], var[:, :], tmp[:, :], mix_agg)
                v.tensor_tensor(tmp[:, :], mean[:, :], mean[:, :], ALU.mult).then_inc(chain, 1)
                v.wait_ge(chain, 1)
                v.scalar_tensor_tensor(root[:, 1, :], var[:, :], 1e-6, tmp[:, :], ALU.add, ALU.add).then_inc(root_in, 1)
                v.wait_ge(root_in, 1)
                mean_and_variance(v, s.gat_stats, mean[:, :], var[:, :], tmp[:, :], gat_agg)
                v.tensor_scalar(root[:, 0, :], var[:, :], 1e-5, None, ALU.add).then_inc(root_in, 1)
                v.wait_ge(rooted, 2)
                v.reciprocal(a_mix[:, :], root[:, 1, :]).then_inc(scales_ready, 1)
                v.reciprocal(a_gat[:, :], root[:, 0, :]).then_inc(scales_ready, 1)
                v.wait_ge(scales_ready, 2)
                v.scalar_tensor_tensor(b_gat[:, :], mean[:, :], -1.0, a_gat[:, :], ALU.mult, ALU.mult).then_inc(scales_ready, 1)
                v.wait_ge(w_in, 48)
                with v.Fori(0, TILES - 1, 2) as t0:
                    for u in range(2):
                        t = t0 + u
                        state = s.sums[:, bass.ds(t, 1), 0:D].rearrange("p t d -> p (t d)")
                        v.wait_ge(yl_ready, t + 1)
                        v.tensor_tensor(g1[:, 0, :], yl[:, u, :], gamma_b[:, :], ALU.mult).then_inc(g_step, 1)
                        v.wait_ge(g_step, 4 * t + 1)
                        v.tensor_tensor(g1[:, 1, :], g1[:, 0, :], beta_b[:, :], ALU.add).then_inc(g_step, 1)
                        v.wait_ge(g_step, 4 * t + 2)
                        v.wait_ge(loaded[u], 16 * t0 + 32)
                        v.scalar_tensor_tensor(g1[:, 2, :], g1[:, 1, :], 0.0, x_row[:, u, :], ALU.max, ALU.add).then_inc(g_step, 1)
                        v.wait_ge(g_step, 4 * t + 3)
                        v.wait_ge(both_ready, t + 1)
                        v.tensor_tensor(state, g1[:, 2, :], both[:, u, :], ALU.add).then_inc(g_step, 1)
                        v.wait_ge(g_step, 4 * t + 4)
                        v.sem_inc(tile_done, 1)
                        v.bn_stats(s.gat_stats[:, bass.ds(t, 1), :].rearrange("p t k -> p (t k)"), state).then_inc(stat, 1)
                v.wait_ge(stat, TILES)
                mean_and_variance(v, s.gat_stats, s.state_mean[:, :], s.state_var[:, :], tmp[:, :], stat_agg)


def flat(table, t, *cols):
    part = table[(slice(None), bass.ds(t, 1)) + cols]
    return part.rearrange("p t d -> p (t d)") if len(part.shape) == 3 else part


def route(nc, s, gamma, beta, Wr, br):
    with ExitStack() as ctx:
        def sb(name, shape, dt=F32):
            return ctx.enter_context(nc.sbuf_tensor(name, shape, dt))

        def psum(name):
            return ctx.enter_context(nc.psum_tensor(name, [P, 2, 512], F32))

        def sem(name):
            return nc.alloc_semaphore(name=name)

        TE = [P, TILES, EXPERTS]
        a_in = sb("a_in", [P, TILES])
        b_in = sb("b_in", [P, TILES])
        root = sb("f_root", [P, TILES])
        tmp = sb("f_tmp", [P, TILES])
        gamma_b = sb("f_gamma_b", [P, D])
        beta_b = sb("f_beta_b", [P, D])
        wr = sb("wr", [P, C, EXPERTS])
        br_b = sb("br_b", [P, EXPERTS])
        centred = sb("centred", [P, 2, D])
        scaled = sb("scaled", [P, 2, D])
        rows = sb("f_rows", [P, 2, D])
        rowsT = sb("f_rowsT", [P, 2, C, P])
        logits = sb("logits", TE)
        lane = sb("lane", TE)
        picked = [sb("picked0", TE), sb("picked1", TE)]
        work = sb("f_work", TE)
        work2 = sb("f_work2", TE)
        taken = sb("taken", TE)
        totals = sb("totals", TE)
        running = sb("running", TE)
        place = sb("place", TE)
        best = sb("best", [P, 2, TILES])
        lowest = sb("lowest", [P, 2, TILES])
        gap = sb("gap", [P, TILES])
        odds = sb("odds", [P, TILES])
        slot_f = sb("slot_f", [P, 2, TILES])
        zeros = sb("f_zeros", [P, TILES])
        tiles_i = sb("tiles_i", [P, EXPERTS], I32)
        tiles_f = sb("tiles_f", [P, EXPERTS])
        tile_end = sb("tile_end", [P, EXPERTS])
        tile_start = sb("tile_start", [P, EXPERTS])
        earlier = sb("earlier", [P, P])
        tile_id = sb("tile_id", [1, EX_TILES])
        owner = sb("f_owner", [1, 2, EX_TILES])
        ps_t = psum("f_ps_t")
        ps_l = psum("f_ps_l")
        ps_rank = psum("f_ps_rank")
        ps_tot = psum("f_ps_tot")

        w_in = sem("f_w_in")
        consts = sem("f_consts")
        chain = sem("f_chain")
        root_in = sem("f_root_in")
        rooted = sem("f_rooted")
        scales = sem("f_scales")
        centred_ready = sem("f_centred_ready")
        scaled_ready = sem("f_scaled_ready")
        rows_ready = sem("f_rows_ready")
        rowsT_psum = sem("f_rowsT_psum")
        rowsT_ready = sem("f_rowsT_ready")
        logit_psum = sem("f_logit_psum")
        logit_ready = sem("f_logit_ready")
        row_free = sem("f_row_free")
        stored = [sem(f"f_stored{u}") for u in range(2)]
        gap_ready = sem("f_gap_ready")
        odds_ready = sem("f_odds_ready")
        taken_ready = sem("f_taken_ready")
        ranked = sem("f_ranked")
        step = sem("f_step")
        HALF = TILES // 2

        with nc.Block() as block:

            @block.sync
            def _(sp):
                sp.dma_start(gamma_b[:, :], gamma.partition_broadcast(P)).then_inc(w_in, 16)
                sp.dma_start(beta_b[:, :], beta.partition_broadcast(P)).then_inc(w_in, 16)
                sp.dma_start(br_b[:, :], br.partition_broadcast(P)).then_inc(w_in, 16)
                sp.dma_start(wr[:, :, :], Wr.rearrange("(c p) e -> p c e", p=P)).then_inc(w_in, 16)
                sp.sem_inc(row_free, 2)
                with sp.Fori(0, TILES - 1, 2) as t0:
                    for u in range(2):
                        t = t0 + u
                        sp.wait_ge(rows_ready, t + 1)
                        sp.dma_start(s.ffn_in[bass.ds(t * P, P), :], rows[:, u, :]).then_inc(stored[u], 16)
                        sp.wait_ge(stored[u], 8 * t0 + 16)
                        sp.sem_inc(row_free, 1)

            @block.gpsimd
            def _(g):
                g.iota(lane[:, :, :], [[0, TILES], [1, EXPERTS]], base=0, channel_multiplier=0,
                       allow_small_or_imprecise_dtypes=True).then_inc(consts, 1)
                g.iota(tile_id[:, :], [[1, EX_TILES]], base=0, channel_multiplier=0,
                       allow_small_or_imprecise_dtypes=True).then_inc(consts, 1)
                g.memset(zeros[:, :], 0.0).then_inc(consts, 1)
                g.memset(owner[:, 0, :], 0.0).then_inc(consts, 1)
                g.memset(earlier[:, :], 1.0).then_inc(consts, 1)
                g.wait_ge(consts, 5)
                g.affine_select(out=earlier[:, :], in_=earlier[:, :], compare_op=ALU.is_gt, fill=0.0,
                                base=0, pattern=[[1, P]], channel_multiplier=-1).then_inc(consts, 1)

            @block.scalar
            def _(act):
                act.wait_ge(root_in, 1)
                act.activation(root[:, :], tmp[:, :], ACT.Sqrt).then_inc(rooted, 1)
                act.wait_ge(root_in, 2)
                act.activation(root[:, :], tmp[:, :], ACT.Sqrt).then_inc(rooted, 1)
                act.wait_ge(scales, 2)

                def centre(t, u):
                    act.activation(centred[:, u, :], flat(s.sums, t, slice(0, D)), ACT.Identity,
                                   bias=b_in[:, bass.ds(t, 1)], scale=a_in[:, bass.ds(t, 1)]).then_inc(centred_ready, 1)

                def copy_rowsT(t, u):
                    act.wait_ge(rowsT_psum, t + 1)
                    act.activation(rowsT[:, u, :, :], ps_t[:, u, 0:D].rearrange("p (c n) -> p c n", c=C), ACT.Copy).then_inc(rowsT_ready, 1)

                centre(0, 0)
                centre(1, 1)
                with act.Fori(0, TILES - 3, 2) as t0:
                    for u in range(2):
                        copy_rowsT(t0 + u, u)
                        centre(t0 + u + 2, u)
                for u in range(2):
                    copy_rowsT(TILES - 2 + u, u)
                act.wait_ge(gap_ready, 1)
                act.activation(odds[:, :], gap[:, :], ACT.Exp).then_inc(odds_ready, 1)

            @block.tensor
            def _(pe):
                pe.wait_ge(w_in, 64)
                with pe.Fori(0, TILES - 1, 2) as t0:
                    for u in range(2):
                        t = t0 + u
                        pe.wait_ge(rows_ready, t + 1)
                        for c in range(C):
                            mm = pe.transpose(ps_t[:, u, c * P:(c + 1) * P], rows[:, u, c * P:(c + 1) * P], s.ident[:, :])
                        mm.then_inc(rowsT_psum, 1)
                        pe.wait_ge(rowsT_ready, t + 1)
                        for c in range(C):
                            mm = pe.matmul(ps_l[:, u, 0:EXPERTS], rowsT[:, u, c, :], wr[:, c, :], start=(c == 0), stop=(c == C - 1))
                        mm.then_inc(logit_psum, 1)
                pe.wait_ge(consts, 6)
                pe.wait_ge(taken_ready, 1)
                for k in range(2):
                    part = taken[:, k * HALF:(k + 1) * HALF, :].rearrange("p t e -> p (t e)")
                    pe.matmul(ps_rank[:, k, 0:HALF * EXPERTS], earlier[:, :], part, start=True, stop=True)
                    mm = pe.matmul(ps_tot[:, k, 0:HALF * EXPERTS], s.ones[:, :], part, start=True, stop=True)
                mm.then_inc(ranked, 1)

            @block.vector
            def _(v):
                v.tensor_scalar(tmp[:, :], s.state_var[:, :], 1e-5, None, ALU.add).then_inc(root_in, 1)
                v.wait_ge(rooted, 1)
                v.reciprocal(a_in[:, :], root[:, :]).then_inc(chain, 1)
                v.wait_ge(chain, 1)
                v.tensor_tensor(tmp[:, :], a_in[:, :], a_in[:, :], ALU.mult).then_inc(chain, 1)
                v.wait_ge(chain, 2)
                v.tensor_tensor(b_in[:, :], tmp[:, :], s.state_var[:, :], ALU.mult).then_inc(chain, 1)
                v.wait_ge(chain, 3)
                v.tensor_scalar(tmp[:, :], b_in[:, :], 1e-5, None, ALU.add).then_inc(root_in, 1)
                v.wait_ge(rooted, 2)
                v.reciprocal(b_in[:, :], root[:, :]).then_inc(chain, 1)
                v.wait_ge(chain, 4)
                v.tensor_tensor(a_in[:, :], a_in[:, :], b_in[:, :], ALU.mult).then_inc(scales, 1)
                v.wait_ge(scales, 1)
                v.scalar_tensor_tensor(b_in[:, :], s.state_mean[:, :], -1.0, a_in[:, :], ALU.mult, ALU.mult).then_inc(scales, 1)
                v.wait_ge(w_in, 64)
                with v.Fori(0, TILES - 1, 2) as t0:
                    for u in range(2):
                        t = t0 + u
                        v.wait_ge(centred_ready, t + 1)
                        v.tensor_tensor(scaled[:, u, :], centred[:, u, :], gamma_b[:, :], ALU.mult).then_inc(scaled_ready, 1)
                        v.wait_ge(scaled_ready, t + 1)
                        v.wait_ge(row_free, t + 1)
                        v.tensor_tensor(rows[:, u, :], scaled[:, u, :], beta_b[:, :], ALU.add).then_inc(rows_ready, 1)
                        v.wait_ge(logit_psum, t + 1)
                        v.tensor_tensor(flat(logits, t, slice(0, EXPERTS)), ps_l[:, u, 0:EXPERTS], br_b[:, :], ALU.add).then_inc(logit_ready, 1)
                v.wait_ge(consts, 6)
                v.wait_ge(logit_ready, TILES)
                n = [0]

                def done(ins):
                    n[0] += 1
                    ins.then_inc(step, 1)
                    v.wait_ge(step, n[0])

                def over_experts(a):
                    return a.unsqueeze(2).to_broadcast(TE)

                for k, table in enumerate((logits, work)):
                    done(v.tensor_reduce(best[:, k, :], table[:, :, :], AX.X, ALU.max))
                    done(v.tensor_tensor(work2[:, :, :], table[:, :, :], over_experts(best[:, k, :]), ALU.is_ge))
                    done(v.scalar_tensor_tensor(place[:, :, :], work2[:, :, :], -float(EXPERTS), lane[:, :, :], ALU.mult, ALU.add))
                    done(v.tensor_reduce(lowest[:, k, :], place[:, :, :], AX.X, ALU.min))
                    done(v.tensor_tensor(picked[k][:, :, :], place[:, :, :], over_experts(lowest[:, k, :]), ALU.is_equal))
                    if k == 0:
                        done(v.tensor_scalar(work2[:, :, :], picked[0][:, :, :], -1.0, 1.0, ALU.mult, ALU.add))
                        done(v.tensor_tensor(place[:, :, :], logits[:, :, :], work2[:, :, :], ALU.mult))
                        done(v.scalar_tensor_tensor(work[:, :, :], picked[0][:, :, :], -3e38, place[:, :, :], ALU.mult, ALU.add))
                v.tensor_tensor(gap[:, :], best[:, 1, :], best[:, 0, :], ALU.subtract).then_inc(gap_ready, 1)
                done(v.tensor_tensor(work[:, :, :], picked[0][:, :, :], picked[1][:, :, :], ALU.add))
                v.tensor_tensor(taken[:, :, :], work[:, :, :], over_experts(s.valid[:, :]), ALU.mult).then_inc(taken_ready, 1)
                v.wait_ge(odds_ready, 1)
                done(v.tensor_scalar(tmp[:, :], odds[:, :], 1.0, None, ALU.add))
                done(v.reciprocal(s.weight[:, 0, :], tmp[:, :]))
                done(v.tensor_tensor(s.weight[:, 1, :], odds[:, :], s.weight[:, 0, :], ALU.mult))
                v.wait_ge(ranked, 1)
                halves = "p (t e) -> p t e"
                for k in range(2):
                    done(v.tensor_copy(totals[:, k * HALF:(k + 1) * HALF, :], ps_tot[:, k, 0:HALF * EXPERTS].rearrange(halves, e=EXPERTS)))
                for e in range(EXPERTS):
                    done(v.tensor_tensor_scan(running[:, :, e], totals[:, :, e], zeros[:, :], 0.0, ALU.add, ALU.add))
                done(v.tensor_scalar(tiles_i[:, :], running[:, TILES - 1, :], float(P - 1), None, ALU.add))
                done(v.tensor_scalar(tiles_i[:, :], tiles_i[:, :], P.bit_length() - 1, None, ALU.arith_shift_right))
                done(v.tensor_copy(tiles_f[:, :], tiles_i[:, :]))
                done(v.tensor_tensor_scan(tile_end[:, :], tiles_f[:, :], zeros[:, 0:EXPERTS], 0.0, ALU.add, ALU.add))
                done(v.tensor_tensor(tile_start[:, :], tile_end[:, :], tiles_f[:, :], ALU.subtract))
                done(v.tensor_tensor(place[:, :, :], running[:, :, :], totals[:, :, :], ALU.subtract))
                for k in range(2):
                    part = slice(k * HALF, (k + 1) * HALF)
                    done(v.tensor_tensor(work[:, part, :], place[:, part, :], ps_rank[:, k, 0:HALF * EXPERTS].rearrange(halves, e=EXPERTS), ALU.add))
                done(v.scalar_tensor_tensor(place[:, :, :], tile_start[:, :].unsqueeze(1).to_broadcast(TE), float(P), work[:, :, :], ALU.mult, ALU.add))
                for k in range(2):
                    done(v.tensor_tensor(work[:, :, :], picked[k][:, :, :], place[:, :, :], ALU.mult))
                    done(v.tensor_reduce(slot_f[:, k, :], work[:, :, :], AX.X, ALU.add))
                done(v.tensor_copy(s.slot[:, :, :], slot_f[:, :, :]))
                for e in range(EXPERTS):
                    done(v.scalar_tensor_tensor(owner[:, 1 - e % 2, :], tile_id[:, :], tile_end[0:1, e:e + 1], owner[:, e % 2, :], ALU.is_ge, ALU.add))
                done(v.tensor_scalar(s.expert_of[:, :], owner[:, EXPERTS % 2, :], float(EXPERTS - 1), None, ALU.min))


def scatter_rows(nc, s):
    with ExitStack() as ctx:
        rows = ctx.enter_context(nc.sbuf_tensor("g_rows", [P, 4, D], F32))
        index = ctx.enter_context(nc.sbuf_tensor("g_index", [P, 4, 2], I32))
        loaded = [nc.alloc_semaphore(name=f"g_loaded{j}") for j in range(4)]
        scattered = [[nc.alloc_semaphore(name=f"g_scattered{j}_{k}") for k in range(2)] for j in range(4)]
        indexed = nc.alloc_semaphore(name="g_indexed")

        with nc.Block() as block:

            @block.sync
            def _(sp):
                def load(t, j, turn):
                    row = fixed(sp, t * P)
                    times = fixed(sp, turn * 16)
                    for k in range(2):
                        from_item(sp, scattered[j][k], t, 4, times)
                    sp.dma_start(rows[:, j, :], s.ffn_in[bass.ds(row, P), :]).then_inc(loaded[j], 16)

                in_step(sp, [load], [0], TILES, 6, 4)

            @block.gpsimd
            def _(g):
                def scatter(t, j, turn, count=P):
                    g.wait_ge(loaded[j], turn * 16 + 16)
                    g.sem_inc(s.wait_seen, 1)
                    g.tensor_copy(index[:, j, :], s.slot[:, :, bass.ds(t, 1)].rearrange("p k t -> p (k t)")).then_inc(indexed, 1)
                    g.wait_ge(indexed, t + 1)
                    g.sem_inc(s.wait_seen, 1)
                    for k in range(2):
                        g.indirect_dma_start(s.expert_in, bass.IndirectOffsetOnAxis(ap=index[0:count, j, k:k + 1], axis=0),
                                             rows[0:count, j, :], None).then_inc(scattered[j][k], 16)

                def scatter_or_tail(t, j, turn):
                    scatter(t, j, turn, TAIL if isinstance(t, int) and t == TILES - 1 else P)

                in_step(g, [scatter_or_tail], [0], TILES - 1, 5, 4)
                scatter_or_tail(TILES - 1, (TILES - 1) % 4, (TILES - 1) // 4)
                for j in range(4):
                    for k in range(2):
                        g.wait_ge(scattered[j][k], 16 * len(range(j, TILES, 4)))


def run_experts(nc, s, W1, b1, W2, b2):
    with ExitStack() as ctx:
        def sb(name, shape, dt=F32):
            return ctx.enter_context(nc.sbuf_tensor(name, shape, dt))

        def psum(name):
            return ctx.enter_context(nc.psum_tensor(name, [P, 2, 512], F32))

        def sem(name):
            return nc.alloc_semaphore(name=name)

        w1 = sb("w1", [P, EXPERTS, C * HID])
        w2 = sb("w2", [P, EXPERTS, HC * D])
        b1T = sb("b1T", [P, EXPERTS * HC])
        b2_b = sb("b2_b", [P, EXPERTS, D])
        rows = sb("x_rows", [P, EX_RING, D])
        rowsT = sb("x_rowsT", [P, 2, C, P])
        pre = sb("x_pre", [P, 2, HID])
        actT = sb("x_actT", [P, 2, HC, P])
        outs = sb("x_outs", [P, EX_RING, D])
        ps_t = psum("x_ps_t")
        ps_up = psum("x_ps_up")
        ps_hT = psum("x_ps_hT")
        ps_out = psum("x_ps_out")

        w_in = sem("x_w_in")
        loaded = [sem(f"x_loaded{j}") for j in range(EX_RING)]
        stored = [sem(f"x_stored{j}") for j in range(EX_RING)]
        rowsT_psum = sem("x_rowsT_psum")
        rowsT_ready = sem("x_rowsT_ready")
        up_psum = sem("x_up_psum")
        pre_ready = sem("x_pre_ready")
        hT_psum = sem("x_hT_psum")
        act_ready = sem("x_act_ready")
        out_psum = sem("x_out_psum")
        out_ready = sem("x_out_ready")

        def in_tiles(eng, steps, lag):
            in_step(eng, steps, lag, EX_TILES, EX_HEAD, EX_RING)

        def expert(eng, n):
            return eng.value_load(s.expert_of[0:1, bass.ds(n, 1)], min_val=0, max_val=EXPERTS - 1)

        with nc.Block() as block:

            @block.sync
            def _(sp):
                for e in range(EXPERTS):
                    sp.dma_start(w1[:, e, :].rearrange("p (c n) -> p c n", c=C), W1[e].rearrange("(c p) n -> p c n", p=P)).then_inc(w_in, 16)
                    sp.dma_start(w2[:, e, :].rearrange("p (c n) -> p c n", c=HC), W2[e].rearrange("(c p) n -> p c n", p=P)).then_inc(w_in, 16)
                    for c in range(HC):
                        sp.dma_start(b1T[:, e * HC + c:e * HC + c + 1], b1[e, c * P:(c + 1) * P].rearrange("(p o) -> p o", o=1)).then_inc(w_in, 16)
                sp.dma_start(b2_b[:, :, :].rearrange("p e d -> p (e d)"), b2.rearrange("e d -> (e d)").partition_broadcast(P)).then_inc(w_in, 16)

                def load(n, j, turn):
                    row = fixed(sp, n * P)
                    from_item(sp, rowsT_psum, n, EX_RING, n - EX_RING + 1)
                    sp.dma_start(rows[:, j, :], s.expert_in[bass.ds(row, P), :]).then_inc(loaded[j], 16)

                def store(n, j, turn):
                    row = fixed(sp, n * P)
                    sp.wait_ge(out_ready, n + 1)
                    sp.dma_start(s.expert_out[bass.ds(row, P), :], outs[:, j, :]).then_inc(stored[j], 16)

                in_tiles(sp, [load, store], [0, EX_HEAD])
                for j in range(EX_RING):
                    sp.wait_ge(stored[j], 16 * (EX_TILES // EX_RING))

            WEIGHTS = 16 * (EXPERTS * (2 + HC) + 1)

            @block.tensor
            def _(pe):
                pe.wait_ge(w_in, WEIGHTS)

                def turn_rows(n, j, turn):
                    pe.wait_ge(loaded[j], turn * 16 + 16)
                    from_item(pe, rowsT_ready, n, 2, n - 1)
                    for c in range(C):
                        mm = pe.transpose(ps_t[:, j % 2, c * P:(c + 1) * P], rows[:, j, c * P:(c + 1) * P], s.ident[:, :])
                    mm.then_inc(rowsT_psum, 1)

                def up(n, j, turn):
                    e = expert(pe, n)
                    pe.wait_ge(rowsT_ready, n + 1)
                    from_item(pe, pre_ready, n, 2, n - 1)
                    for c in range(C):
                        mm = pe.matmul(ps_up[:, j % 2, :], rowsT[:, j % 2, c, :],
                                       w1[:, bass.ds(e, 1), c * HID:(c + 1) * HID].rearrange("p e n -> p (e n)"),
                                       start=(c == 0), stop=(c == C - 1))
                    mm.then_inc(up_psum, 1)

                def turn_hidden(n, j, turn):
                    pe.wait_ge(pre_ready, n + 1)
                    from_item(pe, act_ready, n, 2, n - 1)
                    for c in range(HC):
                        mm = pe.transpose(ps_hT[:, j % 2, c * P:(c + 1) * P], pre[:, j % 2, c * P:(c + 1) * P], s.ident[:, :])
                    mm.then_inc(hT_psum, 1)

                def down(n, j, turn):
                    e = expert(pe, n)
                    pe.wait_ge(act_ready, n + 1)
                    from_item(pe, out_ready, n, 2, n - 1)
                    for c in range(HC):
                        mm = pe.matmul(ps_out[:, j % 2, 0:D], actT[:, j % 2, c, :],
                                       w2[:, bass.ds(e, 1), c * D:(c + 1) * D].rearrange("p e n -> p (e n)"),
                                       start=(c == 0), stop=(c == HC - 1))
                    mm.then_inc(out_psum, 1)

                in_tiles(pe, [turn_rows, down, up, turn_hidden], [0, 3, 1, 2])

            @block.scalar
            def _(act):
                act.wait_ge(w_in, WEIGHTS)

                def gelu(n, j, turn):
                    e = expert(act, n)
                    act.wait_ge(hT_psum, n + 1)
                    for c in range(HC):
                        ins = act.activation(actT[:, j % 2, c, :], ps_hT[:, j % 2, c * P:(c + 1) * P], ACT.Gelu,
                                             bias=b1T[:, bass.ds(e * HC + c, 1)])
                    ins.then_inc(act_ready, 1)

                in_tiles(act, [gelu], [2])

            @block.vector
            def _(v):
                v.wait_ge(w_in, WEIGHTS)

                def copy_rowsT(n, j, turn):
                    v.wait_ge(rowsT_psum, n + 1)
                    v.tensor_copy(rowsT[:, j % 2, :, :], ps_t[:, j % 2, 0:D].rearrange("p (c n) -> p c n", c=C)).then_inc(rowsT_ready, 1)

                def copy_pre(n, j, turn):
                    v.wait_ge(up_psum, n + 1)
                    v.tensor_copy(pre[:, j % 2, :], ps_up[:, j % 2, :]).then_inc(pre_ready, 1)

                def add_bias(n, j, turn):
                    e = expert(v, n)
                    v.wait_ge(out_psum, n + 1)
                    from_item(v, stored[j], n, EX_RING, turn * 16)
                    v.tensor_tensor(outs[:, j, :], ps_out[:, j % 2, 0:D], flat(b2_b, e, slice(0, D)), ALU.add).then_inc(out_ready, 1)

                in_tiles(v, [copy_rowsT, add_bias, copy_pre], [0, 3, 1])


def finish(nc, s, out):
    with ExitStack() as ctx:
        def sb(name, shape, dt=F32):
            return ctx.enter_context(nc.sbuf_tensor(name, shape, dt))

        def sem(name):
            return nc.alloc_semaphore(name=name)

        rows = sb("k_rows", [P, 4, 2 * D])
        index = sb("k_index", [P, 4, 2], I32)
        part = sb("k_part", [P, 2, D])
        result = sb("k_result", [P, 4, D])
        gathered = [sem(f"k_gathered{j}") for j in range(4)]
        indexed = sem("k_indexed")
        halfway = sem("k_halfway")
        summed = sem("k_summed")
        stored = [sem(f"k_stored{j}") for j in range(4)]

        with nc.Block() as block:

            @block.gpsimd
            def _(g):
                def gather(t, j, turn):
                    count = TAIL if isinstance(t, int) and t == TILES - 1 else P
                    from_item(g, summed, t, 4, t - 3)
                    g.tensor_copy(index[:, j, :], s.slot[:, :, bass.ds(t, 1)].rearrange("p k t -> p (k t)")).then_inc(indexed, 1)
                    g.wait_ge(indexed, t + 1)
                    g.sem_inc(s.wait_seen, 1)
                    for k in range(2):
                        g.indirect_dma_start(rows[0:count, j, k * D:(k + 1) * D], None, s.expert_out,
                                             bass.IndirectOffsetOnAxis(ap=index[0:count, j, k:k + 1], axis=0)).then_inc(gathered[j], 16)

                in_step(g, [gather], [0], TILES - 1, 5, 4)
                gather(TILES - 1, (TILES - 1) % 4, (TILES - 1) // 4)

            @block.vector
            def _(v):
                def first(t, j, turn):
                    from_item(v, summed, t, 2, t - 1)
                    v.wait_ge(gathered[j], turn * 32 + 32)
                    v.scalar_tensor_tensor(part[:, j % 2, :], rows[:, j, 0:D], s.weight[:, 0, bass.ds(t, 1)],
                                           flat(s.sums, t, slice(0, D)), ALU.mult, ALU.add).then_inc(halfway, 1)

                def second(t, j, turn):
                    v.wait_ge(halfway, t + 1)
                    from_item(v, stored[j], t, 4, turn * 16)
                    v.scalar_tensor_tensor(result[:, j, :], rows[:, j, D:2 * D], s.weight[:, 1, bass.ds(t, 1)],
                                           part[:, j % 2, :], ALU.mult, ALU.add).then_inc(summed, 1)

                in_step(v, [second, first], [1, 0], TILES, 6, 4)

            @block.sync
            def _(sp):
                def store(t, j, turn):
                    count = TAIL if isinstance(t, int) and t == TILES - 1 else P
                    row = fixed(sp, t * P)
                    sp.wait_ge(summed, t + 1)
                    sp.dma_start(out[bass.ds(row, count), :], result[0:count, j, :]).then_inc(stored[j], 16)

                in_step(sp, [store], [0], TILES - 1, 5, 4)
                store(TILES - 1, (TILES - 1) % 4, (TILES - 1) // 4)
                for j in range(4):
                    sp.wait_ge(stored[j], 16 * len(range(j, TILES, 4)))


class Plan:
    pass


def program(nc, x, src, dst, W, att_src, att_dst, gat_bias, ln_gamma, ln_beta, w_norm1, w_qkv, w_out, b_out, w_norm2,
            gamma, beta, Wr, br, W1, b1, W2, b2, out):
    with ExitStack() as ctx:
        def sb(name, shape, dt=F32):
            return ctx.enter_context(nc.sbuf_tensor(name, shape, dt))
        s = allocate(nc, ctx)
        s.gat_stats = sb("gat_stats", [P, TILES, 6])
        s.mix_stats = sb("mix_stats", [P, TILES, 6])
        s.state_mean = sb("state_mean", [P, TILES])
        s.state_var = sb("state_var", [P, TILES])
        s.slot = sb("slot", [P, 2, TILES], I32)
        s.weight = sb("weight", [P, 2, TILES])
        s.expert_of = sb("expert_of", [1, EX_TILES], I32)
        s.gat_stat = ctx.enter_context(nc.semaphore("gat_stat"))
        s.wait_seen = ctx.enter_context(nc.semaphore("wait_seen"))
        s.mix_stat = ctx.enter_context(nc.semaphore("mix_stat"))
        with stage(nc):
            project(nc, s, x, src, dst, W, att_src, att_dst, w_norm1, w_qkv)
        with stage(nc), ExitStack() as plan_ctx:
            plan = Plan()
            plan.edge0 = plan_ctx.enter_context(nc.sbuf_tensor("edge0", [1, GROUPS], I32))
            plan.window = plan_ctx.enter_context(nc.sbuf_tensor("window", [1, GROUPS], I32))
            plan.target0 = plan_ctx.enter_context(nc.sbuf_tensor("target0", [P, GROUPS], F32))
            plan_groups(nc, s, plan)
            attend_edges(nc, s, plan)
        with stage(nc):
            combine(nc, s, x, gat_bias, w_out, b_out)
            join(nc, s, x, ln_gamma, ln_beta, w_norm2)
            route(nc, s, gamma, beta, Wr, br)
        with stage(nc):
            scatter_rows(nc, s)
            run_experts(nc, s, W1, b1, W2, b2)
            finish(nc, s, out)


_INS = ['x', 'src', 'dst', 'L0_gnn_W', 'L0_gnn_att_src', 'L0_gnn_att_dst', 'L0_gnn_bias', 'L0_gnn_ln_gamma', 'L0_gnn_ln_beta',
        'L0_mix_w_norm1', 'L0_mix_w_qkv', 'L0_mix_w_out', 'L0_mix_b_out', 'L0_mix_w_norm2',
        'L0_ffn_gamma', 'L0_ffn_beta', 'L0_ffn_Wr', 'L0_ffn_br', 'L0_ffn_W1', 'L0_ffn_b1', 'L0_ffn_W2', 'L0_ffn_b2']
_OUTS = [((N, D), 'float32')]


def kernel(**inputs):
    import numpy as _np
    import concourse.bacc as _bacc
    from concourse import mybir as _mybir
    from concourse.bass_utils import run_bass_kernel_spmd as _run

    nc = _bacc.Bacc("TRN2", target_bir_lowering=False, num_devices=1)
    arrays, args = {}, []
    for name in _INS:
        a = _np.ascontiguousarray(inputs[name])
        arrays[f"in_{name}_dram"] = a
        args.append(nc.dram_tensor(f"in_{name}_dram", a.shape, _mybir.dt.from_np(a.dtype), kind="ExternalInput").ap())
    for i, (shape, dtype) in enumerate(_OUTS):
        args.append(nc.dram_tensor(f"out_{i}_dram", shape, _mybir.dt.from_np(_np.dtype(dtype)), kind="ExternalOutput").ap())
    program(nc, *args)
    r = _run(nc, [arrays], core_ids=[0])
    return r.results[0]["out_0_dram"]
```

```python
from contextlib import ExitStack, contextmanager

import concourse.bass as bass
from concourse import mybir

P = 128
N = 12500
D = 256
E = 200000
TILES = (N + P - 1) // P
TAIL = N - (TILES - 1) * P
NP = TILES * P
GH = 4
GF = D // GH
MH = 8
MF = D // MH
C = D // P
ROW = D + GH
G = 3
SPAN = G * P
RING = 8
HEAD = 5
INVERSE_BITS = 11
INVERSE = -(-(1 << INVERSE_BITS) // G)
assert all(x * INVERSE >> INVERSE_BITS == x // G for x in range(E // P + 1 + G))
GROUPS = -(-E // SPAN) + TILES
GROUPS = HEAD + -(-(GROUPS - HEAD) // RING) * RING
EPART = 125
ECOL = E // EPART
CHUNKS = -(-E // P)
NO_NODE = 1 << 20
SPREAD = 50.0
FAR = 1e30
EXPERTS = 8
HID = 512
HC = HID // P
EX_RING = 4
EX_HEAD = 4
EX_TILES = (2 * N + EXPERTS * (P - 1)) // P
EX_TILES = EX_HEAD + -(-(EX_TILES - EX_HEAD) // EX_RING) * EX_RING
ZERO_TILES = 12

F32 = mybir.dt.float32
I32 = mybir.dt.int32
U32 = mybir.dt.uint32
ALU = mybir.AluOpType
ACT = mybir.ActivationFunctionType
AX = mybir.AxisListType
RMAX = bass.bass_isa.ReduceOp.max


class Store:
    pass


def allocate(nc, ctx):
    def sb(name, shape, dt=F32):
        return ctx.enter_context(nc.sbuf_tensor(name, shape, dt))

    s = Store()
    s.node_rows = nc.dram_tensor("node_rows", [NP, ROW], F32).ap()
    s.queries = nc.dram_tensor("queries", [NP, D], F32).ap()
    s.edges = nc.dram_tensor("edges", [E + SPAN, 2], I32).ap()
    s.sorted = nc.dram_tensor("sorted_edges", [P * CHUNKS, 2], I32).ap()
    s.mixed = nc.dram_tensor("mixed", [NP, D], F32).ap()
    s.ffn_in = nc.dram_tensor("ffn_in", [NP, D], F32).ap()
    s.expert_in = nc.dram_tensor("expert_in", [EX_TILES * P, D], F32).ap()
    s.expert_out = nc.dram_tensor("expert_out", [EX_TILES * P, D], F32).ap()
    s.big = sb("big", [P, TILES * ROW])
    s.x_tiles = s.big[:, 0:(TILES + 1) * D].rearrange("p (t d) -> p t d", d=D)
    s.sums = s.big[:, :].rearrange("p (t d) -> p t d", d=ROW)
    s.scores = sb("scores", [P, TILES, 2 * GH])
    s.shift = sb("shift", [P, TILES, 2 * GH])
    s.ln_scale = sb("ln_scale", [P, TILES + 1])
    s.ln_bias = sb("ln_bias", [P, TILES + 1])
    s.kv = sb("kv", [P, C, P + 4])
    s.ident = sb("ident", [P, P])
    s.row_iota = sb("row_iota", [P, P])
    s.valid = sb("valid", [P, TILES])
    s.first_edge = sb("first_edge", [P, 1])
    s.ones = sb("ones", [P, P])
    return s


@contextmanager
def stage(nc):
    before = nc.snapshot_sems()
    yield
    nc.clear_and_free_semaphores(nc.allocated_since(before))
    nc.all_engine_barrier()


def in_step(eng, steps, lag, count, head, ring):
    assert max(lag) <= head and (count - head) % ring == 0
    for n in range(head):
        for k, step in enumerate(steps):
            if n - lag[k] >= 0:
                step(n - lag[k], (n - lag[k]) % ring, (n - lag[k]) // ring)
    with eng.Fori(0, (count - head) // ring) as i:
        for m in range(ring):
            for k, step in enumerate(steps):
                off = head + m - lag[k]
                step(i * ring + off, off % ring, i + off // ring)
    for n in range(count, count + max(lag)):
        for k, step in enumerate(steps):
            if n - lag[k] < count:
                step(n - lag[k], (n - lag[k]) % ring, (n - lag[k]) // ring)


def from_item(eng, sem, n, first, value):
    if not isinstance(n, int) or n >= first:
        eng.wait_ge(sem, value)


def fixed(eng, value):
    return value if isinstance(value, int) else eng.snap(value)


def mean_and_variance(v, stats, mean, var, tmp, done):
    v.tensor_tensor(mean, stats[:, :, 1], stats[:, :, 4], ALU.add).then_inc(done, 1)
    v.tensor_tensor(tmp, stats[:, :, 1], stats[:, :, 4], ALU.subtract).then_inc(done, 1)
    v.tensor_tensor(var, stats[:, :, 2], stats[:, :, 5], ALU.add).then_inc(done, 1)
    v.wait_ge(done, 3)
    v.tensor_scalar(mean, mean, 0.5, None, ALU.mult).then_inc(done, 1)
    v.scalar_tensor_tensor(tmp, tmp, 0.25, tmp, ALU.mult, ALU.mult).then_inc(done, 1)
    v.wait_ge(done, 5)
    v.scalar_tensor_tensor(var, var, 1.0 / D, tmp, ALU.mult, ALU.add).then_inc(done, 1)
    v.wait_ge(done, 6)


def project(nc, s, x, src, dst, W, att_src, att_dst, w_norm1, w_qkv):
    with ExitStack() as ctx:
        def sb(name, shape, dt=F32):
            return ctx.enter_context(nc.sbuf_tensor(name, shape, dt))

        def psum(name, shape):
            return ctx.enter_context(nc.psum_tensor(name, shape, F32))

        def sem(name):
            return nc.alloc_semaphore(name=name)

        w_ext = sb("w_ext", [P, C, D + 2 * GH])
        wq = sb("wq", [P, C, 3 * D])
        att = sb("att", [P, 2, D])
        att_w = sb("att_w", [P, 4, D])
        wn = sb("wn", [P, C])
        stats = sb("stats", [P, TILES + 1, 6])
        mean = sb("mean", [P, TILES + 1])
        var = sb("var", [P, TILES + 1])
        tmp = sb("tmp", [P, TILES + 1])
        h_scale = sb("h_scale", [P, TILES + 1])
        r_scale = sb("r_scale", [P, TILES + 1])
        r_bias = sb("r_bias", [P, TILES + 1])
        r = sb("r", [P, 2, D])
        rT = sb("rT", [P, 2, C, P])
        k_exp = sb("k_exp", [P, 2, D])
        q_exp = sb("q_exp", [P, 2, D])
        keys = sb("keys", [P, 2, D])
        values = sb("values", [P, 2, D])
        q_out = sb("q_out", [P, 2, D])
        h_out = sb("h_out", [P, 2, ROW])
        edge_src = sb("edge_src", [P, ECOL], I32)
        edge_dst = sb("edge_dst", [P, ECOL], I32)
        edge_pair = sb("edge_pair", [P, ECOL, 2], I32)
        edge_pad = sb("edge_pad", [P, G, 2], I32)
        node_id = sb("node_id", [P, TILES])
        pos = sb("pos", [P, 1])
        cand = sb("cand", [P, 1])
        probe = sb("probe", [P, 1], I32)
        found = sb("found", [P, 1], I32)
        below = sb("below", [P, 1])
        inside = sb("inside", [P, 1])
        window_key = sb("window_key", [P, 1])

        ps_t = psum("ps_t", [P, 2, 512])
        ps_h = psum("ps_h", [P, 512])
        ps_kv = psum("ps_kv", [P, 2, 512])
        ps_q = psum("ps_q", [P, 2, 512])
        ps_acc = psum("ps_acc", [P, 512])
        acc = ps_acc[:, 0:C * (P + 1)].rearrange("p (c n) -> p c n", c=C)

        pad_set = sem("a_pad_set")
        x_in = [sem(f"a_x_in{j}") for j in range(7)]
        w_in = sem("a_w_in")
        w_ready = sem("a_w_ready")
        w_steps = sem("a_w_steps")
        consts = sem("a_consts")
        stats_done = sem("a_stats_done")
        agg_done = sem("a_agg_done")
        var_eps = sem("a_var_eps")
        var_sqrt = sem("a_var_sqrt")
        ms_eps = sem("a_ms_eps")
        ms_sqrt = sem("a_ms_sqrt")
        chain = sem("a_scales_chain")
        r_ready = sem("a_r_ready")
        rT_psum = sem("a_rT_psum")
        rT_ready = sem("a_rT_ready")
        kv_psum = sem("a_kv_psum")
        q_psum = sem("a_q_psum")
        h_psum = sem("a_h_psum")
        acc_done = sem("a_acc_done")
        h_free = sem("a_h_free")
        k_free = sem("a_k_free")
        v_ready = sem("a_v_ready")
        q_free = sem("a_q_free")
        k_min = sem("a_k_min")
        q_min = sem("a_q_min")
        k_expd = sem("a_k_expd")
        q_expd = sem("a_q_expd")
        k_ready = sem("a_k_ready")
        q_ready = sem("a_q_ready")
        h_ready = sem("a_h_ready")
        store_free = sem("a_store_free")
        h_stored = [sem(f"a_h_stored{u}") for u in range(2)]
        q_stored = [sem(f"a_q_stored{u}") for u in range(2)]
        kv_parts = sem("a_kv_parts")
        e_in = sem("a_e_in")
        pair_ready = sem("a_pair_ready")
        pair_stored = sem("a_pair_stored")
        pool_step = sem("a_pool_step")
        probed = sem("a_probed")

        with nc.Block() as block:

            @block.sync
            def _(sp):
                sp.dma_start(w_ext[:, :, 0:D], W.rearrange("(c p) n -> p c n", p=P)).then_inc(w_in, 16)
                sp.dma_start(wq[:, :, :], w_qkv.rearrange("(c p) n -> p c n", p=P)).then_inc(w_in, 16)
                sp.dma_start(att[:, 0, :], att_src.rearrange("h f -> (h f)").partition_broadcast(P)).then_inc(w_in, 16)
                sp.dma_start(att[:, 1, :], att_dst.rearrange("h f -> (h f)").partition_broadcast(P)).then_inc(w_in, 16)
                for c in range(C):
                    sp.dma_start(wn[:, c:c + 1], w_norm1[c * P:(c + 1) * P].rearrange("(p o) -> p o", o=1)).then_inc(w_in, 16)
                for j in range(7):
                    full = 14 if j < 6 else 13
                    sp.dma_start(s.x_tiles[:, 14 * j:14 * j + full, :],
                                 x[14 * j * P:(14 * j + full) * P, :].rearrange("(t p) d -> p t d", p=P)).then_inc(x_in[j], 16)
                sp.wait_ge(pad_set, 1)
                sp.dma_start(s.x_tiles[0:TAIL, TILES - 1, :], x[N - TAIL:N, :]).then_inc(x_in[6], 16)
                sp.sem_inc(store_free, 2)
                with sp.Fori(0, TILES - 1, 2) as t0:
                    for u in range(2):
                        t = t0 + u
                        sp.wait_ge(h_ready, 2 * t + 2)
                        sp.dma_start(s.node_rows[bass.ds(t * P, P), :], h_out[:, u, :]).then_inc(h_stored[u], 16)
                        sp.wait_ge(q_ready, t + 1)
                        sp.dma_start(s.queries[bass.ds(t * P, P), :], q_out[:, u, :]).then_inc(q_stored[u], 16)
                        sp.wait_ge(h_stored[u], 8 * t0 + 16)
                        sp.wait_ge(q_stored[u], 8 * t0 + 16)
                        sp.sem_inc(store_free, 1)

            @block.gpsimd
            def _(g):
                g.dma_start(edge_src[0:EPART, :], src.rearrange("(p c) -> p c", p=EPART)).then_inc(e_in, 16)
                g.dma_start(edge_dst[0:EPART, :], dst.rearrange("(p c) -> p c", p=EPART)).then_inc(e_in, 16)
                g.memset(s.ident[:, :], 0.0).then_inc(consts, 1)
                g.memset(s.ones[:, :], 1.0).then_inc(consts, 1)
                g.iota(s.row_iota[:, :], [[1, P]], base=0, channel_multiplier=0,
                       allow_small_or_imprecise_dtypes=True).then_inc(consts, 1)
                g.iota(node_id[:, :], [[P, TILES]], base=0, channel_multiplier=1,
                       allow_small_or_imprecise_dtypes=True).then_inc(consts, 1)
                g.iota(window_key[:, :], [[0, 1]], base=0, channel_multiplier=P,
                       allow_small_or_imprecise_dtypes=True).then_inc(consts, 1)
                g.memset(pos[:, :], 0.0).then_inc(consts, 1)
                g.memset(edge_pad[:, :, 0:1], 0).then_inc(consts, 1)
                g.memset(edge_pad[:, :, 1:2].bitcast(F32), float(NO_NODE)).then_inc(consts, 1)
                g.wait_ge(consts, 8)
                g.affine_select(out=s.ident[:, :], in_=s.ident[:, :], compare_op=ALU.not_equal, fill=1.0,
                                base=0, pattern=[[-1, P]], channel_multiplier=1).then_inc(consts, 1)
                g.tensor_scalar(s.valid[:, :], node_id[:, :], float(N), None, ALU.is_lt).then_inc(consts, 1)
                g.wait_ge(e_in, 32)
                g.tensor_copy(edge_pair[0:EPART, :, 0], edge_src[0:EPART, :]).then_inc(pair_ready, 1)
                g.tensor_copy(edge_pair[0:EPART, :, 1:2].bitcast(F32), edge_dst[0:EPART, :]).then_inc(pair_ready, 1)
                g.wait_ge(pair_ready, 2)
                g.dma_start(s.edges[0:E, :].rearrange("(p c) k -> p c k", p=EPART), edge_pair[0:EPART, :, :]).then_inc(pair_stored, 16)
                g.dma_start(s.edges[E:E + SPAN, :].rearrange("(p c) k -> p c k", p=P), edge_pad[:, :, :]).then_inc(pair_stored, 16)
                dst_rows = dst.rearrange("(e o) -> e o", o=1)
                step = 1 << (E.bit_length() - 1)
                n = 0
                k = 0
                while step:
                    g.tensor_scalar(cand[:, :], pos[:, :], float(step), None, ALU.add).then_inc(pool_step, 1)
                    g.wait_ge(pool_step, n + 1)
                    g.tensor_scalar(probe[:, :], cand[:, :], float(E), -1.0, ALU.min, ALU.add).then_inc(pool_step, 1)
                    g.tensor_scalar(inside[:, :], cand[:, :], float(E), float(step), ALU.is_le, ALU.mult).then_inc(pool_step, 1)
                    g.wait_ge(pool_step, n + 3)
                    g.indirect_dma_start(found[:, :], None, dst_rows,
                                         bass.IndirectOffsetOnAxis(ap=probe[:, :], axis=0)).then_inc(probed, 16)
                    g.wait_ge(probed, 16 * (k + 1))
                    g.tensor_scalar(below[:, :], found[:, :], window_key[:, :], inside[:, :], ALU.is_lt, ALU.mult).then_inc(pool_step, 1)
                    g.wait_ge(pool_step, n + 4)
                    g.tensor_tensor(pos[:, :], pos[:, :], below[:, :], ALU.add).then_inc(pool_step, 1)
                    g.wait_ge(pool_step, n + 5)
                    n += 5
                    k += 1
                    step >>= 1
                g.tensor_copy(s.first_edge[:, :], pos[:, :]).then_inc(pool_step, 1)
                g.wait_ge(pair_stored, 32)

            @block.vector
            def _(v):
                v.memset(s.x_tiles[:, TILES - 1:TILES + 1, :], 0.0).then_inc(pad_set, 1)
                v.wait_ge(w_in, 6 * 16)
                for c in range(C):
                    for a in range(2):
                        v.tensor_tensor(att_w[:, 2 * c + a, :], w_ext[:, c, 0:D], att[:, a, :], ALU.mult).then_inc(w_steps, 1)
                v.wait_ge(w_steps, 4)
                for c in range(C):
                    for a in range(2):
                        v.tensor_reduce(w_ext[:, c, D + GH * a:D + GH * (a + 1)],
                                        att_w[:, 2 * c + a, :].rearrange("p (h f) -> p h f", h=GH), AX.X, ALU.add).then_inc(w_ready, 1)
                for c in range(C):
                    v.tensor_scalar(wq[:, c, :], wq[:, c, :], wn[:, c:c + 1], None, ALU.mult).then_inc(w_ready, 1)
                for j in range(7):
                    v.wait_ge(x_in[j], 16 if j < 6 else 32)
                    with v.Fori(14 * j, 14 * (j + 1) + (j == 6)) as t:
                        v.bn_stats(stats[:, bass.ds(t, 1), :].rearrange("p t k -> p (t k)"),
                                   s.x_tiles[:, bass.ds(t, 1), :].rearrange("p t d -> p (t d)")).then_inc(stats_done, 1)
                v.wait_ge(stats_done, TILES + 1)
                mean_and_variance(v, stats, mean[:, :], var[:, :], tmp[:, :], agg_done)
                v.tensor_scalar(tmp[:, :], var[:, :], 1e-5, None, ALU.add).then_inc(var_eps, 1)
                v.wait_ge(var_sqrt, 1)
                v.reciprocal(s.ln_scale[:, :], tmp[:, :]).then_inc(chain, 1)
                v.wait_ge(chain, 1)
                v.tensor_tensor(tmp[:, :], s.ln_scale[:, :], s.ln_scale[:, :], ALU.mult).then_inc(chain, 1)
                v.scalar_tensor_tensor(s.ln_bias[:, :], mean[:, :], -1.0, s.ln_scale[:, :], ALU.mult, ALU.mult).then_inc(chain, 1)
                v.wait_ge(chain, 3)
                v.tensor_tensor(tmp[:, :], tmp[:, :], var[:, :], ALU.mult).then_inc(chain, 1)
                v.wait_ge(chain, 4)
                v.tensor_scalar(tmp[:, :], tmp[:, :], 1e-6, None, ALU.add).then_inc(ms_eps, 1)
                v.wait_ge(ms_sqrt, 1)
                v.reciprocal(tmp[:, :], h_scale[:, :]).then_inc(chain, 1)
                v.wait_ge(chain, 5)
                v.tensor_tensor(r_scale[:, :], s.ln_scale[:, :], tmp[:, :], ALU.mult).then_inc(chain, 1)
                v.tensor_tensor(r_bias[:, :], s.ln_bias[:, :], tmp[:, :], ALU.mult).then_inc(chain, 1)
                v.wait_ge(chain, 7)

                def normalise(t, u):
                    v.tensor_scalar(r[:, u, :], s.x_tiles[:, bass.ds(t, 1), :].rearrange("p t d -> p (t d)"),
                                    r_scale[:, bass.ds(t, 1)], r_bias[:, bass.ds(t, 1)], ALU.mult, ALU.add).then_inc(r_ready, 1)

                v.sem_inc(h_free, 1)
                v.sem_inc(k_free, 2)
                v.sem_inc(q_free, 2)
                normalise(0, 0)
                with v.Fori(0, TILES - 1, 2) as t0:
                    for u in range(2):
                        t = t0 + u
                        normalise(t + 1, 1 - u)
                        v.wait_ge(kv_psum, t + 1)
                        v.tensor_scalar(k_exp[:, u, :], ps_kv[:, u, 0:D], 0.0, None, ALU.min).then_inc(k_min, 1)
                        v.wait_ge(q_psum, t + 1)
                        v.tensor_scalar(q_exp[:, u, :], ps_q[:, u, 0:D], 0.0, None, ALU.min).then_inc(q_min, 1)
                        v.wait_ge(k_expd, t + 1)
                        v.scalar_tensor_tensor(keys[:, u, :], ps_kv[:, u, 0:D], 0.0, k_exp[:, u, :],
                                               ALU.max, ALU.add).then_inc(k_ready, 1)
                        v.wait_ge(k_ready, t + 1)
                        v.sem_inc(k_free, 1)
                        v.wait_ge(h_psum, t + 1)
                        v.wait_ge(store_free, t + 1)
                        v.tensor_scalar(h_out[:, u, :], ps_h[:, 0:ROW], h_scale[:, bass.ds(t, 1)], None, ALU.mult).then_inc(h_ready, 1)
                        v.tensor_scalar(s.scores[:, bass.ds(t, 1), :].rearrange("p t k -> p (t k)"), ps_h[:, D:D + 2 * GH],
                                        h_scale[:, bass.ds(t, 1)], None, ALU.mult).then_inc(h_ready, 1)
                        v.wait_ge(h_ready, 2 * t + 2)
                        v.sem_inc(h_free, 1)
                        v.wait_ge(q_expd, t + 1)
                        v.scalar_tensor_tensor(q_out[:, u, :], ps_q[:, u, 0:D], 0.0, q_exp[:, u, :],
                                               ALU.max, ALU.add).then_inc(q_ready, 1)
                        v.wait_ge(q_ready, t + 1)
                        v.sem_inc(q_free, 1)
                v.wait_ge(acc_done, 1)
                v.memset(s.kv[:, :, :], 0.0).then_inc(kv_parts, 1)
                v.wait_ge(kv_parts, 1)
                for j in range(4):
                    a, b = MF * j, MF * (j + 1)
                    v.tensor_copy(s.kv[a:b, :, a:b], acc[a:b, :, a:b]).then_inc(kv_parts, 1)
                    v.tensor_copy(s.kv[a:b, :, P + j:P + j + 1], acc[a:b, :, P:P + 1]).then_inc(kv_parts, 1)

            @block.scalar
            def _(act):
                act.wait_ge(var_eps, 1)
                act.activation(tmp[:, :], tmp[:, :], ACT.Sqrt).then_inc(var_sqrt, 1)
                act.wait_ge(ms_eps, 1)
                act.activation(h_scale[:, :], tmp[:, :], ACT.Sqrt).then_inc(ms_sqrt, 1)

                def copy_rT(t, u):
                    act.wait_ge(rT_psum, t + 1)
                    act.activation(rT[:, u, :, :], ps_t[:, u, 0:D].rearrange("p (c n) -> p c n", c=C), ACT.Copy).then_inc(rT_ready, 1)

                copy_rT(0, 0)
                with act.Fori(0, TILES - 1, 2) as t0:
                    for u in range(2):
                        t = t0 + u
                        act.wait_ge(k_min, t + 1)
                        act.activation(values[:, u, :], ps_kv[:, u, D:2 * D], ACT.Copy).then_inc(v_ready, 1)
                        act.activation(k_exp[:, u, :], k_exp[:, u, :], ACT.Exp).then_inc(k_expd, 1)
                        act.wait_ge(q_min, t + 1)
                        act.activation(q_exp[:, u, :], q_exp[:, u, :], ACT.Exp).then_inc(q_expd, 1)
                        copy_rT(t + 1, 1 - u)

            @block.tensor
            def _(pe):
                pe.wait_ge(consts, 10)
                pe.wait_ge(w_ready, 6)

                def transpose_r(t, u):
                    pe.wait_ge(r_ready, t + 1)
                    for c in range(C):
                        mm = pe.transpose(ps_t[:, u, c * P:(c + 1) * P], r[:, u, c * P:(c + 1) * P], s.ident[:, :])
                    mm.then_inc(rT_psum, 1)

                pe.wait_ge(pad_set, 1)
                nothing = s.x_tiles[:, TILES, :]
                pe.matmul(ps_acc[:, 0:D], s.ident[:, :], nothing, start=True, stop=False, skip_group_check=True)
                pe.matmul(ps_acc[:, D:C * (P + 1)], s.ident[:, :], nothing[:, 0:C], start=False, stop=False,
                          skip_group_check=True)
                transpose_r(0, 0)
                with pe.Fori(0, TILES - 1, 2) as t0:
                    for u in range(2):
                        t = t0 + u
                        pe.wait_ge(rT_ready, t + 1)
                        pe.wait_ge(k_free, t + 1)
                        for c in range(C):
                            mm = pe.matmul(ps_kv[:, u, :], rT[:, u, c, :], wq[:, c, D:3 * D], start=(c == 0), stop=(c == C - 1))
                        mm.then_inc(kv_psum, 1)
                        pe.wait_ge(q_free, t + 1)
                        for m in range(C):
                            for c in range(C):
                                mm = pe.matmul(ps_q[:, u, m * P:(m + 1) * P], wq[:, c, m * P:(m + 1) * P], rT[:, u, c, :],
                                               start=(c == 0), stop=(c == C - 1))
                        mm.then_inc(q_psum, 1)
                        pe.wait_ge(h_free, t + 1)
                        for c in range(C):
                            mm = pe.matmul(ps_h[:, 0:D + 2 * GH], rT[:, u, c, :], w_ext[:, c, :], start=(c == 0), stop=(c == C - 1))
                        mm.then_inc(h_psum, 1)
                        transpose_r(t + 1, 1 - u)
                        pe.wait_ge(k_ready, t + 1)
                        pe.wait_ge(v_ready, t + 1)
                        for m in range(C):
                            pe.matmul(acc[:, m, 0:P], keys[:, u, m * P:(m + 1) * P], values[:, u, m * P:(m + 1) * P],
                                      start=False, stop=False, skip_group_check=True)
                            pe.matmul(acc[:, m, P:P + 1], keys[:, u, m * P:(m + 1) * P], s.valid[:, bass.ds(t, 1)],
                                      start=False, stop=False, skip_group_check=True)
                pe.matmul(acc[:, 0, P:P + 1], s.ident[:, :], s.x_tiles[:, TILES, 0:1],
                          start=False, stop=True, skip_group_check=True).then_inc(acc_done, 1)


def check_inputs(nc, s, dst):
    with ExitStack() as ctx:
        def sb(name, shape, dt=F32):
            return ctx.enter_context(nc.sbuf_tensor(name, shape, dt))

        here = sb("i_here", [P, ECOL], I32)
        behind = sb("i_behind", [P, ECOL], I32)
        signs = sb("i_signs", [P, 1 + 2 * GH])
        signs_all = sb("i_signs_all", [P, 1 + 2 * GH])
        spread = sb("i_spread", [P, GH])
        widest = sb("i_widest", [P, 1])
        dst_in = nc.alloc_semaphore(name="i_dst_in")
        step = nc.alloc_semaphore(name="i_step")
        signs_ready = nc.alloc_semaphore(name="i_signs_ready")
        reduced = nc.alloc_semaphore(name="i_reduced")

        with nc.Block() as block:

            @block.sync
            def _(sp):
                rows = EPART - 1
                sp.dma_start(here[0:EPART, :], dst.rearrange("(p c) -> p c", p=EPART)).then_inc(dst_in, 16)
                sp.dma_start(behind[0:rows, :], dst[1:1 + rows * ECOL].rearrange("(p c) -> p c", p=rows)).then_inc(dst_in, 16)
                sp.dma_start(behind[rows:EPART, 0:ECOL - 1], dst[1 + rows * ECOL:E].rearrange("(p c) -> p c", p=1)).then_inc(dst_in, 16)
                sp.dma_start(behind[rows:EPART, ECOL - 1:ECOL], dst[E - 1:E].rearrange("(p c) -> p c", p=1)).then_inc(dst_in, 16)

            @block.gpsimd
            def _(g):
                g.wait_ge(signs_ready, 4)
                g.partition_all_reduce(signs_all[:, :], signs[:, :], P, RMAX).then_inc(reduced, 1)

            @block.vector
            def _(v):
                v.memset(signs[:, 0:1], 0.0).then_inc(signs_ready, 1)
                scores = s.scores[:, :, 0:GH].rearrange("p t h -> p h t")
                v.tensor_reduce(signs[:, 1:1 + GH], scores, AX.X, ALU.max).then_inc(signs_ready, 1)
                v.tensor_reduce(spread[:, :], scores, AX.X, ALU.min).then_inc(step, 1)
                v.wait_ge(step, 1)
                v.tensor_scalar(signs[:, 1 + GH:], spread[:, :], -1.0, None, ALU.mult).then_inc(signs_ready, 1)
                v.wait_ge(dst_in, 64)
                v.tensor_tensor(here[0:EPART, :], here[0:EPART, :], behind[0:EPART, :], ALU.subtract).then_inc(step, 1)
                v.wait_ge(step, 2)
                v.wait_ge(signs_ready, 1)
                v.tensor_reduce(signs[0:EPART, 0:1], here[0:EPART, :], AX.X, ALU.max).then_inc(signs_ready, 1)
                v.wait_ge(reduced, 1)
                v.tensor_tensor(spread[:, :], signs_all[:, 1:1 + GH], signs_all[:, 1 + GH:], ALU.add).then_inc(step, 1)
                v.wait_ge(step, 3)
                v.tensor_reduce(widest[:, :], spread[:, :], AX.X, ALU.max).then_inc(step, 1)
                v.wait_ge(step, 4)
                v.tensor_scalar(s.fault[:, 0:1], signs_all[:, 0:1], 0.0, None, ALU.is_gt).then_inc(step, 1)
                v.tensor_scalar(s.fault[:, 1:2], widest[:, :], SPREAD, None, ALU.is_gt).then_inc(step, 1)


def faulty(eng, s, k):
    return eng.value_load(s.fault[0:1, k:k + 1], min_val=0, max_val=1)


def sort_by_window(nc, s):
    with ExitStack() as ctx:
        def sb(name, shape, dt=F32):
            return ctx.enter_context(nc.sbuf_tensor(name, shape, dt))

        def sem(name):
            return nc.alloc_semaphore(name=name)

        every = sb("j_every", [P, CHUNKS, 2], I32)
        window_i = sb("j_window_i", [P, CHUNKS], I32)
        window = sb("j_window", [P, CHUNKS])
        before = sb("j_before", [P, P])
        hot = sb("j_hot", [P, P])
        total = sb("j_total", [P, P])
        zeros = sb("j_zeros", [P, P])
        start = sb("j_start", [P, P + 1])
        place = sb("j_place", [P, P])
        own = sb("j_own", [P, P])
        pos = sb("j_pos", [P, 1])
        pos_i = sb("j_pos_i", [P, 1], I32)
        pair = sb("j_pair", [P, 2], I32)
        ps_rank = ctx.enter_context(nc.psum_tensor("j_ps_rank", [P, 512], F32))
        ps_count = ctx.enter_context(nc.psum_tensor("j_ps_count", [P, 512], F32))
        edges_in = sem("j_edges_in")
        masked = sem("j_masked")
        step = sem("j_step")
        hot_ready = sem("j_hot_ready")
        counted = sem("j_counted")
        placed = sem("j_placed")
        scattered = [sem(f"j_scattered{u}") for u in range(2)]
        placed_parts = sem("j_placed_parts")
        copied = sem("j_copied")

        with nc.Block() as block:

            @block.sync
            def _(sp):
                with sp.If(faulty(sp, s, 0) != 0):
                    sp.dma_start(every[:, :, :], s.edges[0:P * CHUNKS, :].rearrange("(p c) k -> p c k", p=P)).then_inc(edges_in, 16)

            @block.gpsimd
            def _(g):
                with g.If(faulty(g, s, 0) != 0):
                    g.memset(before[:, :], 1.0).then_inc(masked, 1)
                    g.wait_ge(masked, 1)
                    g.affine_select(out=before[:, :], in_=before[:, :], compare_op=ALU.is_gt, fill=0.0,
                                    base=0, pattern=[[1, P]], channel_multiplier=-1).then_inc(masked, 1)

                    def scatter(c, u):
                        g.wait_ge(placed, c + 1)
                        g.sem_inc(s.wait_seen, 1)
                        g.indirect_dma_start(s.sorted, bass.IndirectOffsetOnAxis(ap=pos_i[:, :], axis=0),
                                             pair[:, :], None).then_inc(scattered[u], 16)

                    with g.Fori(0, CHUNKS // 2) as i:
                        for u in range(2):
                            scatter(i * 2 + u, u)
                    for c in range(CHUNKS // 2 * 2, CHUNKS):
                        scatter(c, c % 2)
                    for u in range(2):
                        g.wait_ge(scattered[u], 16 * len(range(u, CHUNKS, 2)))
                    g.dma_start(s.edges[0:P * CHUNKS, :], s.sorted[:, :]).then_inc(copied, 16)
                    g.wait_ge(copied, 16)

            @block.tensor
            def _(pe):
                with pe.If(faulty(pe, s, 0) != 0):
                    with pe.Fori(0, CHUNKS) as c:
                        pe.wait_ge(hot_ready, c + 1)
                        pe.matmul(ps_count[:, 0:P], s.ones[:, :], hot[:, :], start=True, stop=True).then_inc(counted, 1)
                    pe.wait_ge(masked, 2)
                    with pe.Fori(0, CHUNKS) as c:
                        pe.wait_ge(hot_ready, c + (CHUNKS + 1))
                        pe.matmul(ps_count[:, 0:P], s.ones[:, :], hot[:, :], start=True, stop=True)
                        pe.matmul(ps_rank[:, 0:P], before[:, :], hot[:, :], start=True, stop=True).then_inc(counted, 1)

            @block.vector
            def _(v):
                with v.If(faulty(v, s, 0) != 0):
                    v.memset(zeros[:, :], 0.0).then_inc(step, 1)
                    v.memset(total[:, :], 0.0).then_inc(step, 1)
                    v.wait_ge(edges_in, 16)
                    v.tensor_copy(window_i[:, :], every[:, :, 1].bitcast(F32)).then_inc(step, 1)
                    v.wait_ge(step, 3)
                    v.tensor_scalar(window_i[:, :], window_i[:, :], P.bit_length() - 1, None, ALU.arith_shift_right).then_inc(step, 1)
                    v.wait_ge(step, 4)
                    v.tensor_scalar(window[:, :], window_i[:, :], float(P - 1), None, ALU.min).then_inc(step, 1)
                    v.wait_ge(step, 5)

                    def one_hot(c):
                        v.tensor_scalar(hot[:, :], s.row_iota[:, :], window[:, bass.ds(c, 1)], None, ALU.is_equal).then_inc(hot_ready, 1)

                    with v.Fori(0, CHUNKS) as c:
                        one_hot(c)
                        v.wait_ge(counted, c + 1)
                        v.tensor_tensor(total[:, :], total[:, :], ps_count[:, 0:P], ALU.add).then_inc(step, 1)
                        v.wait_ge(step, c + 6)
                    done = 5 + CHUNKS
                    v.tensor_tensor_scan(start[:, 1:P + 1], total[:, :], zeros[:, :], 0.0, ALU.add, ALU.add).then_inc(step, 1)
                    v.memset(start[:, 0:1], 0.0).then_inc(step, 1)
                    v.wait_ge(step, done + 2)
                    v.tensor_tensor(own[:, :], start[:, 0:P], s.ident[:, :], ALU.mult).then_inc(step, 1)
                    v.wait_ge(step, done + 3)
                    v.tensor_reduce(s.first_edge[:, :], own[:, :], AX.X, ALU.add).then_inc(step, 1)
                    done += 4
                    v.wait_ge(step, done)

                    def place_chunk(c, u, turn, n):
                        one_hot(c)
                        from_item(v, scattered[1 - u], c, 1, turn * 16 + 16 * u)
                        v.tensor_copy(pair[:, :], every[:, bass.ds(c, 1), :].rearrange("p c k -> p (c k)")).then_inc(placed_parts, 1)
                        v.wait_ge(counted, c + (CHUNKS + 1))
                        v.tensor_tensor(place[:, :], start[:, 0:P], ps_rank[:, 0:P], ALU.add).then_inc(step, 1)
                        v.wait_ge(step, n + 1)
                        v.tensor_tensor(own[:, :], place[:, :], hot[:, :], ALU.mult).then_inc(step, 1)
                        v.tensor_tensor(start[:, 0:P], start[:, 0:P], ps_count[:, 0:P], ALU.add).then_inc(step, 1)
                        v.wait_ge(step, n + 3)
                        v.tensor_reduce(pos[:, :], own[:, :], AX.X, ALU.add).then_inc(step, 1)
                        v.wait_ge(step, n + 4)
                        v.wait_ge(placed_parts, c + 1)
                        v.tensor_copy(pos_i[:, :], pos[:, :]).then_inc(placed, 1)

                    for c in range(2):
                        place_chunk(c, c, 0, done + 4 * c)
                    with v.Fori(1, CHUNKS // 2) as i:
                        for u in range(2):
                            place_chunk(i * 2 + u, u, i, i * 8 + (done + 4 * u))
                    for c in range(CHUNKS // 2 * 2, CHUNKS):
                        place_chunk(c, c % 2, c // 2, done + 4 * c)


def shift_by_target(nc, s, plan):
    with ExitStack() as ctx:
        def sb(name, shape, dt=F32):
            return ctx.enter_context(nc.sbuf_tensor(name, shape, dt))

        def sem(name):
            return nc.alloc_semaphore(name=name)

        pairs = sb("l_pairs", [P, G, 2], I32)
        rows = sb("l_rows", [P, G, ROW])
        rel = sb("l_rel", [P, G])
        hot = sb("l_hot", [P, G, P])
        wide = sb("l_wide", [P, G, GH, P])
        away = sb("l_away", [P, G, P])
        reach = sb("l_reach", [P, G, GH, P])
        best = sb("l_best", [P, GH, G])
        best_of = sb("l_best_of", [P, GH])
        peaks = sb("l_peaks", [P, TILES, GH])
        ps_hot = ctx.enter_context(nc.psum_tensor("l_ps_hot", [P, 512], F32))
        ps_wide = ctx.enter_context(nc.psum_tensor("l_ps_wide", [P, G, 512], F32))
        pairs_in = sem("l_pairs_in")
        rows_in = sem("l_rows_in")
        step = sem("l_step")
        masks_ready = sem("l_masks_ready")
        turned = sem("l_turned")
        folded = sem("l_folded")
        STEPS = 3 + 2 * G

        with nc.Block() as block:

            @block.sync
            def _(sp):
                with sp.If(faulty(sp, s, 1) != 0):
                    with sp.Fori(0, GROUPS) as n:
                        first = sp.value_load(plan.edge0[0:1, bass.ds(n, 1)], min_val=0, max_val=E)
                        sp.wait_ge(folded, n + 1)
                        sp.dma_start(pairs[:, :, :], s.edges[bass.ds(first, SPAN), :].rearrange("(p g) k -> p g k", p=P))\
                          .then_inc(pairs_in, 16)

            @block.gpsimd
            def _(g):
                with g.If(faulty(g, s, 1) != 0):
                    with g.Fori(0, GROUPS) as n:
                        g.wait_ge(pairs_in, n * 16 + 16)
                        g.sem_inc(s.wait_seen, 1)
                        for k in range(G):
                            g.indirect_dma_start(rows[:, k, :], None, s.node_rows,
                                                 bass.IndirectOffsetOnAxis(ap=pairs[:, k, 0:1], axis=0)).then_inc(rows_in, 16)

            @block.tensor
            def _(pe):
                with pe.If(faulty(pe, s, 1) != 0):
                    with pe.Fori(0, GROUPS) as n:
                        pe.wait_ge(masks_ready, n * 2 + 2)
                        for k in range(G):
                            pe.transpose(ps_hot[:, k * P:(k + 1) * P], hot[:, k, :], s.ident[:, :])
                        for k in range(G):
                            for h in range(GH):
                                mm = pe.matmul(ps_wide[:, k, h * P:(h + 1) * P], wide[:, k, h, :], s.ident[:, :], start=True, stop=True)
                        mm.then_inc(turned, 1)

            @block.vector
            def _(v):
                with v.If(faulty(v, s, 1) != 0):
                    v.tensor_copy(peaks[:, :, :], s.scores[:, :, 0:GH]).then_inc(folded, 1)
                    with v.Fori(0, GROUPS) as n:
                        w = v.value_load(plan.window[0:1, bass.ds(n, 1)], min_val=0, max_val=TILES - 1)
                        m = n * STEPS
                        v.wait_ge(pairs_in, n * 16 + 16)
                        v.wait_ge(folded, n + 1)
                        v.tensor_scalar(rel[:, :], pairs[:, :, 1].bitcast(F32), plan.target0[:, bass.ds(n, 1)], None,
                                        ALU.subtract).then_inc(step, 1)
                        v.wait_ge(step, m + 1)
                        v.tensor_tensor(hot[:, :, :], s.row_iota[:, :].unsqueeze(1).to_broadcast([P, G, P]),
                                        rel[:, :].unsqueeze(2).to_broadcast([P, G, P]), ALU.is_equal).then_inc(masks_ready, 1)
                        v.wait_ge(rows_in, n * (16 * G) + 16 * G)
                        v.tensor_copy(wide[:, :, :, :],
                                      rows[:, :, D:ROW].unsqueeze(3).to_broadcast([P, G, GH, P])).then_inc(masks_ready, 1)
                        v.wait_ge(turned, n + 1)
                        v.tensor_scalar(away[:, :, :], ps_hot[:, 0:G * P].rearrange("p (g n) -> p g n", g=G), -1.0, FAR,
                                        ALU.add, ALU.mult).then_inc(step, 1)
                        v.wait_ge(step, m + 2)
                        for k in range(G):
                            v.tensor_tensor(reach[:, k, :, :], ps_wide[:, k, :].rearrange("p (h n) -> p h n", h=GH),
                                            away[:, k, :].unsqueeze(1).to_broadcast([P, GH, P]), ALU.add).then_inc(step, 1)
                        v.wait_ge(step, m + (2 + G))
                        for k in range(G):
                            v.tensor_reduce(best[:, :, k:k + 1], reach[:, k, :, :], AX.X, ALU.max).then_inc(step, 1)
                        v.wait_ge(step, m + (2 + 2 * G))
                        v.tensor_reduce(best_of[:, :], best[:, :, :], AX.X, ALU.max).then_inc(step, 1)
                        v.wait_ge(step, m + (3 + 2 * G))
                        mine = peaks[:, bass.ds(w, 1), :].rearrange("p t h -> p (t h)")
                        v.tensor_tensor(mine, mine, best_of[:, :], ALU.max).then_inc(folded, 1)
                    v.wait_ge(folded, GROUPS + 1)
                    v.tensor_tensor(peaks[:, :, :], peaks[:, :, :], s.scores[:, :, GH:2 * GH], ALU.add).then_inc(step, 1)
                    v.wait_ge(step, GROUPS * STEPS + 1)
                    v.scalar_tensor_tensor(s.shift[:, :, GH:2 * GH], peaks[:, :, :], 0.2, peaks[:, :, :],
                                           ALU.mult, ALU.max).then_inc(step, 1)


def plan_groups(nc, s, plan):
    with ExitStack() as ctx:
        def sb(name, shape, dt=F32):
            return ctx.enter_context(nc.sbuf_tensor(name, shape, dt))

        def sem(name):
            return nc.alloc_semaphore(name=name)

        bounds = sb("bounds", [1, P])
        length = sb("length", [1, P])
        length_i = sb("length_i", [1, P], I32)
        ends = sb("ends", [1, P])
        ahead = sb("ahead", [1, P])
        zeros = sb("zeros", [1, P])
        columns = sb("columns", [P, 4])
        group_id = sb("group_id", [P, GROUPS])
        after = sb("after", [P, GROUPS])
        owner = sb("owner", [P, GROUPS])
        from_window = sb("from_window", [1, GROUPS])
        window_f = sb("window_f", [1, GROUPS])
        peak = sb("peak", [P, GH])
        peak_all = sb("peak_all", [P, GH])
        sloped = sb("sloped", [P, TILES, GH])
        ps = [ctx.enter_context(nc.psum_tensor(f"plan_ps{j}", [P, 512], F32)) for j in range(4)]

        iotas = sem("b_iotas")
        step = sem("b_step")
        turned = sem("b_turned")
        columned = sem("b_columned")
        masks = sem("b_masks")
        counted = sem("b_counted")
        evacuated = sem("b_evacuated")
        peaked = sem("b_peaked")
        reduced = sem("b_reduced")
        shifted = sem("b_shifted")
        divided = sem("b_divided")
        CH = 448
        chunks = [(a, min(a + CH, GROUPS)) for a in range(0, GROUPS, CH)]

        with nc.Block() as block:

            @block.gpsimd
            def _(g):
                g.iota(group_id[:, :], [[1, GROUPS]], base=0, channel_multiplier=0,
                       allow_small_or_imprecise_dtypes=True).then_inc(iotas, 1)
                g.wait_ge(peaked, 1)
                g.partition_all_reduce(peak_all[:, :], peak[:, :], P, RMAX).then_inc(reduced, 1)

            @block.tensor
            def _(pe):
                pe.transpose(ps[0][0:1, 0:P], s.first_edge[:, :], s.ident[:, :]).then_inc(turned, 1)
                pe.wait_ge(step, 8)
                for j, row in enumerate((bounds, ahead, ends)):
                    mm = pe.matmul(ps[1][:, j:j + 1], row[0:1, :], s.ones[0:1, 0:1], start=True, stop=True)
                mm.then_inc(columned, 1)
                for k, (a, b) in enumerate(chunks):
                    pe.wait_ge(masks, 2)
                    if k >= 1:
                        pe.wait_ge(evacuated, 3 * k)
                    pe.matmul(ps[2][:, 0:b - a], s.ones[0:TILES, :], after[0:TILES, a:b], start=True, stop=True)
                    pe.matmul(ps[3][0:1, 0:b - a], columns[0:TILES, 3:4], owner[0:TILES, a:b], start=True, stop=True).then_inc(counted, 1)

            @block.vector
            def _(v):
                v.memset(zeros[:, :], 0.0).then_inc(step, 1)
                v.memset(bounds[:, :], 0.0).then_inc(step, 1)
                v.memset(ahead[:, :], 0.0).then_inc(step, 1)
                v.wait_ge(turned, 1)
                v.wait_ge(step, 3)
                v.tensor_copy(bounds[0:1, :], ps[0][0:1, 0:P]).then_inc(step, 1)
                v.wait_ge(step, 4)
                v.tensor_tensor(length[0:1, 0:P - 1], bounds[0:1, 1:P], bounds[0:1, 0:P - 1], ALU.subtract).then_inc(step, 1)
                v.wait_ge(step, 5)
                v.tensor_scalar(length_i[0:1, 0:P - 1], length[0:1, 0:P - 1], float(P - 1), None, ALU.add).then_inc(step, 1)
                v.wait_ge(step, 6)
                v.tensor_scalar(length_i[0:1, 0:P - 1], length_i[0:1, 0:P - 1], P.bit_length() - 1, None,
                                ALU.arith_shift_right).then_inc(step, 1)
                v.memset(ends[:, :], 0.0).then_inc(shifted, 1)
                v.wait_ge(step, 7)
                v.tensor_scalar(length_i[0:1, 0:P - 1], length_i[0:1, 0:P - 1], float(G - 1), float(INVERSE),
                                ALU.add, ALU.mult).then_inc(divided, 1)
                v.wait_ge(divided, 1)
                v.tensor_scalar(length_i[0:1, 0:P - 1], length_i[0:1, 0:P - 1], INVERSE_BITS, None,
                                ALU.arith_shift_right).then_inc(divided, 1)
                v.wait_ge(divided, 2)
                v.wait_ge(shifted, 1)
                v.tensor_copy(length[0:1, 0:P - 1], length_i[0:1, 0:P - 1]).then_inc(shifted, 1)
                v.wait_ge(shifted, 2)
                v.tensor_tensor_scan(ends[0:1, 0:P - 1], length[0:1, 0:P - 1], zeros[0:1, 0:P - 1], 0.0,
                                     ALU.add, ALU.add).then_inc(shifted, 1)
                v.wait_ge(shifted, 3)
                v.tensor_copy(ahead[0:1, 1:P], ends[0:1, 0:P - 1]).then_inc(step, 1)
                v.wait_ge(columned, 1)
                v.tensor_copy(columns[:, 0:3], ps[1][:, 0:3]).then_inc(shifted, 1)
                v.wait_ge(shifted, 4)
                v.scalar_tensor_tensor(columns[:, 3:4], columns[:, 1:2], -float(SPAN), columns[:, 0:1],
                                       ALU.mult, ALU.add).then_inc(shifted, 1)
                v.wait_ge(iotas, 1)
                v.wait_ge(shifted, 5)
                v.tensor_scalar(owner[:, :], group_id[:, :], columns[:, 1:2], None, ALU.is_ge).then_inc(shifted, 1)
                v.tensor_scalar(after[:, :], group_id[:, :], columns[:, 2:3], None, ALU.is_ge).then_inc(masks, 1)
                v.wait_ge(shifted, 6)
                v.wait_ge(masks, 1)
                v.tensor_tensor(owner[:, :], owner[:, :], after[:, :], ALU.subtract).then_inc(masks, 1)
                for k, (a, b) in enumerate(chunks):
                    v.wait_ge(counted, k + 1)
                    v.tensor_scalar(plan.target0[:, a:b], ps[2][:, 0:b - a], float(P), None, ALU.mult).then_inc(evacuated, 1)
                    v.tensor_scalar(plan.window[0:1, a:b], ps[2][0:1, 0:b - a], float(TILES - 1), None, ALU.min).then_inc(evacuated, 1)
                    v.scalar_tensor_tensor(from_window[0:1, a:b], group_id[0:1, a:b], float(SPAN), ps[3][0:1, 0:b - a],
                                           ALU.mult, ALU.add).then_inc(evacuated, 1)
                v.wait_ge(evacuated, 3 * len(chunks))
                v.tensor_scalar(plan.edge0[0:1, :], from_window[0:1, :], float(E), None, ALU.min).then_inc(shifted, 1)
                v.tensor_reduce(peak[:, :], s.scores[:, :, 0:GH].rearrange("p t h -> p h t"), AX.X, ALU.max).then_inc(peaked, 1)
                v.tensor_copy(s.shift[:, :, 0:GH], s.scores[:, :, GH:2 * GH]).then_inc(shifted, 1)
                v.wait_ge(reduced, 1)
                v.tensor_tensor(sloped[:, :, :], s.scores[:, :, GH:2 * GH],
                                peak_all[:, :].unsqueeze(1).to_broadcast([P, TILES, GH]), ALU.add).then_inc(shifted, 1)
                v.wait_ge(shifted, 9)
                v.scalar_tensor_tensor(s.shift[:, :, GH:2 * GH], sloped[:, :, :], 0.2, sloped[:, :, :],
                                       ALU.mult, ALU.max).then_inc(shifted, 1)
                v.memset(s.big[:, :], 0.0).then_inc(shifted, 1)


def attend_edges(nc, s, plan):
    with ExitStack() as ctx:
        def sb(name, shape, dt=F32):
            return ctx.enter_context(nc.sbuf_tensor(name, shape, dt))

        def sem(name):
            return nc.alloc_semaphore(name=name)

        pairs = sb("pairs", [P, RING, G, 2], I32)
        rows = sb("rows", [P, RING, G * ROW])
        rows4 = rows[:, :, :].rearrange("p r (g n) -> p r g n", g=G)
        rel = sb("rel", [P, RING, G])
        hot = sb("hot", [P, RING, G, P])
        hotT = sb("hotT", [P, 2, G, P])
        e1 = sb("e1", [P, 2, G, GH])
        e2 = sb("e2", [P, 2, G, GH])
        e3 = sb("e3", [P, 2, G, GH])
        msg = sb("msg", [P, 4, G, ROW])
        ps_hot = ctx.enter_context(nc.psum_tensor("ps_hot", [P, 2, 512], F32))
        ps_tgt = ctx.enter_context(nc.psum_tensor("ps_tgt", [P, 2, 512], F32))
        ps_sum = ctx.enter_context(nc.psum_tensor("ps_sum", [P, 2, 512], F32))

        zeros = sb("c_zeros", [P, ZERO_TILES, D])
        zeros_set = sem("c_zeros_set")
        zeros_stored = sem("c_zeros_stored")
        pairs_in = [sem(f"c_pairs_in{j}") for j in range(RING)]
        rows_in = [sem(f"c_rows_in{j}") for j in range(RING)]
        pairs_seen = sem("c_pairs_seen")
        rel_done = sem("c_rel_done")
        hot_ready = sem("c_hot_ready")
        hotT_psum = sem("c_hotT_psum")
        hotT_ready = sem("c_hotT_ready")
        tgt_psum = sem("c_tgt_psum")
        scored = sem("c_scored")
        leaked = sem("c_leaked")
        e_shifted = sem("c_e_shifted")
        e_ready = sem("c_e_ready")
        w_ready = sem("c_w_ready")
        msg_ready = sem("c_msg_ready")
        sum_psum = sem("c_sum_psum")
        sum_added = sem("c_sum_added")

        LOOPS = (GROUPS - HEAD) // RING

        with nc.Block() as block:

            @block.sync
            def _(sp):
                def load(n, j):
                    first = sp.value_load(plan.edge0[0:1, bass.ds(n, 1)], min_val=0, max_val=E)
                    sp.dma_start(pairs[:, j, :, :], s.edges[bass.ds(first, SPAN), :].rearrange("(p g) k -> p g k", p=P))\
                      .then_inc(pairs_in[j], 16)

                for n in range(RING):
                    load(n, n)
                with sp.Fori(0, LOOPS - 1) as i:
                    for j in range(RING):
                        n = i * RING + RING + j
                        sp.wait_ge(msg_ready, n - RING + 1)
                        load(n, j)
                for n in range(LOOPS * RING, GROUPS):
                    sp.wait_ge(msg_ready, n - RING + 1)
                    load(n, n % RING)

            @block.gpsimd
            def _(g):
                def gather(j):
                    for k in range(G):
                        g.indirect_dma_start(rows[:, j, k * ROW:(k + 1) * ROW], None, s.node_rows,
                                             bass.IndirectOffsetOnAxis(ap=pairs[:, j, k, 0:1], axis=0)).then_inc(rows_in[j], 16)

                g.memset(zeros[:, :, :], 0.0).then_inc(zeros_set, 1)
                with g.Fori(0, LOOPS) as i:
                    for j in range(RING):
                        g.wait_ge(pairs_in[j], 16 * i + 16)
                        g.sem_inc(pairs_seen, 1)
                        gather(j)
                for n in range(LOOPS * RING, GROUPS):
                    g.wait_ge(pairs_in[n % RING], 16 * (n // RING + 1))
                    gather(n % RING)

            def in_groups(eng, steps, lag):
                in_step(eng, steps, lag, GROUPS, HEAD, RING)

            @block.vector
            def _(v):
                def relative(n, j, turn):
                    v.wait_ge(pairs_in[j], turn * 16 + 16)
                    v.tensor_scalar(rel[:, j, :], pairs[:, j, :, 1].bitcast(F32), plan.target0[:, bass.ds(n, 1)], None,
                                    ALU.subtract).then_inc(rel_done, 1)

                def one_hot(n, j, turn):
                    v.wait_ge(rel_done, n + 1)
                    v.tensor_tensor(hot[:, j, :, :], s.row_iota[:, :].unsqueeze(1).to_broadcast([P, G, P]),
                                    rel[:, j, :].unsqueeze(2).to_broadcast([P, G, P]), ALU.is_equal).then_inc(hot_ready, 1)

                def target(j):
                    return ps_tgt[:, j % 2, 0:G * 2 * GH].rearrange("p (g k) -> p g k", g=G)

                def score(n, j, turn):
                    v.wait_ge(rows_in[j], turn * (16 * G) + 16 * G)
                    v.wait_ge(tgt_psum, n + 1)
                    v.tensor_tensor(e1[:, j % 2, :, :], rows4[:, j, :, D:ROW], target(j)[:, :, 0:GH], ALU.add).then_inc(scored, 1)

                def leaky(n, j, turn):
                    v.wait_ge(scored, n + 1)
                    b = j % 2
                    v.scalar_tensor_tensor(e2[:, b, :, :], e1[:, b, :, :], 0.2, e1[:, b, :, :], ALU.mult, ALU.max).then_inc(leaked, 1)

                def shifted(n, j, turn):
                    v.wait_ge(leaked, n + 1)
                    v.tensor_tensor(e3[:, j % 2, :, :], e2[:, j % 2, :, :], target(j)[:, :, GH:2 * GH], ALU.subtract).then_inc(e_shifted, 1)

                def bounded(n, j, turn):
                    v.wait_ge(e_shifted, n + 1)
                    v.tensor_scalar(e1[:, j % 2, :, :], e3[:, j % 2, :, :], 0.0, None, ALU.min).then_inc(e_ready, 1)

                def weigh(n, j, turn):
                    v.wait_ge(w_ready, n + 1)
                    m = msg[:, j % 4, :, :]
                    for k in range(G):
                        mm = v.tensor_tensor(m[:, k, 0:D].rearrange("p (h f) -> p h f", h=GH),
                                             rows4[:, j, k, 0:D].rearrange("p (h f) -> p h f", h=GH),
                                             m[:, k, D:ROW].unsqueeze(2).to_broadcast([P, GH, GF]), ALU.mult)
                    mm.then_inc(msg_ready, 1)

                def add_sum(n, j, turn):
                    w = v.value_load(plan.window[0:1, bass.ds(n, 1)], min_val=0, max_val=TILES - 1)
                    v.wait_ge(sum_psum, n + 1)
                    from_item(v, sum_added, n, 1, n)
                    dest = s.sums[:, bass.ds(w, 1), :].rearrange("p t d -> p (t d)")
                    v.tensor_tensor(dest, dest, ps_sum[:, j % 2, 0:ROW], ALU.add).then_inc(sum_added, 1)

                in_groups(v, [relative, score, one_hot, leaky, add_sum, shifted, weigh, bounded], [0, 2, 0, 2, 5, 2, 3, 2])

            @block.scalar
            def _(act):
                def copy_hotT(n, j, turn):
                    act.wait_ge(hotT_psum, n + 1)
                    act.activation(hotT[:, j % 2, :, :], ps_hot[:, j % 2, 0:G * P].rearrange("p (g n) -> p g n", g=G),
                                   ACT.Copy).then_inc(hotT_ready, 1)

                def weights(n, j, turn):
                    act.wait_ge(e_ready, n + 1)
                    act.activation(msg[:, j % 4, :, D:ROW], e1[:, j % 2, :, :], ACT.Exp).then_inc(w_ready, 1)

                act.wait_ge(zeros_set, 1)
                for a in range(0, EX_TILES, ZERO_TILES):
                    b = min(a + ZERO_TILES, EX_TILES)
                    act.dma_start(s.expert_in[a * P:b * P, :].rearrange("(t p) d -> p t d", p=P), zeros[:, 0:b - a, :]).then_inc(zeros_stored, 16)
                in_groups(act, [copy_hotT, weights], [0, 2])
                act.wait_ge(zeros_stored, 16 * -(-EX_TILES // ZERO_TILES))

            @block.tensor
            def _(pe):
                def turn_hot(n, j, turn):
                    pe.wait_ge(hot_ready, n + 1)
                    for k in range(G):
                        mm = pe.transpose(ps_hot[:, j % 2, k * P:(k + 1) * P], hot[:, j, k, :], s.ident[:, :])
                    mm.then_inc(hotT_psum, 1)

                def target_scores(n, j, turn):
                    w = pe.value_load(plan.window[0:1, bass.ds(n, 1)], min_val=0, max_val=TILES - 1)
                    pe.wait_ge(hotT_ready, n + 1)
                    from_item(pe, e_ready, n, 2, n - 1)
                    for k in range(G):
                        mm = pe.matmul(ps_tgt[:, j % 2, k * 2 * GH:(k + 1) * 2 * GH], hotT[:, j % 2, k, :],
                                       s.shift[:, bass.ds(w, 1), :].rearrange("p t k -> p (t k)"), start=True, stop=True)
                    mm.then_inc(tgt_psum, 1)

                def sum_group(n, j, turn):
                    pe.wait_ge(msg_ready, n + 1)
                    for k in range(G):
                        mm = pe.matmul(ps_sum[:, j % 2, 0:ROW], hot[:, j, k, :], msg[:, j % 4, k, :],
                                       start=(k == 0), stop=(k == G - 1))
                    mm.then_inc(sum_psum, 1)

                in_groups(pe, [turn_hot, target_scores, sum_group], [0, 1, 4])


def combine(nc, s, x, gat_bias, w_out, b_out):
    with ExitStack() as ctx:
        def sb(name, shape, dt=F32):
            return ctx.enter_context(nc.sbuf_tensor(name, shape, dt))

        def psum(name):
            return ctx.enter_context(nc.psum_tensor(name, [P, 2, 512], F32))

        def sem(name):
            return nc.alloc_semaphore(name=name)

        h_row = sb("h_row", [P, 2, ROW])
        q_in = sb("q_in", [P, 2, D])
        x_row = sb("x_row", [P, 2, D])
        self_w = sb("self_w", [P, TILES, GH])
        self_t = sb("self_t", [P, TILES, GH])
        rden = sb("rden", [P, TILES, GH])
        xn = sb("xn", [P, 2, D])
        xn_bias = sb("xn_bias", [P, 2, D])
        xn_bout = sb("xn_bout", [P, 2, D])
        own = sb("own", [P, 3, D])
        z = sb("z", [P, 2, MH])
        heads = sb("heads", [P, 2, D])
        headsT = sb("headsT", [P, 2, C, P])
        wo = sb("wo", [P, C, D])
        bias_b = sb("bias_b", [P, D])
        bout_b = sb("bout_b", [P, D])
        hh = sb("hh", [P, 2, D])
        ps_a = psum("ps_a")
        ps_at = psum("ps_at")
        ps_o = psum("ps_o")

        w_in = sem("d_w_in")
        loaded = [sem(f"d_loaded{u}") for u in range(2)]
        self_step = sem("d_self_step")
        self_exp = sem("d_self_exp")
        xn_ready = sem("d_xn_ready")
        xn_biased = sem("d_xn_biased")
        attended = sem("d_attended")
        z_step = sem("d_z_step")
        heads_ready = sem("d_heads_ready")
        headsT_psum = sem("d_headsT_psum")
        headsT_ready = sem("d_headsT_ready")
        out_psum = sem("d_out_psum")
        hh_ready = sem("d_hh_ready")
        own_step = sem("d_own_step")
        tile_done = sem("d_tile_done")
        stored = [sem(f"d_stored{u}") for u in range(2)]
        hh_free = sem("d_hh_free")

        with nc.Block() as block:

            @block.sync
            def _(sp):
                sp.dma_start(wo[:, :, :], w_out.rearrange("(c p) n -> p c n", p=P)).then_inc(w_in, 16)
                sp.dma_start(bias_b[:, :], gat_bias.partition_broadcast(P)).then_inc(w_in, 16)
                sp.dma_start(bout_b[:, :], b_out.partition_broadcast(P)).then_inc(w_in, 16)
                sp.sem_inc(tile_done, 2)

                def load(t, u, rows):
                    sp.wait_ge(tile_done, t + 1)
                    sp.dma_start(h_row[:, u, :], s.node_rows[bass.ds(t * P, P), :]).then_inc(loaded[u], 16)
                    sp.dma_start(q_in[:, u, :], s.queries[bass.ds(t * P, P), :]).then_inc(loaded[u], 16)
                    sp.dma_start(x_row[0:rows, u, :], x[bass.ds(t * P, rows), :]).then_inc(loaded[u], 16)

                with sp.Fori(0, TILES - 3, 2) as t0:
                    load(t0, 0, P)
                    load(t0 + 1, 1, P)
                load(TILES - 2, 0, P)
                load(TILES - 1, 1, TAIL)

            @block.gpsimd
            def _(g):
                g.sem_inc(hh_free, 2)
                g.wait_ge(w_in, 48)
                with g.Fori(0, TILES - 1, 2) as t0:
                    for u in range(2):
                        t = t0 + u
                        g.wait_ge(xn_ready, t + 1)
                        g.tensor_tensor(xn_bias[:, u, :], xn[:, u, :], bias_b[:, :], ALU.add).then_inc(xn_biased, 1)
                        g.tensor_tensor(xn_bout[:, u, :], xn[:, u, :], bout_b[:, :], ALU.add).then_inc(xn_biased, 1)

            @block.scalar
            def _(act):
                act.wait_ge(self_step, 4)
                act.activation(self_w[:, :, :], self_t[:, :, :], ACT.Exp).then_inc(self_exp, 1)

                def tile(t, t0, u, first):
                    act.wait_ge(loaded[u], 24 * t0 + 48)
                    act.wait_ge(tile_done, t + 1)
                    act.activation(xn[:, u, :], x_row[:, u, :], ACT.Identity, bias=s.ln_bias[:, bass.ds(t, 1)],
                                   scale=s.ln_scale[:, bass.ds(t, 1)]).then_inc(xn_ready, 1)
                    act.wait_ge(headsT_psum, t + 1)
                    act.activation(headsT[:, u, :, :], ps_at[:, u, 0:D].rearrange("p (c n) -> p c n", c=C),
                                   ACT.Copy).then_inc(headsT_ready, 1)
                    act.wait_ge(hh_ready, t + 1)
                    act.dma_start(s.mixed[bass.ds(t * P, P), :], hh[:, u, :]).then_inc(stored[u], 16)
                    if not first:
                        act.wait_ge(stored[1 - u], 8 * t0 + 16 * u)
                        act.sem_inc(hh_free, 1)

                tile(0, 0, 0, True)
                tile(1, 0, 1, False)
                with act.Fori(2, TILES - 1, 2) as t0:
                    tile(t0, t0, 0, False)
                    tile(t0 + 1, t0, 1, False)
                for u in range(2):
                    act.wait_ge(stored[u], 16 * (TILES // 2))

            @block.tensor
            def _(pe):
                pe.wait_ge(w_in, 48)
                with pe.Fori(0, TILES - 1, 2) as t0:
                    for u in range(2):
                        t = t0 + u
                        pe.wait_ge(loaded[u], 24 * t0 + 48)
                        pe.wait_ge(tile_done, t + 1)
                        for c in range(C):
                            mm = pe.matmul(ps_a[:, u, c * (P + 4):(c + 1) * (P + 4)], q_in[:, u, c * P:(c + 1) * P], s.kv[:, c, :],
                                           start=True, stop=True)
                        mm.then_inc(attended, 1)
                        pe.wait_ge(heads_ready, t + 1)
                        for c in range(C):
                            mm = pe.transpose(ps_at[:, u, c * P:(c + 1) * P], heads[:, u, c * P:(c + 1) * P], s.ident[:, :])
                        mm.then_inc(headsT_psum, 1)
                        pe.wait_ge(headsT_ready, t + 1)
                        for c in range(C):
                            mm = pe.matmul(ps_o[:, u, 0:D], headsT[:, u, c, :], wo[:, c, :], start=(c == 0), stop=(c == C - 1))
                        mm.then_inc(out_psum, 1)

            @block.vector
            def _(v):
                v.tensor_tensor(self_w[:, :, :], s.scores[:, :, 0:GH], s.scores[:, :, GH:2 * GH], ALU.add).then_inc(self_step, 1)
                v.wait_ge(self_step, 1)
                v.scalar_tensor_tensor(self_t[:, :, :], self_w[:, :, :], 0.2, self_w[:, :, :], ALU.mult, ALU.max).then_inc(self_step, 1)
                v.wait_ge(self_step, 2)
                v.tensor_tensor(self_w[:, :, :], self_t[:, :, :], s.shift[:, :, GH:2 * GH], ALU.subtract).then_inc(self_step, 1)
                v.wait_ge(self_step, 3)
                v.tensor_scalar(self_t[:, :, :], self_w[:, :, :], 0.0, None, ALU.min).then_inc(self_step, 1)
                v.wait_ge(self_exp, 1)
                v.tensor_tensor(self_t[:, :, :], self_w[:, :, :], s.sums[:, :, D:ROW], ALU.add).then_inc(self_step, 1)
                v.wait_ge(self_step, 5)
                v.reciprocal(rden[:, :, :], self_t[:, :, :]).then_inc(self_step, 1)
                v.wait_ge(self_step, 6)
                with v.Fori(0, TILES - 1, 2) as t0:
                    for u in range(2):
                        t = t0 + u
                        base = t * 4
                        total = s.sums[:, bass.ds(t, 1), 0:D].rearrange("p t d -> p (t d)")

                        def per_head(table):
                            return table[:, bass.ds(t, 1), :].rearrange("p t h -> p (t h)").unsqueeze(2).to_broadcast([P, GH, GF])

                        def split(a):
                            return a.rearrange("p (h f) -> p h f", h=GH)

                        v.wait_ge(loaded[u], 24 * t0 + 48)
                        v.tensor_tensor(split(own[:, 0, :]), split(h_row[:, u, 0:D]), per_head(self_w), ALU.mult).then_inc(own_step, 1)
                        v.wait_ge(attended, t + 1)
                        att = ps_a[:, u, 0:C * (P + 4)].rearrange("p (c n) -> p c n", c=C)
                        v.tensor_scalar(z[:, 0, :].rearrange("p (c j) -> p c j", c=C), att[:, :, P:P + 4], 1e-6, None, ALU.add).then_inc(z_step, 1)
                        v.wait_ge(z_step, 2 * t + 1)
                        v.reciprocal(z[:, 1, :], z[:, 0, :]).then_inc(z_step, 1)
                        v.wait_ge(z_step, 2 * t + 2)
                        for c in range(C):
                            mm = v.tensor_tensor(heads[:, u, c * P:(c + 1) * P].rearrange("p (j m) -> p j m", j=4),
                                                 att[:, c, 0:P].rearrange("p (j m) -> p j m", j=4),
                                                 z[:, 1, 4 * c:4 * c + 4].unsqueeze(2).to_broadcast([P, 4, MF]), ALU.mult)
                        mm.then_inc(heads_ready, 1)
                        v.wait_ge(own_step, base + 1)
                        v.tensor_tensor(own[:, 1, :], own[:, 0, :], total, ALU.add).then_inc(own_step, 1)
                        v.wait_ge(own_step, base + 2)
                        v.tensor_tensor(split(own[:, 2, :]), split(own[:, 1, :]), per_head(rden), ALU.mult).then_inc(own_step, 1)
                        v.wait_ge(own_step, base + 3)
                        v.wait_ge(xn_biased, 2 * t + 2)
                        v.tensor_tensor(total, own[:, 2, :], xn_bias[:, u, :], ALU.add).then_inc(own_step, 1)
                        v.wait_ge(own_step, base + 4)
                        v.bn_stats(s.gat_stats[:, bass.ds(t, 1), :].rearrange("p t k -> p (t k)"), total).then_inc(s.gat_stat, 1)
                        v.wait_ge(out_psum, t + 1)
                        v.wait_ge(hh_free, t + 1)
                        v.tensor_tensor(hh[:, u, :], ps_o[:, u, 0:D], xn_bout[:, u, :], ALU.add).then_inc(hh_ready, 1)
                        v.wait_ge(hh_ready, t + 1)
                        v.bn_stats(s.mix_stats[:, bass.ds(t, 1), :].rearrange("p t k -> p (t k)"), hh[:, u, :]).then_inc(s.mix_stat, 1)
                        v.wait_ge(s.mix_stat, t + 1)
                        v.sem_inc(tile_done, 1)


def join(nc, s, x, gamma, beta, w_norm2):
    with ExitStack() as ctx:
        def sb(name, shape, dt=F32):
            return ctx.enter_context(nc.sbuf_tensor(name, shape, dt))

        def sem(name):
            return nc.alloc_semaphore(name=name)

        x_row = sb("e_x_row", [P, 2, D])
        hh = sb("e_hh", [P, 2, D])
        mean = sb("e_mean", [P, TILES])
        var = sb("e_var", [P, TILES])
        tmp = sb("e_tmp", [P, TILES])
        a_gat = sb("a_gat", [P, TILES])
        b_gat = sb("b_gat", [P, TILES])
        a_mix = sb("a_mix", [P, TILES])
        root = sb("e_root", [P, 2, TILES])
        gamma_b = sb("gamma_b", [P, D])
        beta_b = sb("beta_b", [P, D])
        w2_b = sb("w2_b", [P, D])
        yl = sb("yl", [P, 2, D])
        hr = sb("hr", [P, 2, D])
        hw = sb("hw", [P, 2, D])
        both = sb("both", [P, 2, D])
        g1 = sb("g1", [P, 3, D])

        w_in = sem("e_w_in")
        loaded = [sem(f"e_loaded{u}") for u in range(2)]
        gat_agg = sem("e_gat_agg")
        mix_agg = sem("e_mix_agg")
        chain = sem("e_chain")
        root_in = sem("e_root_in")
        rooted = sem("e_rooted")
        scales_ready = sem("e_scales_ready")
        yl_ready = sem("e_yl_ready")
        hr_ready = sem("e_hr_ready")
        hw_ready = sem("e_hw_ready")
        both_ready = sem("e_both_ready")
        g_step = sem("e_g_step")
        tile_done = sem("e_tile_done")
        stat = sem("e_stat")
        stat_agg = sem("e_stat_agg")

        with nc.Block() as block:

            @block.sync
            def _(sp):
                sp.dma_start(gamma_b[:, :], gamma.partition_broadcast(P)).then_inc(w_in, 16)
                sp.dma_start(beta_b[:, :], beta.partition_broadcast(P)).then_inc(w_in, 16)
                sp.dma_start(w2_b[:, :], w_norm2.partition_broadcast(P)).then_inc(w_in, 16)
                sp.sem_inc(tile_done, 2)

                def load(t, u, rows):
                    sp.wait_ge(tile_done, t + 1)
                    sp.dma_start(hh[:, u, :], s.mixed[bass.ds(t * P, P), :]).then_inc(loaded[u], 16)
                    sp.dma_start(x_row[0:rows, u, :], x[bass.ds(t * P, rows), :]).then_inc(loaded[u], 16)

                with sp.Fori(0, TILES - 3, 2) as t0:
                    load(t0, 0, P)
                    load(t0 + 1, 1, P)
                load(TILES - 2, 0, P)
                load(TILES - 1, 1, TAIL)

            @block.gpsimd
            def _(g):
                g.wait_ge(w_in, 48)
                with g.Fori(0, TILES - 1, 2) as t0:
                    for u in range(2):
                        t = t0 + u
                        g.wait_ge(hr_ready, t + 1)
                        g.tensor_tensor(hw[:, u, :], hr[:, u, :], w2_b[:, :], ALU.mult).then_inc(hw_ready, 1)
                        g.wait_ge(hw_ready, t + 1)
                        g.tensor_tensor(both[:, u, :], hw[:, u, :], hh[:, u, :], ALU.add).then_inc(both_ready, 1)

            @block.scalar
            def _(act):
                act.wait_ge(root_in, 2)
                act.activation(root[:, 0, :], root[:, 0, :], ACT.Sqrt).then_inc(rooted, 1)
                act.activation(root[:, 1, :], root[:, 1, :], ACT.Sqrt).then_inc(rooted, 1)
                act.wait_ge(scales_ready, 3)
                with act.Fori(0, TILES - 1, 2) as t0:
                    for u in range(2):
                        t = t0 + u
                        act.wait_ge(tile_done, t + 1)
                        act.activation(yl[:, u, :], s.sums[:, bass.ds(t, 1), 0:D].rearrange("p t d -> p (t d)"), ACT.Identity,
                                       bias=b_gat[:, bass.ds(t, 1)], scale=a_gat[:, bass.ds(t, 1)]).then_inc(yl_ready, 1)
                        act.wait_ge(loaded[u], 16 * t0 + 32)
                        act.activation(hr[:, u, :], hh[:, u, :], ACT.Copy, scale=a_mix[:, bass.ds(t, 1)]).then_inc(hr_ready, 1)

            @block.vector
            def _(v):
                mean_and_variance(v, s.mix_stats, mean[:, :], var[:, :], tmp[:, :], mix_agg)
                v.tensor_tensor(tmp[:, :], mean[:, :], mean[:, :], ALU.mult).then_inc(chain, 1)
                v.wait_ge(chain, 1)
                v.scalar_tensor_tensor(root[:, 1, :], var[:, :], 1e-6, tmp[:, :], ALU.add, ALU.add).then_inc(root_in, 1)
                v.wait_ge(root_in, 1)
                mean_and_variance(v, s.gat_stats, mean[:, :], var[:, :], tmp[:, :], gat_agg)
                v.tensor_scalar(root[:, 0, :], var[:, :], 1e-5, None, ALU.add).then_inc(root_in, 1)
                v.wait_ge(rooted, 2)
                v.reciprocal(a_mix[:, :], root[:, 1, :]).then_inc(scales_ready, 1)
                v.reciprocal(a_gat[:, :], root[:, 0, :]).then_inc(scales_ready, 1)
                v.wait_ge(scales_ready, 2)
                v.scalar_tensor_tensor(b_gat[:, :], mean[:, :], -1.0, a_gat[:, :], ALU.mult, ALU.mult).then_inc(scales_ready, 1)
                v.wait_ge(w_in, 48)
                with v.Fori(0, TILES - 1, 2) as t0:
                    for u in range(2):
                        t = t0 + u
                        state = s.sums[:, bass.ds(t, 1), 0:D].rearrange("p t d -> p (t d)")
                        v.wait_ge(yl_ready, t + 1)
                        v.tensor_tensor(g1[:, 0, :], yl[:, u, :], gamma_b[:, :], ALU.mult).then_inc(g_step, 1)
                        v.wait_ge(g_step, 4 * t + 1)
                        v.tensor_tensor(g1[:, 1, :], g1[:, 0, :], beta_b[:, :], ALU.add).then_inc(g_step, 1)
                        v.wait_ge(g_step, 4 * t + 2)
                        v.wait_ge(loaded[u], 16 * t0 + 32)
                        v.scalar_tensor_tensor(g1[:, 2, :], g1[:, 1, :], 0.0, x_row[:, u, :], ALU.max, ALU.add).then_inc(g_step, 1)
                        v.wait_ge(g_step, 4 * t + 3)
                        v.wait_ge(both_ready, t + 1)
                        v.tensor_tensor(state, g1[:, 2, :], both[:, u, :], ALU.add).then_inc(g_step, 1)
                        v.wait_ge(g_step, 4 * t + 4)
                        v.sem_inc(tile_done, 1)
                        v.bn_stats(s.gat_stats[:, bass.ds(t, 1), :].rearrange("p t k -> p (t k)"), state).then_inc(stat, 1)
                v.wait_ge(stat, TILES)
                mean_and_variance(v, s.gat_stats, s.state_mean[:, :], s.state_var[:, :], tmp[:, :], stat_agg)


def flat(table, t, *cols):
    part = table[(slice(None), bass.ds(t, 1)) + cols]
    return part.rearrange("p t d -> p (t d)") if len(part.shape) == 3 else part


def route(nc, s, gamma, beta, Wr, br):
    with ExitStack() as ctx:
        def sb(name, shape, dt=F32):
            return ctx.enter_context(nc.sbuf_tensor(name, shape, dt))

        def psum(name):
            return ctx.enter_context(nc.psum_tensor(name, [P, 2, 512], F32))

        def sem(name):
            return nc.alloc_semaphore(name=name)

        TE = [P, TILES, EXPERTS]
        a_in = sb("a_in", [P, TILES])
        b_in = sb("b_in", [P, TILES])
        root = sb("f_root", [P, TILES])
        tmp = sb("f_tmp", [P, TILES])
        gamma_b = sb("f_gamma_b", [P, D])
        beta_b = sb("f_beta_b", [P, D])
        wr = sb("wr", [P, C, EXPERTS])
        br_b = sb("br_b", [P, EXPERTS])
        centred = sb("centred", [P, 2, D])
        scaled = sb("scaled", [P, 2, D])
        rows = sb("f_rows", [P, 2, D])
        rowsT = sb("f_rowsT", [P, 2, C, P])
        logits = sb("logits", TE)
        lane = sb("lane", TE)
        picked = [sb("picked0", TE), sb("picked1", TE)]
        work = sb("f_work", TE)
        work2 = sb("f_work2", TE)
        taken = sb("taken", TE)
        totals = sb("totals", TE)
        running = sb("running", TE)
        place = sb("place", TE)
        best = sb("best", [P, 2, TILES])
        lowest = sb("lowest", [P, 2, TILES])
        gap = sb("gap", [P, TILES])
        odds = sb("odds", [P, TILES])
        slot_f = sb("slot_f", [P, 2, TILES])
        zeros = sb("f_zeros", [P, TILES])
        tiles_i = sb("tiles_i", [P, EXPERTS], I32)
        tiles_f = sb("tiles_f", [P, EXPERTS])
        tile_end = sb("tile_end", [P, EXPERTS])
        tile_start = sb("tile_start", [P, EXPERTS])
        earlier = sb("earlier", [P, P])
        tile_id = sb("tile_id", [1, EX_TILES])
        owner = sb("f_owner", [1, 2, EX_TILES])
        ps_t = psum("f_ps_t")
        ps_l = psum("f_ps_l")
        ps_rank = psum("f_ps_rank")
        ps_tot = psum("f_ps_tot")

        w_in = sem("f_w_in")
        consts = sem("f_consts")
        chain = sem("f_chain")
        root_in = sem("f_root_in")
        rooted = sem("f_rooted")
        scales = sem("f_scales")
        centred_ready = sem("f_centred_ready")
        scaled_ready = sem("f_scaled_ready")
        rows_ready = sem("f_rows_ready")
        rowsT_psum = sem("f_rowsT_psum")
        rowsT_ready = sem("f_rowsT_ready")
        logit_psum = sem("f_logit_psum")
        logit_ready = sem("f_logit_ready")
        row_free = sem("f_row_free")
        stored = [sem(f"f_stored{u}") for u in range(2)]
        gap_ready = sem("f_gap_ready")
        odds_ready = sem("f_odds_ready")
        taken_ready = sem("f_taken_ready")
        ranked = sem("f_ranked")
        step = sem("f_step")
        HALF = TILES // 2

        with nc.Block() as block:

            @block.sync
            def _(sp):
                sp.dma_start(gamma_b[:, :], gamma.partition_broadcast(P)).then_inc(w_in, 16)
                sp.dma_start(beta_b[:, :], beta.partition_broadcast(P)).then_inc(w_in, 16)
                sp.dma_start(br_b[:, :], br.partition_broadcast(P)).then_inc(w_in, 16)
                sp.dma_start(wr[:, :, :], Wr.rearrange("(c p) e -> p c e", p=P)).then_inc(w_in, 16)
                sp.sem_inc(row_free, 2)
                with sp.Fori(0, TILES - 1, 2) as t0:
                    for u in range(2):
                        t = t0 + u
                        sp.wait_ge(rows_ready, t + 1)
                        sp.dma_start(s.ffn_in[bass.ds(t * P, P), :], rows[:, u, :]).then_inc(stored[u], 16)
                        sp.wait_ge(stored[u], 8 * t0 + 16)
                        sp.sem_inc(row_free, 1)

            @block.gpsimd
            def _(g):
                g.iota(lane[:, :, :], [[0, TILES], [1, EXPERTS]], base=0, channel_multiplier=0,
                       allow_small_or_imprecise_dtypes=True).then_inc(consts, 1)
                g.iota(tile_id[:, :], [[1, EX_TILES]], base=0, channel_multiplier=0,
                       allow_small_or_imprecise_dtypes=True).then_inc(consts, 1)
                g.memset(zeros[:, :], 0.0).then_inc(consts, 1)
                g.memset(owner[:, 0, :], 0.0).then_inc(consts, 1)
                g.memset(earlier[:, :], 1.0).then_inc(consts, 1)
                g.wait_ge(consts, 5)
                g.affine_select(out=earlier[:, :], in_=earlier[:, :], compare_op=ALU.is_gt, fill=0.0,
                                base=0, pattern=[[1, P]], channel_multiplier=-1).then_inc(consts, 1)

            @block.scalar
            def _(act):
                act.wait_ge(root_in, 1)
                act.activation(root[:, :], tmp[:, :], ACT.Sqrt).then_inc(rooted, 1)
                act.wait_ge(root_in, 2)
                act.activation(root[:, :], tmp[:, :], ACT.Sqrt).then_inc(rooted, 1)
                act.wait_ge(scales, 2)

                def centre(t, u):
                    act.activation(centred[:, u, :], flat(s.sums, t, slice(0, D)), ACT.Identity,
                                   bias=b_in[:, bass.ds(t, 1)], scale=a_in[:, bass.ds(t, 1)]).then_inc(centred_ready, 1)

                def copy_rowsT(t, u):
                    act.wait_ge(rowsT_psum, t + 1)
                    act.activation(rowsT[:, u, :, :], ps_t[:, u, 0:D].rearrange("p (c n) -> p c n", c=C), ACT.Copy).then_inc(rowsT_ready, 1)

                centre(0, 0)
                centre(1, 1)
                with act.Fori(0, TILES - 3, 2) as t0:
                    for u in range(2):
                        copy_rowsT(t0 + u, u)
                        centre(t0 + u + 2, u)
                for u in range(2):
                    copy_rowsT(TILES - 2 + u, u)
                act.wait_ge(gap_ready, 1)
                act.activation(odds[:, :], gap[:, :], ACT.Exp).then_inc(odds_ready, 1)

            @block.tensor
            def _(pe):
                pe.wait_ge(w_in, 64)
                with pe.Fori(0, TILES - 1, 2) as t0:
                    for u in range(2):
                        t = t0 + u
                        pe.wait_ge(rows_ready, t + 1)
                        for c in range(C):
                            mm = pe.transpose(ps_t[:, u, c * P:(c + 1) * P], rows[:, u, c * P:(c + 1) * P], s.ident[:, :])
                        mm.then_inc(rowsT_psum, 1)
                        pe.wait_ge(rowsT_ready, t + 1)
                        for c in range(C):
                            mm = pe.matmul(ps_l[:, u, 0:EXPERTS], rowsT[:, u, c, :], wr[:, c, :], start=(c == 0), stop=(c == C - 1))
                        mm.then_inc(logit_psum, 1)
                pe.wait_ge(consts, 6)
                pe.wait_ge(taken_ready, 1)
                for k in range(2):
                    part = taken[:, k * HALF:(k + 1) * HALF, :].rearrange("p t e -> p (t e)")
                    pe.matmul(ps_rank[:, k, 0:HALF * EXPERTS], earlier[:, :], part, start=True, stop=True)
                    mm = pe.matmul(ps_tot[:, k, 0:HALF * EXPERTS], s.ones[:, :], part, start=True, stop=True)
                mm.then_inc(ranked, 1)

            @block.vector
            def _(v):
                v.tensor_scalar(tmp[:, :], s.state_var[:, :], 1e-5, None, ALU.add).then_inc(root_in, 1)
                v.wait_ge(rooted, 1)
                v.reciprocal(a_in[:, :], root[:, :]).then_inc(chain, 1)
                v.wait_ge(chain, 1)
                v.tensor_tensor(tmp[:, :], a_in[:, :], a_in[:, :], ALU.mult).then_inc(chain, 1)
                v.wait_ge(chain, 2)
                v.tensor_tensor(b_in[:, :], tmp[:, :], s.state_var[:, :], ALU.mult).then_inc(chain, 1)
                v.wait_ge(chain, 3)
                v.tensor_scalar(tmp[:, :], b_in[:, :], 1e-5, None, ALU.add).then_inc(root_in, 1)
                v.wait_ge(rooted, 2)
                v.reciprocal(b_in[:, :], root[:, :]).then_inc(chain, 1)
                v.wait_ge(chain, 4)
                v.tensor_tensor(a_in[:, :], a_in[:, :], b_in[:, :], ALU.mult).then_inc(scales, 1)
                v.wait_ge(scales, 1)
                v.scalar_tensor_tensor(b_in[:, :], s.state_mean[:, :], -1.0, a_in[:, :], ALU.mult, ALU.mult).then_inc(scales, 1)
                v.wait_ge(w_in, 64)
                with v.Fori(0, TILES - 1, 2) as t0:
                    for u in range(2):
                        t = t0 + u
                        v.wait_ge(centred_ready, t + 1)
                        v.tensor_tensor(scaled[:, u, :], centred[:, u, :], gamma_b[:, :], ALU.mult).then_inc(scaled_ready, 1)
                        v.wait_ge(scaled_ready, t + 1)
                        v.wait_ge(row_free, t + 1)
                        v.tensor_tensor(rows[:, u, :], scaled[:, u, :], beta_b[:, :], ALU.add).then_inc(rows_ready, 1)
                        v.wait_ge(logit_psum, t + 1)
                        v.tensor_tensor(flat(logits, t, slice(0, EXPERTS)), ps_l[:, u, 0:EXPERTS], br_b[:, :], ALU.add).then_inc(logit_ready, 1)
                v.wait_ge(consts, 6)
                v.wait_ge(logit_ready, TILES)
                n = [0]

                def done(ins):
                    n[0] += 1
                    ins.then_inc(step, 1)
                    v.wait_ge(step, n[0])

                def over_experts(a):
                    return a.unsqueeze(2).to_broadcast(TE)

                for k, table in enumerate((logits, work)):
                    done(v.tensor_reduce(best[:, k, :], table[:, :, :], AX.X, ALU.max))
                    done(v.tensor_tensor(work2[:, :, :], table[:, :, :], over_experts(best[:, k, :]), ALU.is_ge))
                    done(v.scalar_tensor_tensor(place[:, :, :], work2[:, :, :], -float(EXPERTS), lane[:, :, :], ALU.mult, ALU.add))
                    done(v.tensor_reduce(lowest[:, k, :], place[:, :, :], AX.X, ALU.min))
                    done(v.tensor_tensor(picked[k][:, :, :], place[:, :, :], over_experts(lowest[:, k, :]), ALU.is_equal))
                    if k == 0:
                        done(v.tensor_scalar(work2[:, :, :], picked[0][:, :, :], -1.0, 1.0, ALU.mult, ALU.add))
                        done(v.tensor_tensor(place[:, :, :], logits[:, :, :], work2[:, :, :], ALU.mult))
                        done(v.scalar_tensor_tensor(work[:, :, :], picked[0][:, :, :], -3e38, place[:, :, :], ALU.mult, ALU.add))
                v.tensor_tensor(gap[:, :], best[:, 1, :], best[:, 0, :], ALU.subtract).then_inc(gap_ready, 1)
                done(v.tensor_tensor(work[:, :, :], picked[0][:, :, :], picked[1][:, :, :], ALU.add))
                v.tensor_tensor(taken[:, :, :], work[:, :, :], over_experts(s.valid[:, :]), ALU.mult).then_inc(taken_ready, 1)
                v.wait_ge(odds_ready, 1)
                done(v.tensor_scalar(tmp[:, :], odds[:, :], 1.0, None, ALU.add))
                done(v.reciprocal(s.weight[:, 0, :], tmp[:, :]))
                done(v.tensor_tensor(s.weight[:, 1, :], odds[:, :], s.weight[:, 0, :], ALU.mult))
                v.wait_ge(ranked, 1)
                halves = "p (t e) -> p t e"
                for k in range(2):
                    done(v.tensor_copy(totals[:, k * HALF:(k + 1) * HALF, :], ps_tot[:, k, 0:HALF * EXPERTS].rearrange(halves, e=EXPERTS)))
                for e in range(EXPERTS):
                    done(v.tensor_tensor_scan(running[:, :, e], totals[:, :, e], zeros[:, :], 0.0, ALU.add, ALU.add))
                done(v.tensor_scalar(tiles_i[:, :], running[:, TILES - 1, :], float(P - 1), None, ALU.add))
                done(v.tensor_scalar(tiles_i[:, :], tiles_i[:, :], P.bit_length() - 1, None, ALU.arith_shift_right))
                done(v.tensor_copy(tiles_f[:, :], tiles_i[:, :]))
                done(v.tensor_tensor_scan(tile_end[:, :], tiles_f[:, :], zeros[:, 0:EXPERTS], 0.0, ALU.add, ALU.add))
                done(v.tensor_tensor(tile_start[:, :], tile_end[:, :], tiles_f[:, :], ALU.subtract))
                done(v.tensor_tensor(place[:, :, :], running[:, :, :], totals[:, :, :], ALU.subtract))
                for k in range(2):
                    part = slice(k * HALF, (k + 1) * HALF)
                    done(v.tensor_tensor(work[:, part, :], place[:, part, :], ps_rank[:, k, 0:HALF * EXPERTS].rearrange(halves, e=EXPERTS), ALU.add))
                done(v.scalar_tensor_tensor(place[:, :, :], tile_start[:, :].unsqueeze(1).to_broadcast(TE), float(P), work[:, :, :], ALU.mult, ALU.add))
                for k in range(2):
                    done(v.tensor_tensor(work[:, :, :], picked[k][:, :, :], place[:, :, :], ALU.mult))
                    done(v.tensor_reduce(slot_f[:, k, :], work[:, :, :], AX.X, ALU.add))
                done(v.tensor_copy(s.slot[:, :, :], slot_f[:, :, :]))
                for e in range(EXPERTS):
                    done(v.scalar_tensor_tensor(owner[:, 1 - e % 2, :], tile_id[:, :], tile_end[0:1, e:e + 1], owner[:, e % 2, :], ALU.is_ge, ALU.add))
                done(v.tensor_scalar(s.expert_of[:, :], owner[:, EXPERTS % 2, :], float(EXPERTS - 1), None, ALU.min))


def scatter_rows(nc, s):
    with ExitStack() as ctx:
        rows = ctx.enter_context(nc.sbuf_tensor("g_rows", [P, 4, D], F32))
        index = ctx.enter_context(nc.sbuf_tensor("g_index", [P, 4, 2], I32))
        loaded = [nc.alloc_semaphore(name=f"g_loaded{j}") for j in range(4)]
        scattered = [[nc.alloc_semaphore(name=f"g_scattered{j}_{k}") for k in range(2)] for j in range(4)]
        indexed = nc.alloc_semaphore(name="g_indexed")

        with nc.Block() as block:

            @block.sync
            def _(sp):
                def load(t, j, turn):
                    row = fixed(sp, t * P)
                    times = fixed(sp, turn * 16)
                    for k in range(2):
                        from_item(sp, scattered[j][k], t, 4, times)
                    sp.dma_start(rows[:, j, :], s.ffn_in[bass.ds(row, P), :]).then_inc(loaded[j], 16)

                in_step(sp, [load], [0], TILES, 6, 4)

            @block.gpsimd
            def _(g):
                def scatter(t, j, turn, count=P):
                    g.wait_ge(loaded[j], turn * 16 + 16)
                    g.sem_inc(s.wait_seen, 1)
                    g.tensor_copy(index[:, j, :], s.slot[:, :, bass.ds(t, 1)].rearrange("p k t -> p (k t)")).then_inc(indexed, 1)
                    g.wait_ge(indexed, t + 1)
                    g.sem_inc(s.wait_seen, 1)
                    for k in range(2):
                        g.indirect_dma_start(s.expert_in, bass.IndirectOffsetOnAxis(ap=index[0:count, j, k:k + 1], axis=0),
                                             rows[0:count, j, :], None).then_inc(scattered[j][k], 16)

                def scatter_or_tail(t, j, turn):
                    scatter(t, j, turn, TAIL if isinstance(t, int) and t == TILES - 1 else P)

                in_step(g, [scatter_or_tail], [0], TILES - 1, 5, 4)
                scatter_or_tail(TILES - 1, (TILES - 1) % 4, (TILES - 1) // 4)
                for j in range(4):
                    for k in range(2):
                        g.wait_ge(scattered[j][k], 16 * len(range(j, TILES, 4)))


def run_experts(nc, s, W1, b1, W2, b2):
    with ExitStack() as ctx:
        def sb(name, shape, dt=F32):
            return ctx.enter_context(nc.sbuf_tensor(name, shape, dt))

        def psum(name):
            return ctx.enter_context(nc.psum_tensor(name, [P, 2, 512], F32))

        def sem(name):
            return nc.alloc_semaphore(name=name)

        w1 = sb("w1", [P, EXPERTS, C * HID])
        w2 = sb("w2", [P, EXPERTS, HC * D])
        b1T = sb("b1T", [P, EXPERTS * HC])
        b2_b = sb("b2_b", [P, EXPERTS, D])
        rows = sb("x_rows", [P, EX_RING, D])
        rowsT = sb("x_rowsT", [P, 2, C, P])
        w1_now = sb("x_w1_now", [P, 2, C * HID])
        actT = sb("x_actT", [P, 2, HC, P])
        outs = sb("x_outs", [P, EX_RING, D])
        ps_t = psum("x_ps_t")
        ps_hT = psum("x_ps_hT")
        ps_out = psum("x_ps_out")

        w_in = sem("x_w_in")
        loaded = [sem(f"x_loaded{j}") for j in range(EX_RING)]
        stored = [sem(f"x_stored{j}") for j in range(EX_RING)]
        rowsT_psum = sem("x_rowsT_psum")
        rowsT_ready = sem("x_rowsT_ready")
        w1_ready = sem("x_w1_ready")
        hT_psum = sem("x_hT_psum")
        act_ready = sem("x_act_ready")
        out_psum = sem("x_out_psum")
        out_ready = sem("x_out_ready")

        def in_tiles(eng, steps, lag):
            in_step(eng, steps, lag, EX_TILES, EX_HEAD, EX_RING)

        def expert(eng, n):
            return eng.value_load(s.expert_of[0:1, bass.ds(n, 1)], min_val=0, max_val=EXPERTS - 1)

        with nc.Block() as block:

            @block.sync
            def _(sp):
                for e in range(EXPERTS):
                    sp.dma_start(w1[:, e, :].rearrange("p (c n) -> p c n", c=C), W1[e].rearrange("(c p) n -> p c n", p=P)).then_inc(w_in, 16)
                    sp.dma_start(w2[:, e, :].rearrange("p (c n) -> p c n", c=HC), W2[e].rearrange("(c p) n -> p c n", p=P)).then_inc(w_in, 16)
                    for c in range(HC):
                        sp.dma_start(b1T[:, e * HC + c:e * HC + c + 1], b1[e, c * P:(c + 1) * P].rearrange("(p o) -> p o", o=1)).then_inc(w_in, 16)
                sp.dma_start(b2_b[:, :, :].rearrange("p e d -> p (e d)"), b2.rearrange("e d -> (e d)").partition_broadcast(P)).then_inc(w_in, 16)

                def load(n, j, turn):
                    row = fixed(sp, n * P)
                    from_item(sp, rowsT_psum, n, EX_RING, n - EX_RING + 1)
                    sp.dma_start(rows[:, j, :], s.expert_in[bass.ds(row, P), :]).then_inc(loaded[j], 16)

                def store(n, j, turn):
                    row = fixed(sp, n * P)
                    sp.wait_ge(out_ready, n + 1)
                    sp.dma_start(s.expert_out[bass.ds(row, P), :], outs[:, j, :]).then_inc(stored[j], 16)

                in_tiles(sp, [load, store], [0, EX_HEAD])
                for j in range(EX_RING):
                    sp.wait_ge(stored[j], 16 * (EX_TILES // EX_RING))

            WEIGHTS = 16 * (EXPERTS * (2 + HC) + 1)

            @block.tensor
            def _(pe):
                pe.wait_ge(w_in, WEIGHTS)

                def turn_rows(n, j, turn):
                    pe.wait_ge(loaded[j], turn * 16 + 16)
                    from_item(pe, rowsT_ready, n, 2, n - 1)
                    for c in range(C):
                        mm = pe.transpose(ps_t[:, j % 2, c * P:(c + 1) * P], rows[:, j, c * P:(c + 1) * P], s.ident[:, :])
                    mm.then_inc(rowsT_psum, 1)

                def up(n, j, turn):
                    pe.wait_ge(w1_ready, n + 1)
                    pe.wait_ge(rowsT_ready, n + 1)
                    from_item(pe, act_ready, n, 2, n - 1)
                    for k in range(HC):
                        for c in range(C):
                            a = c * HID + k * P
                            mm = pe.matmul(ps_hT[:, j % 2, k * P:(k + 1) * P], w1_now[:, j % 2, a:a + P], rowsT[:, j % 2, c, :],
                                           start=(c == 0), stop=(c == C - 1))
                    mm.then_inc(hT_psum, 1)

                def down(n, j, turn):
                    e = expert(pe, n)
                    pe.wait_ge(act_ready, n + 1)
                    from_item(pe, out_ready, n, 2, n - 1)
                    for c in range(HC):
                        mm = pe.matmul(ps_out[:, j % 2, 0:D], actT[:, j % 2, c, :],
                                       w2[:, bass.ds(e, 1), c * D:(c + 1) * D].rearrange("p e n -> p (e n)"),
                                       start=(c == 0), stop=(c == HC - 1))
                    mm.then_inc(out_psum, 1)

                in_tiles(pe, [turn_rows, down, up], [0, 3, 1])

            @block.scalar
            def _(act):
                act.wait_ge(w_in, WEIGHTS)

                def gelu(n, j, turn):
                    e = expert(act, n)
                    act.wait_ge(hT_psum, n + 1)
                    for c in range(HC):
                        ins = act.activation(actT[:, j % 2, c, :], ps_hT[:, j % 2, c * P:(c + 1) * P], ACT.Gelu,
                                             bias=b1T[:, bass.ds(e * HC + c, 1)])
                    ins.then_inc(act_ready, 1)

                in_tiles(act, [gelu], [1])

            @block.vector
            def _(v):
                v.wait_ge(w_in, WEIGHTS)

                def copy_rowsT(n, j, turn):
                    v.wait_ge(rowsT_psum, n + 1)
                    v.tensor_copy(rowsT[:, j % 2, :, :], ps_t[:, j % 2, 0:D].rearrange("p (c n) -> p c n", c=C)).then_inc(rowsT_ready, 1)

                def add_bias(n, j, turn):
                    e = expert(v, n)
                    v.wait_ge(out_psum, n + 1)
                    from_item(v, stored[j], n, EX_RING, turn * 16)
                    v.tensor_tensor(outs[:, j, :], ps_out[:, j % 2, 0:D], flat(b2_b, e, slice(0, D)), ALU.add).then_inc(out_ready, 1)

                def place_w1(n, j, turn):
                    e = expert(v, n)
                    from_item(v, hT_psum, n, 2, n - 1)
                    v.tensor_copy(w1_now[:, j % 2, :], w1[:, bass.ds(e, 1), :].rearrange("p e n -> p (e n)")).then_inc(w1_ready, 1)

                in_tiles(v, [copy_rowsT, place_w1, add_bias], [0, 0, 3])


def finish(nc, s, out):
    with ExitStack() as ctx:
        def sb(name, shape, dt=F32):
            return ctx.enter_context(nc.sbuf_tensor(name, shape, dt))

        def sem(name):
            return nc.alloc_semaphore(name=name)

        rows = sb("k_rows", [P, 4, 2 * D])
        index = sb("k_index", [P, 4, 2], I32)
        part = sb("k_part", [P, 2, D])
        result = sb("k_result", [P, 4, D])
        gathered = [sem(f"k_gathered{j}") for j in range(4)]
        indexed = sem("k_indexed")
        halfway = sem("k_halfway")
        summed = sem("k_summed")
        stored = [sem(f"k_stored{j}") for j in range(4)]

        with nc.Block() as block:

            @block.gpsimd
            def _(g):
                def gather(t, j, turn):
                    count = TAIL if isinstance(t, int) and t == TILES - 1 else P
                    from_item(g, summed, t, 4, t - 3)
                    g.tensor_copy(index[:, j, :], s.slot[:, :, bass.ds(t, 1)].rearrange("p k t -> p (k t)")).then_inc(indexed, 1)
                    g.wait_ge(indexed, t + 1)
                    g.sem_inc(s.wait_seen, 1)
                    for k in range(2):
                        g.indirect_dma_start(rows[0:count, j, k * D:(k + 1) * D], None, s.expert_out,
                                             bass.IndirectOffsetOnAxis(ap=index[0:count, j, k:k + 1], axis=0)).then_inc(gathered[j], 16)

                in_step(g, [gather], [0], TILES - 1, 5, 4)
                gather(TILES - 1, (TILES - 1) % 4, (TILES - 1) // 4)

            @block.vector
            def _(v):
                def first(t, j, turn):
                    from_item(v, summed, t, 2, t - 1)
                    v.wait_ge(gathered[j], turn * 32 + 32)
                    v.scalar_tensor_tensor(part[:, j % 2, :], rows[:, j, 0:D], s.weight[:, 0, bass.ds(t, 1)],
                                           flat(s.sums, t, slice(0, D)), ALU.mult, ALU.add).then_inc(halfway, 1)

                def second(t, j, turn):
                    v.wait_ge(halfway, t + 1)
                    from_item(v, stored[j], t, 4, turn * 16)
                    v.scalar_tensor_tensor(result[:, j, :], rows[:, j, D:2 * D], s.weight[:, 1, bass.ds(t, 1)],
                                           part[:, j % 2, :], ALU.mult, ALU.add).then_inc(summed, 1)

                in_step(v, [second, first], [1, 0], TILES, 6, 4)

            @block.sync
            def _(sp):
                def store(t, j, turn):
                    count = TAIL if isinstance(t, int) and t == TILES - 1 else P
                    row = fixed(sp, t * P)
                    sp.wait_ge(summed, t + 1)
                    sp.dma_start(out[bass.ds(row, count), :], result[0:count, j, :]).then_inc(stored[j], 16)

                in_step(sp, [store], [0], TILES - 1, 5, 4)
                store(TILES - 1, (TILES - 1) % 4, (TILES - 1) // 4)
                for j in range(4):
                    sp.wait_ge(stored[j], 16 * len(range(j, TILES, 4)))


class Plan:
    pass


def program(nc, x, src, dst, W, att_src, att_dst, gat_bias, ln_gamma, ln_beta, w_norm1, w_qkv, w_out, b_out, w_norm2,
            gamma, beta, Wr, br, W1, b1, W2, b2, out):
    with ExitStack() as ctx:
        def sb(name, shape, dt=F32):
            return ctx.enter_context(nc.sbuf_tensor(name, shape, dt))
        s = allocate(nc, ctx)
        s.fault = sb("fault", [P, 2], I32)
        s.state_mean = sb("state_mean", [P, TILES])
        s.state_var = sb("state_var", [P, TILES])
        s.slot = sb("slot", [P, 2, TILES], I32)
        s.weight = sb("weight", [P, 2, TILES])
        s.expert_of = sb("expert_of", [1, EX_TILES], I32)
        s.gat_stat = ctx.enter_context(nc.semaphore("gat_stat"))
        s.wait_seen = ctx.enter_context(nc.semaphore("wait_seen"))
        s.mix_stat = ctx.enter_context(nc.semaphore("mix_stat"))
        with stage(nc):
            project(nc, s, x, src, dst, W, att_src, att_dst, w_norm1, w_qkv)
        with stage(nc), ExitStack() as plan_ctx:
            plan = Plan()
            plan.edge0 = plan_ctx.enter_context(nc.sbuf_tensor("edge0", [1, GROUPS], I32))
            plan.window = plan_ctx.enter_context(nc.sbuf_tensor("window", [1, GROUPS], I32))
            plan.target0 = plan_ctx.enter_context(nc.sbuf_tensor("target0", [P, GROUPS], F32))
            check_inputs(nc, s, dst)
            sort_by_window(nc, s)
            plan_groups(nc, s, plan)
            shift_by_target(nc, s, plan)
            attend_edges(nc, s, plan)
        with stage(nc), ExitStack() as stats_ctx:
            s.gat_stats = stats_ctx.enter_context(nc.sbuf_tensor("gat_stats", [P, TILES, 6], F32))
            s.mix_stats = stats_ctx.enter_context(nc.sbuf_tensor("mix_stats", [P, TILES, 6], F32))
            combine(nc, s, x, gat_bias, w_out, b_out)
            join(nc, s, x, ln_gamma, ln_beta, w_norm2)
            route(nc, s, gamma, beta, Wr, br)
        with stage(nc):
            scatter_rows(nc, s)
            run_experts(nc, s, W1, b1, W2, b2)
            finish(nc, s, out)


_INS = ['x', 'src', 'dst', 'L0_gnn_W', 'L0_gnn_att_src', 'L0_gnn_att_dst', 'L0_gnn_bias', 'L0_gnn_ln_gamma', 'L0_gnn_ln_beta',
        'L0_mix_w_norm1', 'L0_mix_w_qkv', 'L0_mix_w_out', 'L0_mix_b_out', 'L0_mix_w_norm2',
        'L0_ffn_gamma', 'L0_ffn_beta', 'L0_ffn_Wr', 'L0_ffn_br', 'L0_ffn_W1', 'L0_ffn_b1', 'L0_ffn_W2', 'L0_ffn_b2']
_OUTS = [((N, D), 'float32')]


def kernel(**inputs):
    import numpy as _np
    import concourse.bacc as _bacc
    from concourse import mybir as _mybir
    from concourse.bass_utils import run_bass_kernel_spmd as _run

    nc = _bacc.Bacc("TRN2", target_bir_lowering=False, num_devices=1)
    arrays, args = {}, []
    for name in _INS:
        a = _np.ascontiguousarray(inputs[name])
        arrays[f"in_{name}_dram"] = a
        args.append(nc.dram_tensor(f"in_{name}_dram", a.shape, _mybir.dt.from_np(a.dtype), kind="ExternalInput").ap())
    for i, (shape, dtype) in enumerate(_OUTS):
        args.append(nc.dram_tensor(f"out_{i}_dram", shape, _mybir.dt.from_np(_np.dtype(dtype)), kind="ExternalOutput").ap())
    program(nc, *args)
    r = _run(nc, [arrays], core_ids=[0])
    return r.results[0]["out_0_dram"]
```
